# Optimizing a Trainium2 kernel written in Bass

```python
import numpy as np
import jax
import jax.numpy as jnp

def _softmax(x, axis=-1):
    return jax.nn.softmax(x, axis=axis)

def _gelu(x):
    return jax.nn.gelu(x, approximate=True)

def _silu(x):
    return jax.nn.silu(x)

def _sigmoid(x):
    return jax.nn.sigmoid(x)

def _layernorm(x, axis=-1, eps=1e-05):
    m = jnp.mean(x, axis=axis, keepdims=True)
    v = jnp.var(x, axis=axis, keepdims=True)
    return (x - m) / jnp.sqrt(v + eps)

def _scatter_add(tgt, idx, src, axis=0):
    return tgt.at[idx].add(src)

def _segment_sum(src, seg, n):
    return jax.ops.segment_sum(src, seg, n)
kernel_name = 'mk_vit_tower_d1_tok_img512_r4_12ab9f'

def setup_inputs(seed: int=0):
    np.random.seed(seed)
    _w = jnp.asarray

    def _rec_inputs():
        import jax
        import jax.numpy as jnp
        _rk = jax.random.key(seed)
        x = -0.000147625 + 0.999875 * jax.random.normal(jax.random.fold_in(_rk, 1), (64, 3, 224, 224), jnp.float32)
        return x
    x = _rec_inputs()

    def _L0_tok_setup():
        import jax, jax.numpy as jnp
        import numpy as np
        N_PATCHES = 8
        PATCH = 28
        C = 3
        IN_D = C * PATCH * PATCH
        HID = 128
        SEQ = N_PATCHES * N_PATCHES + 1

        def _positional_embedding(seq_len, dim):
            i = np.arange(seq_len)[:, None].astype(np.float32)
            j = np.arange(dim)[None, :].astype(np.float32)
            ang = i / np.power(100000.0, j / dim)
            pe = np.where(j % 2 == 0, np.sin(ang), np.cos(ang))
            return jnp.asarray(pe, dtype=jnp.float32)
        key = jax.random.key(seed)
        k1, k2, k3, k4 = jax.random.split(key, 4)
        B = 64
        X = jax.random.normal(k1, (B, C, 224, 224), dtype=jnp.float32)
        bound = 1.0 / np.sqrt(IN_D)
        W = jax.random.uniform(k2, (HID, IN_D), minval=-bound, maxval=bound, dtype=jnp.float32)
        b = jax.random.uniform(k3, (HID,), minval=-bound, maxval=bound, dtype=jnp.float32)
        class_token = jax.random.uniform(k4, (1, HID), dtype=jnp.float32)
        pos_embed = _positional_embedding(SEQ, HID)
        return {'X': X, 'W': W, 'b': b, 'class_token': class_token, 'pos_embed': pos_embed}
    _L0_tok_all = _L0_tok_setup()
    _L0_tok_in = {k: v for k, v in _L0_tok_all.items() if k in ('W', 'b', 'class_token', 'pos_embed')}
    del _L0_tok_all

    def _L0_attn_setup():
        import jax, jax.numpy as jnp
        import numpy as np
        DEPTH, EMBED, HEADS, FF = (4, 128, 8, 512)
        POS_SCALE, POS_WEIGHT = (0.1, 1.0)
        EPS = 1e-05

        def _ln(x, g, b):
            m = x.mean(-1, keepdims=True)
            v = ((x - m) ** 2).mean(-1, keepdims=True)
            return (x - m) * jax.lax.rsqrt(v + EPS) * g + b
        key = jax.random.key(seed)
        ks = jax.random.split(key, 6)
        B, L = (8, 256)
        s = 0.02
        x = jax.random.normal(ks[0], (B, L, EMBED), jnp.float32)
        Wqkv = jax.random.normal(ks[1], (DEPTH, 3 * EMBED, EMBED), jnp.float32) * s
        bqkv = jnp.zeros((DEPTH, 3 * EMBED), jnp.float32)
        W1 = jax.random.normal(ks[2], (DEPTH, FF, EMBED), jnp.float32) * s
        b1 = jnp.zeros((DEPTH, FF), jnp.float32)
        W2 = jax.random.normal(ks[3], (DEPTH, EMBED, FF), jnp.float32) * s
        b2 = jnp.zeros((DEPTH, EMBED), jnp.float32)
        g = jnp.ones((DEPTH, EMBED), jnp.float32)
        bt = jnp.zeros((DEPTH, EMBED), jnp.float32)
        return {'input': x, 'Wqkv': Wqkv, 'bqkv': bqkv, 'W1': W1, 'b1': b1, 'W2': W2, 'b2': b2, 'g1': g, 'bt1': bt, 'g2': g, 'bt2': bt, 'g3': g, 'bt3': bt}
    _L0_attn_all = _L0_attn_setup()
    _L0_attn_in = {k: v for k, v in _L0_attn_all.items() if k in ('Wqkv', 'bqkv', 'W1', 'b1', 'W2', 'b2', 'g1', 'bt1', 'g2', 'bt2', 'g3', 'bt3')}
    del _L0_attn_all

    def _L0_ffn_setup():
        import jax, jax.numpy as jnp
        import numpy as np
        B, S, D = (8, 2048, 128)
        E, DFF = (16, 128)
        CAPACITY = 2
        key = jax.random.key(seed)
        ks = jax.random.split(key, 4)
        x = jax.random.normal(ks[0], (B, S, D), dtype=jnp.float32)
        gate_weight = jax.random.normal(ks[1], (D, E), dtype=jnp.float32) * 0.006
        w1 = jax.random.normal(ks[2], (E, D, DFF), dtype=jnp.float32) * 0.02
        b1 = jnp.zeros((E, DFF), dtype=jnp.float32)
        w2 = jax.random.normal(ks[3], (E, DFF, D), dtype=jnp.float32) * 0.02
        b2 = jnp.zeros((E, D), dtype=jnp.float32)
        return {'x': x, 'gate_weight': gate_weight, 'w1': w1, 'b1': b1, 'w2': w2, 'b2': b2}
    _L0_ffn_all = _L0_ffn_setup()
    _L0_ffn_in = {k: v for k, v in _L0_ffn_all.items() if k in ('gate_weight', 'w1', 'b1', 'w2', 'b2')}
    del _L0_ffn_all
    return {'x': x, 'L0_tok_W': _L0_tok_in['W'], 'L0_tok_b': _L0_tok_in['b'], 'L0_tok_class_token': _L0_tok_in['class_token'], 'L0_tok_pos_embed': _L0_tok_in['pos_embed'], 'L0_attn_Wqkv': _L0_attn_in['Wqkv'], 'L0_attn_bqkv': _L0_attn_in['bqkv'], 'L0_attn_W1': _L0_attn_in['W1'], 'L0_attn_b1': _L0_attn_in['b1'], 'L0_attn_W2': _L0_attn_in['W2'], 'L0_attn_b2': _L0_attn_in['b2'], 'L0_attn_g1': _L0_attn_in['g1'], 'L0_attn_bt1': _L0_attn_in['bt1'], 'L0_attn_g2': _L0_attn_in['g2'], 'L0_attn_bt2': _L0_attn_in['bt2'], 'L0_attn_g3': _L0_attn_in['g3'], 'L0_attn_bt3': _L0_attn_in['bt3'], 'L0_ffn_gate_weight': _L0_ffn_in['gate_weight'], 'L0_ffn_w1': _L0_ffn_in['w1'], 'L0_ffn_b1': _L0_ffn_in['b1'], 'L0_ffn_w2': _L0_ffn_in['w2'], 'L0_ffn_b2': _L0_ffn_in['b2']}

def reference(x, L0_tok_W, L0_tok_b, L0_tok_class_token, L0_tok_pos_embed, L0_attn_Wqkv, L0_attn_bqkv, L0_attn_W1, L0_attn_b1, L0_attn_W2, L0_attn_b2, L0_attn_g1, L0_attn_bt1, L0_attn_g2, L0_attn_bt2, L0_attn_g3, L0_attn_bt3, L0_ffn_gate_weight, L0_ffn_w1, L0_ffn_b1, L0_ffn_w2, L0_ffn_b2):
    import jax
    import jax.numpy as jnp

    def _L0_tok_ref(X, W, b, class_token, pos_embed):
        import jax, jax.numpy as jnp
        import numpy as np
        N_PATCHES = 8
        PATCH = 28
        C = 3
        IN_D = C * PATCH * PATCH
        HID = 128
        SEQ = N_PATCHES * N_PATCHES + 1

        def _positional_embedding(seq_len, dim):
            i = np.arange(seq_len)[:, None].astype(np.float32)
            j = np.arange(dim)[None, :].astype(np.float32)
            ang = i / np.power(100000.0, j / dim)
            pe = np.where(j % 2 == 0, np.sin(ang), np.cos(ang))
            return jnp.asarray(pe, dtype=jnp.float32)
        B = X.shape[0]
        patches = X.reshape(B, C, N_PATCHES, PATCH, N_PATCHES, PATCH)
        patches = patches.transpose(0, 2, 4, 1, 3, 5).reshape(B, N_PATCHES * N_PATCHES, IN_D)
        tokens = jnp.einsum('bpi,hi->bph', patches, W) + b
        cls = jnp.broadcast_to(class_token[None, :, :], (B, 1, HID))
        tokens = jnp.concatenate([cls, tokens], axis=1)
        return tokens * pos_embed[None, :, :]

    def _L0_attn_ref(input, Wqkv, bqkv, W1, b1, W2, b2, g1, bt1, g2, bt2, g3, bt3):
        import jax, jax.numpy as jnp
        import numpy as np
        DEPTH, EMBED, HEADS, FF = (4, 128, 8, 512)
        POS_SCALE, POS_WEIGHT = (0.1, 1.0)
        EPS = 1e-05

        def _ln(x, g, b):
            m = x.mean(-1, keepdims=True)
            v = ((x - m) ** 2).mean(-1, keepdims=True)
            return (x - m) * jax.lax.rsqrt(v + EPS) * g + b
        x = input
        B, L, E = x.shape
        hd = E // HEADS
        pos_idx = jnp.arange(L)
        pos = jnp.exp(-jnp.abs(pos_idx[:, None] - pos_idx[None, :]).astype(x.dtype) * POS_SCALE) * POS_WEIGHT
        triu = jnp.triu(jnp.ones((L, L), dtype=bool), 1)
        inv_sqrt_hd = jnp.asarray(1.0 / np.sqrt(hd), x.dtype)
        for d in range(DEPTH):
            qkv = jnp.einsum('ble,fe->blf', x, Wqkv[d]) + bqkv[d]
            q = qkv[..., :E].reshape(B, L, HEADS, hd).transpose(0, 2, 1, 3)
            k = qkv[..., E:2 * E].reshape(B, L, HEADS, hd).transpose(0, 2, 1, 3)
            logits = jnp.einsum('bhqd,bhkd->bhqk', q, k) * inv_sqrt_hd
            A = jax.nn.softmax(logits, axis=-1).mean(axis=1)
            A = jnp.where(triu & (A != 0), -jnp.inf, A)
            W = jax.nn.softmax(A + pos[None], axis=-1)
            sa = jnp.einsum('bqk,bke->bqe', W, x)
            x = _ln(x + sa, g1[d], bt1[d])
            x = _ln(x, g2[d], bt2[d])
            h = jax.nn.relu(jnp.einsum('ble,fe->blf', x, W1[d]) + b1[d])
            ff = jnp.einsum('blf,ef->ble', h, W2[d]) + b2[d]
            x = _ln(x + ff, g3[d], bt3[d])
        return x

    def _L0_ffn_ref(x, gate_weight, w1, b1, w2, b2):
        import jax, jax.numpy as jnp
        import numpy as np
        B, S, D = (8, 2048, 128)
        E, DFF = (16, 128)
        CAPACITY = 2
        Bx, Sx, Dx = x.shape
        num_experts = gate_weight.shape[1]
        k = Sx // num_experts * CAPACITY
        logits = jnp.einsum('bsd,de->bse', x, gate_weight)
        affinity = jax.nn.softmax(logits, axis=-1).transpose(0, 2, 1)
        gating, index = jax.lax.top_k(affinity, k)
        x_in = jnp.take_along_axis(x[:, None, :, :], index[..., None], axis=2)
        h = jax.nn.gelu(jnp.einsum('bekd,edh->bekh', x_in, w1) + b1[None, :, None, :])
        x_e = jnp.einsum('bekh,ehd->bekd', h, w2) + b2[None, :, None, :]
        weighted = gating[..., None] * x_e
        out = jnp.zeros_like(x)
        idx_flat = index.reshape(Bx, num_experts * k)
        vals_flat = weighted.reshape(Bx, num_experts * k, Dx)
        out = out.at[jnp.arange(Bx)[:, None], idx_flat].add(vals_flat)
        return out
    h = _L0_tok_ref(x, L0_tok_W, L0_tok_b, L0_tok_class_token, L0_tok_pos_embed)
    h = h + _L0_attn_ref(_layernorm(h, axis=-1), L0_attn_Wqkv, L0_attn_bqkv, L0_attn_W1, L0_attn_b1, L0_attn_W2, L0_attn_b2, L0_attn_g1, L0_attn_bt1, L0_attn_g2, L0_attn_bt2, L0_attn_g3, L0_attn_bt3)
    h = h + _L0_ffn_ref(_layernorm(h, axis=-1), L0_ffn_gate_weight, L0_ffn_w1, L0_ffn_b1, L0_ffn_w2, L0_ffn_b2)
    return h

_drawn_inputs = setup_inputs


def setup_inputs(seed=0):
    import zlib

    import numpy as np

    out = dict(_drawn_inputs(seed))
    spreads = {'L0_attn_bqkv': (0.0, 2.0),
     'L0_attn_b1': (0.0, 0.1),
     'L0_attn_b2': (0.0, 0.1),
     'L0_attn_g1': (1.0, 0.2),
     'L0_attn_bt1': (0.0, 0.1),
     'L0_attn_g2': (1.0, 0.2),
     'L0_attn_bt2': (0.0, 0.1),
     'L0_attn_g3': (1.0, 0.2),
     'L0_attn_bt3': (0.0, 0.1),
     'L0_ffn_b1': (0.0, 0.8),
     'L0_ffn_b2': (0.0, 0.8)}
    factors = {'L0_attn_Wqkv': 22.143, 'L0_ffn_gate_weight': 7.609, 'L0_ffn_w1': 8.0, 'L0_ffn_w2': 8.0}
    for name, (base, spread) in spreads.items():
        noise = np.random.default_rng([zlib.crc32(name.encode()), seed]).standard_normal(out[name].shape)
        drawn = base * np.exp(spread * noise) if base else spread * noise
        out[name] = jnp.asarray(drawn.astype(out[name].dtype))
    for name, factor in factors.items():
        out[name] = (out[name] * factor).astype(out[name].dtype)
    return out
```

```python
from contextlib import ExitStack
from typing import NamedTuple

import numpy as np

import concourse.bass as bass
from concourse import mybir

F32 = mybir.dt.float32
U32 = mybir.dt.uint32
ALU = mybir.AluOpType
ACT = mybir.ActivationFunctionType
X = mybir.AxisListType.X

B = 64
PATCHES = 64
SEQ = PATCHES + 1
D = 128
IN_D = 2352
MAIN = IN_D // D
REST = IN_D - MAIN * D
LAYERS, HEADS, HD, FF = 4, 8, 16, 512
EXPERTS, SLOTS, DFF = 16, 8, 128
EPS = 1e-5

HALVES = 2
IMG = 8
ITERS = B // (HALVES * IMG)
TILES = 4
SLOTN = TILES + 1
TOK = IMG * SEQ
WIDE = SLOTN * D
CHUNK = 256
UNITS = LAYERS * HALVES
SBANKS = 2

CONST = {}
for _name, _n in (("ident", D), ("stackI", PATCHES), ("pos8", SEQ), ("neg", SEQ), ("posc", SEQ), ("negc", SEQ),
                  ("onehot", SLOTN * IMG), ("headmask", HEADS), ("hsum", IMG), ("target", D), ("targetc", IMG),
                  ("pow", 16), ("par", 2)):
    _at = sum(w for _, w in CONST.values())
    CONST[_name] = (_at, _n)
CONST_W = sum(w for _, w in CONST.values())
VEC = {n: i for i, n in enumerate(("bq", "bk", "g1", "bt1", "g2", "bt2", "b2", "g3", "bt3", "b1_0", "b1_1", "b1_2", "b1_3"))}
NVEC = len(VEC)


def shape_constants():
    c = np.zeros((D, CONST_W), np.float32)

    def put(name, a):
        at, n = CONST[name]
        a = np.asarray(a, np.float32)
        c[:a.shape[0], at:at + n] = a.reshape(a.shape[0], n)

    p = np.arange(D)
    q = 1 + p % PATCHES
    k = np.arange(SEQ)
    far = -1e5
    put("ident", np.eye(D))
    put("stackI", p[:, None] % PATCHES == np.arange(PATCHES)[None, :])
    put("pos8", HEADS * np.exp(-np.abs(q[:, None] - k[None, :]).astype(np.float32) * np.float32(0.1)))
    put("neg", far * (k[None, :] > q[:, None]))
    put("posc", np.broadcast_to(HEADS * np.exp(-k.astype(np.float32) * np.float32(0.1)), (D, SEQ)))
    put("negc", np.broadcast_to(far * (k > 0), (D, SEQ)))
    one = np.zeros((D, SLOTN, IMG))
    for t in range(TILES):
        one[p, t, 2 * t + p // PATCHES] = 1
    one[np.arange(IMG), TILES, np.arange(IMG)] = 1
    put("onehot", one)
    put("headmask", p[:, None] // HD == np.arange(HEADS)[None, :])
    put("hsum", p[:, None] // HEADS == np.arange(IMG)[None, :])
    img = p // EXPERTS
    put("target", np.where(img[:, None] % 2 == p[None, :] // PATCHES, 1 + p[None, :] % PATCHES, -1))
    put("targetc", np.where(img[:, None] == np.arange(IMG)[None, :], 0, -1))
    put("pow", np.full((D, 16), -0.5))
    put("par", np.stack([(p // HD) % 2 == 0, (p // HD) % 2 == 1], 1))
    return c


def schedule(patches):
    def attn(h, l):
        return [("proj", h, l), ("soft0", h, l), ("soft1", h, l), ("soft2", h, l), ("soft3", h, l), ("cls", h, l),
                ("mix", h, l)]

    def ffn(h, l):
        return [("norm1", h, l), ("norm2", h, l), ("ffn0", h, l), ("ffn1", h, l), ("norm3", h, l), ("next", h, l)]

    def weave(a, b):
        out = []
        for i in range(max(len(a), len(b))):
            out += a[i:i + 1] + b[i:i + 1]
        return out

    out = [("init", 0, 0), ("init", 1, 0)] + attn(0, 0)
    for l in range(LAYERS):
        out += weave(attn(1, l), ffn(0, l))
        if patches:
            out.append(("patch", 0, l))
        if l + 1 < LAYERS:
            out += weave(attn(0, l + 1), ffn(1, l))
        else:
            out += ffn(1, l)
    return out + [("moe", 0, 0), ("moe", 1, 0)]


JOBS = {
    "patch": [],
    "init": ["nat0", "nat1", "T0", "T1"],
    "proj": ["q0", "q1", "ke0", "ke1", "ko0", "ko1"],
    "soft0": [], "soft1": [], "soft2": [], "soft3": [],
    "cls": ["score", "heads", "turn"],
    "mix": ["turn", "turnc", "mix0", "mix1", "mixc"],
    "norm1": ["T0", "T1"],
    "norm2": ["nat0", "nat1", "T0", "T1"],
    "ffn0": ["h0", "h1", "h2", "h3"],
    "ffn1": ["h0", "h1", "h2", "h3"],
    "norm3": ["out0", "out1", "nat0", "nat1"],
    "next": ["T0", "T1", "nat0", "nat1"],
    "moe": ["T0", "T1", "gate", "aff", "oh0", "oh1", "ohc0", "ohc1", "xin0", "xin1", "xin2", "xin3",
            "up0", "up1", "down0", "down1", "yT0", "yT1", "sum0", "sum1", "sum2", "sum3", "sumc"],
}
RING = 3


def psum_places():
    place, count, n = {}, [0] * RING, 0
    for seg, h, l in schedule(False):
        for job in JOBS[seg]:
            b = n % RING
            count[b] += 1
            place[(seg, h, l, job)] = (b, count[b])
            n += 1
    return place, count


PLACE, PER_BANK = psum_places()


class Signal:

    def __init__(self, sem, per, units, early=0):
        self.sem, self.per, self.units, self.early = sem, per, units, early

    def at(self, it, unit, k=None):
        return (it * self.units + unit) * self.per + (self.per if k is None else k) + self.early


class Job(NamedTuple):

    bank: object
    filled: object
    drained: object
    nth: object
    before: object


def vit_kernel(nc, x_main, x_rest, wp_main, wp_rest, pvec, post, const, wqk, w1, w2, lvec, gate, ew1, ew2, evec, out):
    ctx = ExitStack()
    with ctx:
        def sb(name, shape, dt=F32):
            return ctx.enter_context(nc.sbuf_tensor(name, shape, dt))

        def both(name, shape):
            return [sb(f"{name}{h}", shape) for h in range(HALVES)]

        def signal(name, per=1, units=UNITS, early=0):
            return Signal(ctx.enter_context(nc.semaphore(name)), per, units, early)

        S = [ctx.enter_context(nc.psum_tensor(f"S{i}", [D, 2, 512], F32)) for i in range(SBANKS)]
        ringbank = [ctx.enter_context(nc.psum_tensor(f"ring{i}", [D, 512], F32)) for i in range(RING)]
        pp = ctx.enter_context(nc.psum_tensor("pp", [D, 512], F32))

        cst = sb("cst", [D, CONST_W])
        wpm = sb("wpm", [D, MAIN, D])
        wpr = sb("wpr", [REST, D])
        pv = sb("pv", [D, 4])
        posT = sb("posT", [D, SEQ])
        wq = sb("wq", [D, LAYERS, 3, D])
        w1s = sb("w1s", [D, LAYERS, FF])
        w2s = sb("w2s", [D, LAYERS, FF // D, D])
        vec = sb("vec", [D, LAYERS, NVEC])
        bq4 = sb("bq4", [D, LAYERS])
        bkm = sb("bkm", [D, LAYERS, 2])
        gw = sb("gw", [D, EXPERTS])
        ew1s = sb("ew1s", [D, EXPERTS, DFF])
        ew2s = sb("ew2s", [DFF, EXPERTS, D])
        ev = sb("ev", [D, 2, EXPERTS])
        pix = [sb(f"pix{i}", [D, MAIN, CHUNK]) for i in range(2)]
        pixr = [sb(f"pixr{i}", [REST, CHUNK]) for i in range(2)]

        h0T = both("h0T", [D, WIDE])
        h0n = both("h0n", [D, SLOTN, D])
        xT = both("xT", [D, WIDE])
        xn = both("xn", [D, SLOTN, D + 1])
        qT = both("qT", [D, TOK])
        qx = both("qx", [D, IMG * (IMG * HEADS + HEADS)])
        kT = both("kT", [D, IMG, 2, SEQ])
        A8 = both("A8", [D, TILES, SEQ])
        U8 = both("U8", [D, TILES, SEQ])
        EX = both("EX", [D, TILES, D + IMG])
        ecl = both("ecl", [D, TILES])
        ET = both("ET", [D, TILES, D])
        EcT = both("EcT", [IMG, TILES, D])
        LC = both("LC", [D, SLOTN, IMG])
        Pc = both("Pc", [IMG * HEADS, SEQ])
        Vc = both("Vc", [IMG, 2, SEQ])
        Ec = both("Ec", [IMG, D + 1])
        r1 = both("r1", [D, SLOTN, D])
        nn = both("nn", [D, SLOTN, D])
        yT = both("yT", [D, WIDE])
        zT = both("zT", [D, WIDE])
        hT = both("hT", [D, FF // D, TOK])
        st = both("st", [D, SLOTN, 6])
        mv = both("mv", [D, SLOTN, 2])
        rs = both("rs", [D, SLOTN])
        sc = both("sc", [D, 16])
        XB = 3
        P = [sb(f"P{i}", [D, HEADS, SEQ]) for i in range(XB)]
        mx = [sb(f"mx{i}", [D, HEADS]) for i in range(XB)]
        sm = [sb(f"sm{i}", [D, HEADS]) for i in range(XB)]
        aff = sb("aff", [D, SLOTN, EXPERTS])
        mxg = sb("mxg", [D, SLOTN])
        smg = sb("smg", [D, SLOTN])
        affT = sb("affT", [D, SEQ])
        gv = sb("gv", [D, SLOTS])
        gi = sb("gi", [D, SLOTS], U32)
        gf = sb("gf", [D, SLOTS])
        OH = sb("OH", [D, SLOTS, D])
        OHc = sb("OHc", [D, SLOTS, IMG])
        OHT = sb("OHT", [D, SLOTS, D])
        OHcT = sb("OHcT", [IMG, SLOTS, D])
        big = sb("big", [D, SLOTS * D])

        def c_(name):
            at, n = CONST[name]
            return cst[:, at:at + n]

        ident = c_("ident")
        onehot = c_("onehot").rearrange("p (s i) -> p s i", s=SLOTN)

        HALF_E = EXPERTS // 2
        XIN = SLOTS * D
        flat = [hT[h][:].rearrange("p f t -> p (f t)") for h in range(HALVES)]
        xin = [f[:, 0:XIN].rearrange("p (e i s) -> p e i s", e=EXPERTS, i=IMG) for f in flat]
        hid = [f[:, XIN:2 * XIN].rearrange("p (e r) -> p e r", e=EXPERTS) for f in flat]
        Y = [f[:, 0:XIN].rearrange("p (s d) -> p s d", s=SLOTS) for f in flat]
        AX = big[:, 0:SLOTN * D].rearrange("p (s i e) -> p s i e", s=SLOTN, i=IMG)
        eo = big[:].rearrange("p (s c) -> p s c", s=SLOTS)
        eo4 = big[:].rearrange("p (s i e) -> p e i s", e=EXPERTS, i=IMG)

        out_h = out.rearrange("(u t a) k d -> u t a k d", t=TILES, a=2)

        w_in = signal("w_in", 16)
        pix_in = [signal(f"pix_in{i}", 64, 1) for i in range(2)]
        out_done = [signal(f"out_done{h}", 48, 1) for h in range(HALVES)]
        set_dve = signal("set_dve")
        set_pool = signal("set_pool")
        filled = [signal(f"filled{b}", PER_BANK[b], 1) for b in range(RING)]
        drained = [signal(f"drained{b}", PER_BANK[b], 1) for b in range(RING)]
        patch_sum = signal("patch_sum", 1, 4)
        patch_out = signal("patch_out", 1, 4)
        qx_in = signal("qx_in")
        s_full = signal("s_full", TILES)
        s_row = signal("s_row", 2 * TILES)
        s_max = signal("s_max", TILES)
        s_sub = signal("s_sub", TILES, early=SBANKS)
        p_exp = signal("p_exp", TILES)
        p_sum = signal("p_sum", TILES)
        p_rec = signal("p_rec", TILES)
        p_mul = signal("p_mul", TILES)
        a_in = signal("a_in", TILES)
        u_in = signal("u_in", 3)
        e_in = signal("e_in")
        ec_in = signal("ec_in")
        cls_dve = signal("cls_dve", 9)
        cls_act = signal("cls_act")
        r_rec = signal("r_rec", 2)
        LN_UNITS = HALVES * (2 + 3 * LAYERS)
        ln_st = signal("ln_st", 2, LN_UNITS)
        ln_mv = signal("ln_mv", 2, LN_UNITS)
        ln_ve = signal("ln_ve", 2, LN_UNITS)
        ln_rs = signal("ln_rs", 2, LN_UNITS)
        ln_in = signal("ln_in", 2, HALVES * (2 + LAYERS))
        moe_dve = signal("moe_dve", 13, HALVES)
        moe_act = signal("moe_act", 3, HALVES)

        ln_order = {}
        for seg, h, l in schedule(False):
            if seg in ("init", "norm1", "norm2", "norm3", "moe"):
                ln_order[(seg, h, l)] = len(ln_order)
        ln_in_order = {key: i for i, key in enumerate(k for k in ln_order if k[0] in ("init", "norm1", "moe"))}

        def job(it, seg, h, l, name):
            b, n = PLACE[(seg, h, l, name)]
            return Job(ringbank[b], filled[b].sem, drained[b].sem, filled[b].at(it, 0, n), filled[b].at(it, 0, n - 1))

        def jobs(it, seg, h, l, *names):
            return [job(it, seg, h, l, name) for name in names]

        def unit(h, l):
            return l * HALVES + h

        def nat(j):
            return range(0, 2) if j == 0 else range(2, SLOTN)

        def cols(j):
            return slice(0, CHUNK) if j == 0 else slice(CHUNK, TOK)

        def width(j):
            return CHUNK if j == 0 else TOK - CHUNK

        N_W = 15
        block = ctx.enter_context(nc.Block())

        @block.sync
        def _(sp):
            for dst, src in ((cst[:], const), (wpr[:], wp_rest), (pv[:, 0:2], pvec), (posT[:], post),
                             (wpm[:], wp_main)):
                sp.dma_start(dst, src).then_inc(w_in.sem, 16)

            def load(m, i):
                sp.dma_start(pix[i][:], x_main[m]).then_inc(pix_in[i].sem, 16)
                sp.dma_start(pixr[i][:], x_rest[m]).then_inc(pix_in[i].sem, 16)

            load(0, 0)
            load(1, 1)
            for dst, src in ((vec[:], lvec), (wq[:, :, 0, :], wqk[:, :, 0, :]), (wq[:, :, 1, :], wqk[:, :, 1, :]),
                             (wq[:, :, 2, :], wqk[:, :, 1, :]), (w1s[:], w1), (w2s[:], w2), (gw[:], gate), (ew1s[:], ew1),
                             (ew2s[:], ew2), (ev[:], evec)):
                sp.dma_start(dst, src).then_inc(w_in.sem, 16)

            def reload(it, c):
                sp.wait_ge(patch_sum.sem, patch_sum.at(it, 0, c - 1))
                load(it * 4 + c, c % 2)

            def iteration(it, more):
                if more:
                    for c in range(4):
                        reload(it + 1, c)
                for h in range(HALVES):
                    o = out_h[it * HALVES + h]
                    for R in jobs(it, "moe", h, 0, "sum0", "sum1", "sum2", "sum3", "sumc"):
                        sp.wait_ge(R.drained, R.nth)
                    for a in range(2):
                        sp.dma_start(o[:, a, 1:SEQ, :].rearrange("t j d -> j t d"),
                                     nn[h][PATCHES * a:PATCHES * (a + 1), 0:TILES, :]).then_inc(out_done[h].sem, 16)
                    sp.dma_start(o[:, :, 0, :], nn[h][0:IMG, TILES, :]).then_inc(out_done[h].sem, 16)

            reload(0, 2)
            reload(0, 3)
            for it in range(ITERS):
                iteration(it, it + 1 < ITERS)
            for h in range(HALVES):
                sp.wait_ge(out_done[h].sem, out_done[h].at(ITERS - 1, 0))

        @block.gpsimd
        def _(pool):
            for h in range(HALVES):
                for z in (qx, EX, r1, LC):
                    pool.memset(z[h][:], 0.0).then_inc(set_pool.sem, 1)

            def rstd(it, key, h, j):
                s = nat(j)
                pool.wait_ge(ln_mv.sem, ln_mv.at(it, ln_order[key], j + 1))
                r = rs[h][:, s[0]:s[-1] + 1]
                pool.tensor_scalar(r, mv[h][:, s[0]:s[-1] + 1, 1], EPS, 1.0, ALU.add, ALU.mult).then_inc(ln_ve.sem, 1)
                pool.wait_ge(ln_ve.sem, ln_ve.at(it, ln_order[key], j + 1))
                pool.tensor_tensor(r, r, c_("pow")[:, 0:len(s)], ALU.pow).then_inc(ln_rs.sem, 1)

            pool.wait_ge(w_in.sem, 16 * N_W)
            pool.wait_ge(set_pool.sem, 4 * HALVES)
            def iteration(it, more):
                for seg, h, l in schedule(more):
                    n = unit(h, l)
                    if seg == "proj":
                        for R in jobs(it, seg, h, l, "q1"):
                            pool.wait_ge(R.drained, R.nth)
                        pool.tensor_tensor(qx[h][:].rearrange("p (i c) -> p i c", i=IMG)[:, :, 0:HEADS],
                                           qT[h][:, CHUNK * 2:TOK].unsqueeze(2).broadcast_to([D, IMG, HEADS]),
                                           c_("headmask").unsqueeze(1).broadcast_to([D, IMG, HEADS]),
                                           ALU.mult).then_inc(qx_in.sem, 1)
                    elif seg[:4] == "soft":
                        t = int(seg[4])
                        g = (n * TILES + t) % XB
                        pool.wait_ge(p_rec.sem, p_rec.at(it, n, t + 1))
                        pool.tensor_tensor(P[g][:], P[g][:], sm[g][:].unsqueeze(2).broadcast_to([D, HEADS, SEQ]),
                                           ALU.mult).then_inc(p_mul.sem, 1)
                    elif seg in ("init", "norm1", "norm2", "norm3", "moe"):
                        for j in range(2):
                            rstd(it, (seg, h, l), h, j)

            for it in range(ITERS):
                iteration(it, it + 1 < ITERS)

        @block.scalar
        def _(act):
            def evacuate(it, seg, h, l, what, dst, bias=None, scale=1.0):
                J = job(it, seg, h, l, what)
                act.wait_ge(J.filled, J.nth)
                ps = J.bank
                src = ps[:, 0:dst.shape[-1]]
                if bias is None:
                    i = act.copy(dst, src)
                else:
                    i = act.activation(dst, src, ACT.Identity, bias=bias, scale=scale)
                i.then_inc(J.drained, 1)

            def natural(it, seg, h, l, dst):
                for j in range(2):
                    J = job(it, seg, h, l, f"nat{j}")
                    act.wait_ge(J.filled, J.nth)
                    ps = J.bank
                    s = nat(j)
                    act.copy(dst[:, s[0]:s[-1] + 1, 0:D],
                             ps[:, 0:len(s) * D].rearrange("p (s d) -> p s d", d=D)
                             ).then_inc(J.drained, 1)

            def v_(l, name):
                return vec[:, l, VEC[name]:VEC[name] + 1]

            act.wait_ge(w_in.sem, 16 * N_W)
            act.wait_ge(set_pool.sem, 4 * HALVES)
            act.wait_ge(set_dve.sem, 1)
            def iteration(it, more):
                for seg, h, l in schedule(more):
                    n = unit(h, l)
                    if seg == "init":
                        natural(it, seg, h, l, h0n[h])
                        for j in range(2):
                            evacuate(it, seg, h, l, f"T{j}", xT[h][:, cols(j)])
                    elif seg == "proj":
                        for j in range(2):
                            evacuate(it, seg, h, l, f"q{j}", qT[h][:, cols(j)], bq4[:, l:l + 1], 0.25)
                        for par, what in enumerate(("ke", "ko")):
                            b = bkm[:, l, par:par + 1]
                            for j in range(2):
                                J = job(it, seg, h, l, f"{what}{j}")
                                act.wait_ge(J.filled, J.nth)
                                ps = J.bank
                                i = act.activation(kT[h][:, 4 * j:4 * j + 4, par, 1:SEQ],
                                                   ps[:, 0:CHUNK].rearrange("p (i k) -> p i k", i=4),
                                                   ACT.Identity, bias=b)
                                if j == 1:
                                    i = act.activation(kT[h][:, :, par, 0], ps[:, CHUNK:width(1)], ACT.Identity, bias=b)
                                i.then_inc(J.drained, 1)
                    elif seg[:4] == "soft":
                        t = int(seg[4])
                        g = (n * TILES + t) % XB
                        act.wait_ge(s_sub.sem, s_sub.at(it, n, t + 1))
                        act.activation(P[g][:], P[g][:], ACT.Exp).then_inc(p_exp.sem, 1)
                    elif seg == "cls":
                        J = job(it, seg, h, l, "score")
                        act.wait_ge(J.filled, J.nth)
                        ps = J.bank
                        act.wait_ge(cls_dve.sem, cls_dve.at(it, n, 2))
                        act.activation(Pc[h][:], ps[0:IMG * HEADS, 0:SEQ], ACT.Exp, bias=sc[h][0:IMG * HEADS, 1:2],
                                       accum_out=sc[h][0:IMG * HEADS, 2:3]).then_inc(J.drained, 1)
                        act.wait_ge(cls_dve.sem, cls_dve.at(it, n, 6))
                        act.activation(Ec[h][:, 0:D].rearrange("p (a k) -> p a k", a=2),
                                       Vc[h][:, 0, 1:SEQ].unsqueeze(1).broadcast_to([IMG, 2, PATCHES]),
                                       ACT.Exp, scale=1.0 / HEADS)
                        act.activation(Ec[h][:, D:D + 1], Vc[h][:, 0, 0:1], ACT.Exp,
                                       scale=1.0 / HEADS).then_inc(cls_act.sem, 1)
                    elif seg == "mix":
                        act.wait_ge(u_in.sem, u_in.at(it, n))
                        for a in range(2):
                            p = slice(PATCHES * a, PATCHES * (a + 1))
                            act.activation(EX[h][p, :, PATCHES * a:PATCHES * (a + 1)], U8[h][p, :, 1:SEQ], ACT.Exp,
                                           scale=1.0 / HEADS)
                        act.activation(ecl[h][:], U8[h][:, :, 0], ACT.Exp, scale=1.0 / HEADS).then_inc(e_in.sem, 1)
                        J = job(it, seg, h, l, "turn")
                        act.wait_ge(J.filled, J.nth)
                        ps = J.bank
                        act.copy(ET[h][:], ps[:, :].rearrange("p (t q) -> p t q", t=TILES)
                                 ).then_inc(J.drained, 1)
                        J = job(it, seg, h, l, "turnc")
                        act.wait_ge(J.filled, J.nth)
                        ps = J.bank
                        act.copy(EcT[h][:], ps[0:IMG, :].rearrange("p (t q) -> p t q", t=TILES)
                                 ).then_inc(J.drained, 1)
                    elif seg == "norm1":
                        for j in range(2):
                            evacuate(it, seg, h, l, f"T{j}", yT[h][:, cols(j)], v_(l, "bt1"), v_(l, "g1"))
                    elif seg == "norm2":
                        for j in range(2):
                            evacuate(it, seg, h, l, f"T{j}", zT[h][:, cols(j)], v_(l, "bt2"), v_(l, "g2"))
                    elif seg[:3] == "ffn":
                        j = int(seg[3])
                        for f in range(FF // D):
                            J = job(it, seg, h, l, f"h{f}")
                            act.wait_ge(J.filled, J.nth)
                            ps = J.bank
                            act.activation(hT[h][:, f, cols(j)], ps[:, 0:width(j)], ACT.Relu,
                                           bias=v_(l, f"b1_{f}")).then_inc(J.drained, 1)
                    elif seg == "next":
                        for j in range(2):
                            evacuate(it, seg, h, l, f"T{j}", xT[h][:, cols(j)], v_(l, "bt3"), v_(l, "g3"))
                        natural(it, seg, h, l, xn[h])
                    elif seg == "moe":
                        for j in range(2):
                            evacuate(it, seg, h, l, f"T{j}", zT[h][:, cols(j)])
                        for R in jobs(it, seg, h, l, "gate"):
                            act.wait_ge(R.drained, R.nth)
                        act.activation(aff[:], aff[:], ACT.Exp).then_inc(moe_act.sem, 1)
                        J = job(it, seg, h, l, "aff")
                        act.wait_ge(J.filled, J.nth)
                        ps = J.bank
                        act.copy(affT[:], ps[:, 0:SEQ]).then_inc(J.drained, 1)
                        for u in range(2):
                            evacuate(it, seg, h, l, f"oh{u}", OHT[:, 4 * u:4 * u + 4, :].rearrange("p s c -> p (s c)"))
                        for u in range(2):
                            J = job(it, seg, h, l, f"ohc{u}")
                            act.wait_ge(J.filled, J.nth)
                            ps = J.bank
                            act.copy(OHcT[:, 4 * u:4 * u + 4, :].rearrange("p s c -> p (s c)"), ps[0:IMG, :]
                                     ).then_inc(J.drained, 1)
                        for t in range(TILES):
                            J = job(it, seg, h, l, f"xin{t}")
                            act.wait_ge(J.filled, J.nth)
                            ps = J.bank
                            act.copy(xin[h][:, :, 2 * t:2 * t + 2, :],
                                     ps[:, 0:2 * D].rearrange("p (s a e) -> p e a s", s=SLOTS, a=2)
                                     ).then_inc(J.drained, 1)
                        for u in range(2):
                            for R in jobs(it, seg, h, l, f"up{u}"):
                                act.wait_ge(R.drained, R.nth)
                            v = hid[h][:, HALF_E * u:HALF_E * (u + 1), :]
                            act.activation(v, v, ACT.Gelu_apprx_tanh).then_inc(moe_act.sem, 1)
                        for u in range(2):
                            evacuate(it, seg, h, l, f"yT{u}", Y[h][:, 4 * u:4 * u + 4, :].rearrange("p s d -> p (s d)"))

            for it in range(ITERS):
                iteration(it, it + 1 < ITERS)

        @block.vector
        def _(dve):
            dve.wait_ge(w_in.sem, 16 * N_W)
            for h in range(HALVES):
                for z in (h0T, xT, yT, zT):
                    dve.memset(z[h][:, TOK:WIDE], 0.0)
                dve.memset(xn[h][:, :, D:D + 1], 1.0)
                dve.tensor_tensor(h0T[h][:, 2 * CHUNK:TOK], pv[:, 1:2].broadcast_to([D, IMG]),
                                  posT[:, 0:1].broadcast_to([D, IMG]), ALU.mult)
            for par in range(2):
                w = wq[:, :, 1 + par, :].rearrange("p l (g a c) -> p l g a c", a=2, c=HD)
                for l in range(LAYERS):
                    dve.memset(w[:, l, :, 1 - par, :], 0.0)
                dve.tensor_scalar(bkm[:, :, par], vec[:, :, VEC["bk"]], c_("par")[:, par:par + 1], None, ALU.mult)
            dve.tensor_scalar(bq4[:], vec[:, :, VEC["bq"]], 0.25, None, ALU.mult).then_inc(set_dve.sem, 1)
            for i in range(SBANKS):
                dve.memset(sc[i][:], 0.0).then_inc(s_sub.sem, 1)

            def patch(it, c):
                h = c // 2
                dve.wait_ge(patch_sum.sem, patch_sum.at(it, 0, c + 1))
                c = c % 2
                dve.scalar_tensor_tensor(
                    h0T[h][:, CHUNK * c:CHUNK * (c + 1)].rearrange("p (i k) -> p i k", i=4),
                    pp[:, 0:CHUNK].rearrange("p (i k) -> p i k", i=4), pv[:, 0:1],
                    posT[:, 1:SEQ].unsqueeze(1).broadcast_to([D, 4, PATCHES]), ALU.add, ALU.mult
                ).then_inc(patch_out.sem, 1)

            def norm(it, seg, h, l, source, dst, ring=None):
                u = ln_order[(seg, h, l)]
                src = {}
                for j in range(2):
                    src[j] = source(j)
                    for i, s in enumerate(nat(j)):
                        ins = dve.bn_stats(st[h][:, s, :], src[j][:, i, :])
                    ins.then_inc(ln_st.sem, 1)
                    dve.wait_ge(ln_st.sem, ln_st.at(it, u, j + 1))
                    for s in nat(j):
                        ins = dve.bn_aggr(mv[h][:, s, :], st[h][:, s, :])
                    ins.then_inc(ln_mv.sem, 1)
                for j in range(2):
                    dve.wait_ge(ln_rs.sem, ln_rs.at(it, u, j + 1))
                    for i, s in enumerate(nat(j)):
                        ins = dve.tensor_scalar(dst[:, s, 0:D], src[j][:, i, :], mv[h][:, s, 0:1], rs[h][:, s:s + 1],
                                                ALU.subtract, ALU.mult)
                    if ring:
                        ins.then_inc(job(it, seg, h, l, ring[j]).drained, 1)
                    else:
                        ins.then_inc(ln_in.sem, 1)

            def heads(it, n, h, t):
                g = (n * TILES + t) % XB
                dve.wait_ge(p_mul.sem, p_mul.at(it, n, t + 1))
                dve.tensor_reduce(A8[h][:, t, :], P[g][:].rearrange("p h k -> p k h"), X, ALU.add).then_inc(a_in.sem, 1)

            for c in range(4):
                patch(0, c)
            def iteration(it, more):
                for seg, h, l in schedule(more):
                    n = unit(h, l)
                    C = IMG * HEADS
                    if seg == "patch":
                        patch(it + 1, l)
                    elif seg == "init":
                        def src(j):
                            for R in jobs(it, seg, h, l, f"nat{j}"):
                                dve.wait_ge(R.drained, R.nth)
                            return h0n[h][:, nat(j)[0]:nat(j)[-1] + 1, :]
                        norm(it, seg, h, l, src, xn[h])
                    elif seg[:4] == "soft":
                        t = int(seg[4])
                        T = n * TILES + t
                        g = T % XB
                        dve.wait_ge(s_full.sem, s_full.at(it, n, t + 1))
                        s4 = S[T % SBANKS][:, :, 0:4 * SEQ].rearrange("p b (h k) -> p b h k", h=4)
                        dve.tensor_reduce(mx[g][:].rearrange("p (b h) -> p b h", b=2), s4, X, ALU.max
                                          ).then_inc(s_max.sem, 1)
                        dve.wait_ge(s_max.sem, s_max.at(it, n, t + 1))
                        dve.tensor_tensor(P[g][:].rearrange("p (b h) k -> p b h k", b=2), s4,
                                          mx[g][:].rearrange("p (b h) -> p b h", b=2).unsqueeze(3)
                                          .broadcast_to([D, 2, 4, SEQ]), ALU.subtract).then_inc(s_sub.sem, 1)
                        if t >= 2:
                            heads(it, n, h, t - 2)
                        dve.wait_ge(p_exp.sem, p_exp.at(it, n, t + 1))
                        dve.tensor_reduce(sm[g][:], P[g][:], X, ALU.add).then_inc(p_sum.sem, 1)
                        dve.wait_ge(p_sum.sem, p_sum.at(it, n, t + 1))
                        dve.reciprocal(sm[g][:], sm[g][:]).then_inc(p_rec.sem, 1)
                    elif seg == "cls":
                        J = job(it, seg, h, l, "score")
                        dve.wait_ge(J.filled, J.nth)
                        ps = J.bank
                        dve.tensor_reduce(sc[h][0:C, 0:1], ps[0:C, 0:SEQ], X, ALU.max).then_inc(cls_dve.sem, 1)
                        dve.wait_ge(cls_dve.sem, cls_dve.at(it, n, 1))
                        dve.tensor_scalar(sc[h][0:C, 1:2], sc[h][0:C, 0:1], -1.0, None, ALU.mult
                                          ).then_inc(cls_dve.sem, 1)
                        for R in jobs(it, seg, h, l, "score"):
                            dve.wait_ge(R.drained, R.nth)
                        dve.reciprocal(sc[h][0:C, 3:4], sc[h][0:C, 2:3]).then_inc(cls_dve.sem, 1)
                        dve.wait_ge(cls_dve.sem, cls_dve.at(it, n, 3))
                        dve.tensor_scalar(Pc[h][:], Pc[h][:], sc[h][0:C, 3:4], None, ALU.mult).then_inc(cls_dve.sem, 1)
                        J = job(it, seg, h, l, "heads")
                        dve.wait_ge(J.filled, J.nth)
                        ps = J.bank
                        dve.scalar_tensor_tensor(Vc[h][:, 0, :], ps[0:IMG, 0:SEQ], 0.0, c_("negc")[0:IMG, :],
                                                 ALU.not_equal, ALU.mult).then_inc(cls_dve.sem, 1)
                        dve.tensor_tensor(Vc[h][:, 1, :], ps[0:IMG, 0:SEQ], c_("posc")[0:IMG, :], ALU.add
                                          ).then_inc(J.drained, 1)
                        dve.wait_ge(cls_dve.sem, cls_dve.at(it, n, 5))
                        for R in jobs(it, seg, h, l, "heads"):
                            dve.wait_ge(R.drained, R.nth)
                        dve.tensor_tensor(Vc[h][:, 0, :], Vc[h][:, 0, :], Vc[h][:, 1, :], ALU.add
                                          ).then_inc(cls_dve.sem, 1)
                        dve.wait_ge(cls_act.sem, cls_act.at(it, n))
                        dve.tensor_reduce(sc[h][0:IMG, 4:5], Ec[h][:, PATCHES:D + 1], X, ALU.add
                                          ).then_inc(cls_dve.sem, 1)
                        dve.wait_ge(cls_dve.sem, cls_dve.at(it, n, 7))
                        dve.reciprocal(sc[h][0:IMG, 5:6], sc[h][0:IMG, 4:5]).then_inc(cls_dve.sem, 1)
                        dve.tensor_scalar(LC[h][0:IMG, TILES, :], ident[0:IMG, 0:IMG], Ec[h][:, D:D + 1], None,
                                          ALU.mult).then_inc(cls_dve.sem, 1)
                        J = job(it, seg, h, l, "turn")
                        dve.wait_ge(J.filled, J.nth)
                        ps = J.bank
                        dve.tensor_tensor(LC[h][:, 0:TILES, :], onehot[:, 0:TILES, :],
                                          ps[:, 0:IMG].unsqueeze(1).broadcast_to([D, TILES, IMG]), ALU.mult
                                          ).then_inc(J.drained, 1)
                    elif seg == "mix":
                        heads(it, n, h, TILES - 2)
                        heads(it, n, h, TILES - 1)
                        dve.wait_ge(a_in.sem, a_in.at(it, n))
                        dve.scalar_tensor_tensor(U8[h][:], A8[h][:], 0.0,
                                                 c_("neg").unsqueeze(1).broadcast_to([D, TILES, SEQ]),
                                                 ALU.not_equal, ALU.mult).then_inc(u_in.sem, 1)
                        dve.tensor_tensor(A8[h][:], A8[h][:], c_("pos8").unsqueeze(1).broadcast_to([D, TILES, SEQ]),
                                          ALU.add).then_inc(u_in.sem, 1)
                        dve.wait_ge(u_in.sem, u_in.at(it, n, 2))
                        dve.tensor_tensor(U8[h][:], U8[h][:], A8[h][:], ALU.add).then_inc(u_in.sem, 1)
                        dve.wait_ge(e_in.sem, e_in.at(it, n))
                        dve.tensor_tensor(EX[h][:, :, D:D + IMG], onehot[:, 0:TILES, :],
                                          ecl[h][:].unsqueeze(2).broadcast_to([D, TILES, IMG]), ALU.mult
                                          ).then_inc(ec_in.sem, 1)
                        for j in range(2):
                            J = job(it, seg, h, l, f"mix{j}")
                            dve.wait_ge(J.filled, J.nth)
                            ps = J.bank
                            v = ps[:, 0:2 * (D + 1)].rearrange("p (t d) -> p t d", t=2)
                            dve.reciprocal(sc[h][:, 8 + 2 * j:10 + 2 * j], v[:, :, D]).then_inc(r_rec.sem, 1)
                            dve.wait_ge(r_rec.sem, r_rec.at(it, n, j + 1))
                            for i in range(2):
                                t = 2 * j + i
                                ins = dve.scalar_tensor_tensor(r1[h][:, t, :], v[:, i, 0:D], sc[h][:, 8 + t:9 + t],
                                                               xn[h][:, t, 0:D], ALU.mult, ALU.add)
                            ins.then_inc(J.drained, 1)
                        J = job(it, seg, h, l, "mixc")
                        dve.wait_ge(J.filled, J.nth)
                        ps = J.bank
                        dve.wait_ge(cls_dve.sem, cls_dve.at(it, n, 8))
                        dve.scalar_tensor_tensor(r1[h][0:IMG, TILES, :], ps[0:IMG, 0:D], sc[h][0:IMG, 5:6],
                                                 xn[h][0:IMG, TILES, 0:D], ALU.mult, ALU.add
                                                 ).then_inc(J.drained, 1)
                    elif seg == "norm1":
                        if l == 0:
                            dve.wait_ge(out_done[h].sem, out_done[h].at(it, 0, 0))

                        def src(j):
                            for R in jobs(it, "mix", h, l, *((f"mix{j}",) if j == 0 else ("mix1", "mixc"))):
                                dve.wait_ge(R.drained, R.nth)
                            return r1[h][:, nat(j)[0]:nat(j)[-1] + 1, :]
                        norm(it, seg, h, l, src, nn[h])
                    elif seg in ("norm2", "norm3"):
                        if seg == "norm3":
                            for j in range(2):
                                J = job(it, seg, h, l, f"out{j}")
                                dve.wait_ge(J.filled, J.nth)
                                ps = J.bank
                                dve.scalar_tensor_tensor(yT[h][:, cols(j)], ps[:, 0:width(j)],
                                                         vec[:, l, VEC["b2"]:VEC["b2"] + 1], zT[h][:, cols(j)],
                                                         ALU.add, ALU.add).then_inc(J.drained, 1)

                        def src(j):
                            J = job(it, seg, h, l, f"nat{j}")
                            dve.wait_ge(J.filled, J.nth)
                            ps = J.bank
                            return ps[:, 0:len(nat(j)) * D].rearrange("p (s d) -> p s d", d=D)
                        norm(it, seg, h, l, src, nn[h], ("nat0", "nat1"))
                    elif seg == "moe":
                        def step(ins):
                            ins.then_inc(moe_dve.sem, 1)

                        def after(k):
                            dve.wait_ge(moe_dve.sem, moe_dve.at(it, h, k))

                        for R in jobs(it, "next", h, LAYERS - 1, "nat0", "nat1"):
                            dve.wait_ge(R.drained, R.nth)
                        step(dve.tensor_tensor(h0n[h][:], h0n[h][:], xn[h][:, :, 0:D], ALU.add))
                        after(1)
                        norm(it, seg, h, l, lambda j: h0n[h][:, nat(j)[0]:nat(j)[-1] + 1, :], nn[h])
                        J = job(it, seg, h, l, "gate")
                        dve.wait_ge(J.filled, J.nth)
                        ps = J.bank
                        g3 = ps[:, 0:SLOTN * EXPERTS].rearrange("p (s e) -> p s e", e=EXPERTS)
                        step(dve.tensor_reduce(mxg[:], g3, X, ALU.max))
                        after(2)
                        dve.tensor_tensor(aff[:], g3, mxg[:].unsqueeze(2).broadcast_to([D, SLOTN, EXPERTS]),
                                          ALU.subtract).then_inc(J.drained, 1)
                        dve.wait_ge(moe_act.sem, moe_act.at(it, h, 1))
                        step(dve.tensor_reduce(smg[:], aff[:], X, ALU.add))
                        after(3)
                        step(dve.reciprocal(smg[:], smg[:]))
                        after(4)
                        step(dve.tensor_tensor(aff[:], aff[:], smg[:].unsqueeze(2).broadcast_to([D, SLOTN, EXPERTS]),
                                               ALU.mult))
                        after(5)
                        step(dve.tensor_tensor(AX, aff[:].unsqueeze(2).broadcast_to([D, SLOTN, IMG, EXPERTS]),
                                               onehot.unsqueeze(3).broadcast_to([D, SLOTN, IMG, EXPERTS]), ALU.mult))
                        for R in jobs(it, seg, h, l, "aff"):
                            dve.wait_ge(R.drained, R.nth)
                        step(dve.max(gv[:], affT[:]))
                        after(7)
                        step(dve.max_index(gi[:], gv[:], affT[:]))
                        after(8)
                        step(dve.tensor_copy(gf[:], gi[:]))
                        after(9)
                        step(dve.tensor_tensor(OH[:], gf[:].unsqueeze(2).broadcast_to([D, SLOTS, D]),
                                               c_("target").unsqueeze(1).broadcast_to([D, SLOTS, D]), ALU.is_equal))
                        step(dve.tensor_tensor(OHc[:], gf[:].unsqueeze(2).broadcast_to([D, SLOTS, IMG]),
                                               c_("targetc").unsqueeze(1).broadcast_to([D, SLOTS, IMG]), ALU.is_equal))
                        J = job(it, seg, h, l, "ohc1")
                        dve.wait_ge(J.filled, J.nth)
                        step(dve.tensor_tensor(OH[:], OH[:], gv[:].unsqueeze(2).broadcast_to([D, SLOTS, D]), ALU.mult))
                        step(dve.tensor_tensor(OHc[:], OHc[:], gv[:].unsqueeze(2).broadcast_to([D, SLOTS, IMG]),
                                               ALU.mult))
                        hid4 = hid[h].rearrange("p e (i s) -> p e i s", i=IMG)
                        for name, dst, k in (("up", hid4, 0), ("down", eo4, 1)):
                            for u in range(2):
                                e = slice(HALF_E * u, HALF_E * (u + 1))
                                J = job(it, seg, h, l, f"{name}{u}")
                                dve.wait_ge(J.filled, J.nth)
                                ps = J.bank
                                dve.tensor_tensor(dst[:, e, :, :], ps[:, :].rearrange("p (e i s) -> p e i s", i=IMG,
                                                                                      s=SLOTS),
                                                  ev[:, k, e].unsqueeze(2).unsqueeze(3).broadcast_to(
                                                      [D, HALF_E, IMG, SLOTS]), ALU.add
                                                  ).then_inc(J.drained, 1)
                        for t in range(TILES):
                            J = job(it, seg, h, l, f"sum{t}")
                            dve.wait_ge(J.filled, J.nth)
                            ps = J.bank
                            dve.tensor_tensor(nn[h][:, t, :], ps[:, 0:D], h0n[h][:, t, :], ALU.add
                                              ).then_inc(J.drained, 1)
                        J = job(it, seg, h, l, "sumc")
                        dve.wait_ge(J.filled, J.nth)
                        ps = J.bank
                        dve.tensor_tensor(nn[h][0:IMG, TILES, :], ps[0:IMG, 0:D], h0n[h][0:IMG, TILES, :], ALU.add
                                          ).then_inc(J.drained, 1)

            for it in range(ITERS):
                iteration(it, it + 1 < ITERS)

        @block.tensor
        def _(pe):
            mm = pe.matmul

            def patch(it, c):
                i = c % 2
                pe.wait_ge(pix_in[i].sem, pix_in[i].at(it, 0, 32 * (c // 2 + 1)))
                pe.wait_ge(patch_out.sem, patch_out.at(it, 0, c))
                for k in range(MAIN):
                    mm(pp[:, 0:CHUNK], wpm[:, k, :], pix[i][:, k, :], start=(k == 0), stop=False)
                mm(pp[:, 0:CHUNK], wpr[:], pixr[i][:], start=False, stop=True).then_inc(patch_sum.sem, 1)

            def to_natural(it, seg, h, l, src):
                for j in range(2):
                    J = job(it, seg, h, l, f"nat{j}")
                    pe.wait_ge(J.drained, J.before)
                    ps = J.bank
                    for i, s in enumerate(nat(j)):
                        ins = pe.transpose(ps[:, D * i:D * (i + 1)], src[:, D * s:D * (s + 1)], ident)
                    ins.then_inc(J.filled, 1)

            def to_T(it, seg, h, l, src, ready):
                for j in range(2):
                    pe.wait_ge(*ready(j))
                    J = job(it, seg, h, l, f"T{j}")
                    pe.wait_ge(J.drained, J.before)
                    ps = J.bank
                    for i, s in enumerate(nat(j)):
                        if s < TILES:
                            ins = pe.transpose(ps[:, D * i:D * (i + 1)], src[:, s, 0:D], ident)
                        else:
                            ins = pe.transpose(ps[:, D * i:D * i + IMG], src[0:IMG, s, 0:D], ident[0:IMG, 0:IMG])
                    ins.then_inc(J.filled, 1)

            pe.wait_ge(w_in.sem, 16 * N_W)
            pe.wait_ge(set_pool.sem, 4 * HALVES)
            pe.wait_ge(set_dve.sem, 1)
            for c in range(4):
                patch(0, c)
            def iteration(it, more):
                for seg, h, l in schedule(more):
                    n = unit(h, l)
                    if seg == "patch":
                        patch(it + 1, l)
                    elif seg == "init":
                        pe.wait_ge(patch_out.sem, patch_out.at(it, 0, 2 * h + 2))
                        to_natural(it, seg, h, l, h0T[h])
                        to_T(it, seg, h, l, xn[h], lambda j: (ln_in.sem, ln_in.at(it, ln_in_order[(seg, h, l)], j + 1)))
                    elif seg == "proj":
                        for k, what in enumerate(("q", "ke", "ko")):
                            for j in range(2):
                                if k == 0:
                                    for R in jobs(it, *(("init", h, 0) if l == 0 else ("next", h, l - 1)), f"T{j}"):
                                        pe.wait_ge(R.drained, R.nth)
                                J = job(it, seg, h, l, f"{what}{j}")
                                pe.wait_ge(J.drained, J.before)
                                ps = J.bank
                                mm(ps[:, 0:width(j)], wq[:, l, k, :], xT[h][:, cols(j)], start=True, stop=True
                                   ).then_inc(J.filled, 1)
                    elif seg[:4] == "soft":
                        t = int(seg[4])
                        T = n * TILES + t
                        if t == 0:
                            for R in jobs(it, "proj", h, l, "q0", "q1", "ke0", "ke1", "ko0", "ko1"):
                                pe.wait_ge(R.drained, R.nth)
                        pe.wait_ge(s_sub.sem, s_sub.at(it, n, t - 1))
                        for k, g in enumerate((0, 2, 1, 3)):
                            f = slice(32 * g, 32 * g + 32)
                            if k >= 2:
                                pe.wait_ge(s_row.sem, s_row.at(it, n, 2 * t + k - 1))
                            for a in range(2):
                                i = 2 * t + a
                                ins = mm(S[T % SBANKS][PATCHES * a:PATCHES * (a + 1), g // 2,
                                                       2 * SEQ * (g % 2):2 * SEQ * (g % 2 + 1)],
                                         qT[h][f, PATCHES * i:PATCHES * (i + 1)],
                                         kT[h][f, i, :, :].rearrange("p a k -> p (a k)"), start=True, stop=True)
                            if k < 2:
                                ins.then_inc(s_row.sem, 1)
                        ins.then_inc(s_full.sem, 1)
                    elif seg == "cls":
                        pe.wait_ge(qx_in.sem, qx_in.at(it, n))
                        J = job(it, seg, h, l, "score")
                        pe.wait_ge(J.drained, J.before)
                        ps = J.bank
                        C = IMG * HEADS
                        for i in range(IMG):
                            for par in range(2):
                                ins = mm(ps[0:C, 0:SEQ], qx[h][:, C * i:C * (i + 1)], kT[h][:, i, par, :],
                                         start=(i == 0 and par == 0), stop=(i == IMG - 1 and par == 1))
                        ins.then_inc(J.filled, 1)
                        pe.wait_ge(cls_dve.sem, cls_dve.at(it, n, 4))
                        J = job(it, seg, h, l, "heads")
                        pe.wait_ge(J.drained, J.before)
                        ps = J.bank
                        mm(ps[0:IMG, 0:SEQ], c_("hsum")[0:C, :], Pc[h][:], start=True, stop=True
                           ).then_inc(J.filled, 1)
                        pe.wait_ge(cls_act.sem, cls_act.at(it, n))
                        J = job(it, seg, h, l, "turn")
                        pe.wait_ge(J.drained, J.before)
                        ps = J.bank
                        pe.transpose(ps[:, 0:IMG], Ec[h][:, 0:D], ident[0:IMG, 0:IMG]
                                     ).then_inc(J.filled, 1)
                    elif seg == "mix":
                        pe.wait_ge(ec_in.sem, ec_in.at(it, n))
                        J = job(it, seg, h, l, "turn")
                        pe.wait_ge(J.drained, J.before)
                        ps = J.bank
                        for t in range(TILES):
                            ins = pe.transpose(ps[:, D * t:D * (t + 1)], EX[h][:, t, 0:D], ident)
                        ins.then_inc(J.filled, 1)
                        J = job(it, seg, h, l, "turnc")
                        pe.wait_ge(J.drained, J.before)
                        ps = J.bank
                        for t in range(TILES):
                            ins = pe.transpose(ps[0:IMG, D * t:D * (t + 1)], EX[h][:, t, D:D + IMG], ident)
                        ins.then_inc(J.filled, 1)
                        for R in jobs(it, seg, h, l, "turn", "turnc"):
                            pe.wait_ge(R.drained, R.nth)
                        if l > 0:
                            for R in jobs(it, "next", h, l - 1, "nat0", "nat1"):
                                pe.wait_ge(R.drained, R.nth)
                        for j in range(2):
                            J = job(it, seg, h, l, f"mix{j}")
                            pe.wait_ge(J.drained, J.before)
                            ps = J.bank
                            for i in range(2):
                                t = 2 * j + i
                                o = ps[:, (D + 1) * i:(D + 1) * (i + 1)]
                                mm(o, ET[h][:, t, :], xn[h][:, t, :], start=True, stop=False)
                                ins = mm(o, EcT[h][:, t, :], xn[h][0:IMG, TILES, :], start=False, stop=True)
                            ins.then_inc(J.filled, 1)
                        J = job(it, seg, h, l, "mixc")
                        pe.wait_ge(J.drained, J.before)
                        ps = J.bank
                        pe.wait_ge(cls_dve.sem, cls_dve.at(it, n, 9))
                        for R in jobs(it, "cls", h, l, "turn"):
                            pe.wait_ge(R.drained, R.nth)
                        for t in range(TILES):
                            mm(ps[0:IMG, 0:D], LC[h][:, t, :], xn[h][:, t, 0:D], start=(t == 0), stop=False)
                        mm(ps[0:IMG, 0:D], LC[h][0:IMG, TILES, :], xn[h][0:IMG, TILES, 0:D], start=False, stop=True
                           ).then_inc(J.filled, 1)
                    elif seg == "norm1":
                        to_T(it, seg, h, l, nn[h], lambda j: (ln_in.sem, ln_in.at(it, ln_in_order[(seg, h, l)], j + 1)))
                    elif seg == "norm2":
                        for R in jobs(it, "norm1", h, l, "T0", "T1"):
                            pe.wait_ge(R.drained, R.nth)
                        to_natural(it, seg, h, l, yT[h])
                        to_T(it, seg, h, l, nn[h], lambda j: job(it, seg, h, l, f"nat{j}")[2:4])
                    elif seg[:3] == "ffn":
                        j = int(seg[3])
                        for R in jobs(it, "norm2", h, l, f"T{j}"):
                            pe.wait_ge(R.drained, R.nth)
                        for f in range(FF // D):
                            J = job(it, seg, h, l, f"h{f}")
                            pe.wait_ge(J.drained, J.before)
                            ps = J.bank
                            mm(ps[:, 0:width(j)], w1s[:, l, D * f:D * (f + 1)], zT[h][:, cols(j)], start=True,
                               stop=True).then_inc(J.filled, 1)
                    elif seg == "norm3":
                        for j in range(2):
                            for R in jobs(it, f"ffn{j}", h, l, "h0", "h1", "h2", "h3"):
                                pe.wait_ge(R.drained, R.nth)
                            J = job(it, seg, h, l, f"out{j}")
                            pe.wait_ge(J.drained, J.before)
                            ps = J.bank
                            for f in range(FF // D):
                                ins = mm(ps[:, 0:width(j)], w2s[:, l, f, :], hT[h][:, f, cols(j)], start=(f == 0),
                                         stop=(f == FF // D - 1))
                            ins.then_inc(J.filled, 1)
                        for R in jobs(it, seg, h, l, "out0", "out1"):
                            pe.wait_ge(R.drained, R.nth)
                        to_natural(it, seg, h, l, yT[h])
                    elif seg == "next":
                        to_T(it, seg, h, l, nn[h], lambda j: job(it, "norm3", h, l, f"nat{j}")[2:4])
                        for R in jobs(it, seg, h, l, "T0", "T1"):
                            pe.wait_ge(R.drained, R.nth)
                        to_natural(it, seg, h, l, xT[h])
                    elif seg == "moe":
                        to_T(it, seg, h, l, nn[h], lambda j: (ln_in.sem, ln_in.at(it, ln_in_order[(seg, h, l)], j + 1)))
                        for R in jobs(it, seg, h, l, "T0", "T1"):
                            pe.wait_ge(R.drained, R.nth)
                        J = job(it, seg, h, l, "gate")
                        pe.wait_ge(J.drained, J.before)
                        ps = J.bank
                        for s in range(SLOTN):
                            ins = mm(ps[:, EXPERTS * s:EXPERTS * (s + 1)], zT[h][:, D * s:D * (s + 1)], gw[:],
                                     start=True, stop=True)
                        ins.then_inc(J.filled, 1)
                        pe.wait_ge(moe_dve.sem, moe_dve.at(it, h, 6))
                        J = job(it, seg, h, l, "aff")
                        pe.wait_ge(J.drained, J.before)
                        ps = J.bank
                        mm(ps[:, 0:1], AX[:, TILES].rearrange("p i e -> p (i e)"), xn[h][:, 0, D:D + 1], start=True,
                           stop=True)
                        for t in range(TILES):
                            ins = mm(ps[:, 1:SEQ], AX[:, t].rearrange("p i e -> p (i e)"), c_("stackI"), start=(t == 0),
                                     stop=(t == TILES - 1))
                        ins.then_inc(J.filled, 1)
                        pe.wait_ge(moe_dve.sem, moe_dve.at(it, h, 11))
                        for u in range(2):
                            J = job(it, seg, h, l, f"oh{u}")
                            pe.wait_ge(J.drained, J.before)
                            ps = J.bank
                            for k in range(4):
                                ins = pe.transpose(ps[:, D * k:D * (k + 1)], OH[:, 4 * u + k, :], ident)
                            ins.then_inc(J.filled, 1)
                        for u in range(2):
                            J = job(it, seg, h, l, f"ohc{u}")
                            pe.wait_ge(J.drained, J.before)
                            ps = J.bank
                            for k in range(4):
                                ins = pe.transpose(ps[0:IMG, D * k:D * (k + 1)], OHc[:, 4 * u + k, :], ident)
                            ins.then_inc(J.filled, 1)
                        for R in jobs(it, seg, h, l, "oh0", "oh1", "ohc0", "ohc1"):
                            pe.wait_ge(R.drained, R.nth)
                        for t in range(TILES):
                            J = job(it, seg, h, l, f"xin{t}")
                            pe.wait_ge(J.drained, J.before)
                            ps = J.bank
                            pair = slice(32 * t, 32 * t + 32)
                            mm(ps[:, 0:2 * D], nn[h][:, t, :], OHT[:, :, pair], start=True, stop=False)
                            mm(ps[:, 0:2 * D], nn[h][0:IMG, TILES, :], OHcT[:, :, pair], start=False, stop=True
                               ).then_inc(J.filled, 1)
                        for R in jobs(it, seg, h, l, "xin0", "xin1", "xin2", "xin3"):
                            pe.wait_ge(R.drained, R.nth)
                        for u in range(2):
                            J = job(it, seg, h, l, f"up{u}")
                            pe.wait_ge(J.drained, J.before)
                            ps = J.bank
                            for k in range(HALF_E):
                                e = HALF_E * u + k
                                ins = mm(ps[:, PATCHES * k:PATCHES * (k + 1)], ew1s[:, e, :],
                                         xin[h][:, e].rearrange("p i s -> p (i s)"), start=True, stop=True)
                            ins.then_inc(J.filled, 1)
                        for u in range(2):
                            pe.wait_ge(moe_act.sem, moe_act.at(it, h, 2 + u))
                            J = job(it, seg, h, l, f"down{u}")
                            pe.wait_ge(J.drained, J.before)
                            ps = J.bank
                            for k in range(HALF_E):
                                e = HALF_E * u + k
                                ins = mm(ps[:, PATCHES * k:PATCHES * (k + 1)], ew2s[:, e, :], hid[h][:, e, :],
                                         start=True, stop=True)
                            ins.then_inc(J.filled, 1)
                        for R in jobs(it, seg, h, l, "down0", "down1"):
                            pe.wait_ge(R.drained, R.nth)
                        for u in range(2):
                            J = job(it, seg, h, l, f"yT{u}")
                            pe.wait_ge(J.drained, J.before)
                            ps = J.bank
                            for k in range(4):
                                ins = pe.transpose(ps[:, D * k:D * (k + 1)], eo[:, 4 * u + k, :], ident)
                            ins.then_inc(J.filled, 1)
                        for R in jobs(it, seg, h, l, "yT0", "yT1"):
                            pe.wait_ge(R.drained, R.nth)
                        pe.wait_ge(moe_dve.sem, moe_dve.at(it, h, 13))
                        for t in range(TILES):
                            J = job(it, seg, h, l, f"sum{t}")
                            pe.wait_ge(J.drained, J.before)
                            ps = J.bank
                            pair = slice(32 * t, 32 * t + 32)
                            for s in range(SLOTS):
                                ins = mm(ps[:, 0:D], OH[pair, s, :], Y[h][pair, s, :], start=(s == 0),
                                         stop=(s == SLOTS - 1))
                            ins.then_inc(J.filled, 1)
                        J = job(it, seg, h, l, "sumc")
                        pe.wait_ge(J.drained, J.before)
                        ps = J.bank
                        for s in range(SLOTS):
                            ins = mm(ps[0:IMG, 0:D], OHc[:, s, :], Y[h][:, s, :], start=(s == 0),
                                     stop=(s == SLOTS - 1))
                        ins.then_inc(J.filled, 1)

            for it in range(ITERS):
                iteration(it, it + 1 < ITERS)


def kernel(**inputs):
    import concourse.bacc as _bacc
    from concourse.bass_utils import run_bass_kernel_spmd as _run

    a = {k: np.asarray(v) for k, v in inputs.items()}
    chunks = B // 4
    x = a["x"].reshape(chunks, 4, 3, 8, 28, 8, 28).transpose(0, 2, 4, 6, 1, 3, 5).reshape(chunks, IN_D, CHUNK)
    w = a["L0_tok_W"].T
    L = "L0_attn_"
    vecs = [a[L + "bqkv"][:, 0:D], a[L + "bqkv"][:, D:2 * D], a[L + "g1"], a[L + "bt1"], a[L + "g2"], a[L + "bt2"],
            a[L + "b2"], a[L + "g3"], a[L + "bt3"]] + [a[L + "b1"][:, D * f:D * (f + 1)] for f in range(FF // D)]
    arrays = {
        "x_main": x[:, :MAIN * D].reshape(chunks, D, MAIN, CHUNK),
        "x_rest": x[:, MAIN * D:],
        "wp_main": w[:MAIN * D].reshape(D, MAIN, D),
        "wp_rest": w[MAIN * D:],
        "pvec": np.stack([a["L0_tok_b"], a["L0_tok_class_token"][0]], 1),
        "post": a["L0_tok_pos_embed"].T,
        "const": shape_constants(),
        "wqk": a[L + "Wqkv"][:, 0:2 * D].reshape(LAYERS, 2, D, D).transpose(3, 0, 1, 2),
        "w1": a[L + "W1"].transpose(2, 0, 1),
        "w2": a[L + "W2"].reshape(LAYERS, D, FF // D, D).transpose(3, 0, 2, 1),
        "lvec": np.stack(vecs, 2).transpose(1, 0, 2),
        "gate": a["L0_ffn_gate_weight"],
        "ew1": a["L0_ffn_w1"].transpose(1, 0, 2),
        "ew2": a["L0_ffn_w2"].transpose(1, 0, 2),
        "evec": np.stack([a["L0_ffn_b1"], a["L0_ffn_b2"]]).transpose(2, 0, 1),
    }
    arrays = {k: np.ascontiguousarray(v) for k, v in arrays.items()}
    nc = _bacc.Bacc("TRN2", target_bir_lowering=False, num_devices=1)
    args = [nc.dram_tensor(k, v.shape, mybir.dt.from_np(v.dtype), kind="ExternalInput").ap() for k, v in arrays.items()]
    args.append(nc.dram_tensor("out", (B, SEQ, D), F32, kind="ExternalOutput").ap())
    vit_kernel(nc, *args)
    r = _run(nc, [arrays], core_ids=[0])
    return r.results[0]["out"]
```

```python
from contextlib import ExitStack
from typing import NamedTuple

import numpy as np

import concourse.bass as bass
from concourse import mybir

F32 = mybir.dt.float32
U32 = mybir.dt.uint32
ALU = mybir.AluOpType
ACT = mybir.ActivationFunctionType
X = mybir.AxisListType.X

B = 64
PATCHES = 64
SEQ = PATCHES + 1
D = 128
IN_D = 2352
MAIN = IN_D // D
REST = IN_D - MAIN * D
LAYERS, HEADS, HD, FF = 4, 8, 16, 512
EXPERTS, SLOTS, DFF = 16, 8, 128
EPS = 1e-5

HALVES = 2
IMG = 8
ITERS = B // (HALVES * IMG)
TILES = 4
SLOTN = TILES + 1
TOK = IMG * SEQ
WIDE = SLOTN * D
CHUNK = 256
UNITS = LAYERS * HALVES
PAIRS = TILES * HALVES
BLOCKS = MAIN + 1
SBANKS = 2

CONST = {}
for _name, _n in (("ident", D), ("stackI", PATCHES), ("pos8", SEQ), ("neg", SEQ), ("posc", SEQ), ("negc", SEQ),
                  ("onehot", SLOTN * IMG), ("headmask", HEADS), ("hsum", IMG), ("target", D), ("targetc", IMG),
                  ("pow", 16), ("par", 2)):
    _at = sum(w for _, w in CONST.values())
    CONST[_name] = (_at, _n)
CONST_W = sum(w for _, w in CONST.values())
VEC = {n: i for i, n in enumerate(("bq", "bk", "g1", "bt1", "g2", "bt2", "g3", "bt3", "b1_0", "b1_1", "b1_2", "b1_3"))}
NVEC = len(VEC)
ROW = {n: i for i, n in enumerate(("g1", "bt1", "g2", "bt2", "g3", "bt3"))}
NROW = len(ROW)


def shape_constants():
    c = np.zeros((D, CONST_W), np.float32)

    def put(name, a):
        at, n = CONST[name]
        a = np.asarray(a, np.float32)
        c[:a.shape[0], at:at + n] = a.reshape(a.shape[0], n)

    p = np.arange(D)
    q = 1 + p % PATCHES
    k = np.arange(SEQ)
    far = -1e5
    put("ident", np.eye(D))
    put("stackI", p[:, None] % PATCHES == np.arange(PATCHES)[None, :])
    put("pos8", HEADS * np.exp(-np.abs(q[:, None] - k[None, :]).astype(np.float32) * np.float32(0.1)))
    put("neg", far * (k[None, :] > q[:, None]))
    put("posc", np.broadcast_to(HEADS * np.exp(-k.astype(np.float32) * np.float32(0.1)), (D, SEQ)))
    put("negc", np.broadcast_to(far * (k > 0), (D, SEQ)))
    one = np.zeros((D, SLOTN, IMG))
    for t in range(TILES):
        one[p, t, 2 * t + p // PATCHES] = 1
    one[np.arange(IMG), TILES, np.arange(IMG)] = 1
    put("onehot", one)
    put("headmask", p[:, None] // HD == np.arange(HEADS)[None, :])
    put("hsum", p[:, None] // HEADS == np.arange(IMG)[None, :])
    img = p // EXPERTS
    put("target", np.where(img[:, None] % 2 == p[None, :] // PATCHES, 1 + p[None, :] % PATCHES, -1))
    put("targetc", np.where(img[:, None] == np.arange(IMG)[None, :], 0, -1))
    put("pow", np.full((D, 16), -0.5))
    put("par", np.stack([(p // HD) % 2 == 0, (p // HD) % 2 == 1], 1))
    return c


PIECE = 5
PIECES = -(-BLOCKS // PIECE)
ATTN = ("proj", "soft0", "cls1", "soft1", "cls2", "soft2", "cls3", "soft3", "mix1", "mix2", "mix3")
FFN = ("norm1", "norm1b", "norm2", "ffn0", "ffn1", "out", "norm3")
MOE = tuple(f"moe{k}" for k in range(1, 10))
PATCH = tuple(f"patch{k}" for k in range(PIECES))
ORDER = {
    ("layer", "pe"):
        "proj soft0 cls1 soft1 patch0 patch1 norm2 cls2 soft2 cls3 soft3 ffn0 ffn1 out mix2 patch2 patch3 "
        "mix3 norm3",
    ("layer", "act"):
        "proj soft0 cls1 soft1 cls2 norm2 soft2 ffn0 soft3 ffn1 mix1 mix2 norm3",
    ("layer", "dve"):
        "norm1 norm1b soft0 cls1 soft1 norm2 cls2 soft2 cls3 soft3 mix1 out norm3 mix3 patch3",
    ("layer", "pool"):
        "norm1 proj norm1b soft0 soft1 soft2 soft3 mix1 ffn0 out norm3",
    ("last", "pe"):
        "patch0 moe2 moe3 patch1 moe4 moe5 norm2 ffn0 moe6 moe7 ffn1 out patch2 moe8 norm3 patch3 moe9",
    ("last", "act"):
        "moe2 moe3 moe4 moe5 norm2 ffn0 moe6 ffn1 moe8 norm3",
    ("last", "dve"):
        "norm1 moe1 moe2 norm1b moe3 moe4 moe5 norm2 moe6 moe7 out norm3 moe9 patch3",
    ("last", "pool"):
        "moe1 norm1 norm1b ffn0 out norm3",
    ("turn", "pe"):
        "init proj moe2 soft0 cls1 soft1 moe3 cls2 moe4 moe5 soft2 moe6 moe7 cls3 soft3 moe8 moe9 mix2 "
        "mix3 init1",
    ("turn", "act"):
        "init proj moe2 soft0 cls1 soft1 moe3 cls2 moe4 moe5 soft2 moe6 soft3 moe8 mix1 mix2 init1",
    ("turn", "dve"):
        "init moe1 moe2 soft0 cls1 soft1 moe3 cls2 moe4 moe5 soft2 moe6 moe7 cls3 soft3 mix1 moe9 mix3 "
        "init1",
    ("turn", "pool"):
        "init moe1 proj soft0 soft1 soft2 soft3 mix1 init1",
}


def schedule(engine):
    def listed(names, *where):
        return [(n, *where) for n in names]

    def weave(slot, *lists):
        items = {x[0] + ("1" if x[0] == "init" and x[2] == 1 else ""): x for each in lists for x in each}
        return [items[name] for name in ORDER[slot, engine].split() if name in items]

    def patches(it, n):
        return listed(PATCH, it, n // TILES, n % TILES) if it < ITERS else []

    out = []
    for n in range(PAIRS):
        out += patches(0, n)
    for it in range(ITERS):
        if it == 0:
            out += [("init", 0, 0, 0), ("init", 0, 1, 0)] + listed(ATTN, 0, 0, 0)
        for l in range(LAYERS):
            out += weave("layer", listed(ATTN, it, 1, l), listed(FFN, it, 0, l), patches(it + 1, 2 * l))
            if l + 1 < LAYERS:
                out += weave("layer", listed(ATTN, it, 0, l + 1), listed(FFN, it, 1, l), patches(it + 1, 2 * l + 1))
            else:
                out += weave("last", listed(FFN, it, 1, l), listed(MOE, it, 0, 0), patches(it + 1, 2 * l + 1))
        if it + 1 < ITERS:
            out += weave("turn", listed(MOE, it, 1, 0),
                         listed(("init",) + ATTN, it + 1, 0, 0) + [("init", it + 1, 1, 0)])
        else:
            out += listed(MOE, it, 1, 0)
    return out


def ring_jobs(seg, l):
    if seg == "norm3" and l + 1 == LAYERS:
        return []
    return {
        "init": ["T0", "T1"],
        "proj": ["q0", "q1", "ke0", "ke1", "ko0", "ko1"],
        "cls1": ["score"], "cls2": ["heads"], "cls3": ["turn"],
        "mix2": ["turn", "turnc"], "mix3": ["mix0", "mix1", "mixc"],
        "norm2": ["T0", "T1"],
        "ffn0": ["h0", "h1", "h2", "h3"],
        "ffn1": ["h0", "h1", "h2", "h3"],
        "out": ["out0", "out1"],
        "norm3": ["T0", "T1"],
        "moe2": ["T0", "T1", "gate"], "moe3": ["aff"], "moe4": ["oh0", "oh1", "ohc0", "ohc1"],
        "moe5": ["xin0", "xin1", "xin2", "xin3"], "moe6": ["up0", "up1"], "moe7": ["down0", "down1"],
        "moe8": ["yT0", "yT1"], "moe9": ["sum0", "sum1", "sum2", "sum3", "sumc"],
    }.get(seg, [])


RING = 3


def psum_places():
    place, count, n = {}, [0] * RING, 0
    for seg, it, h, l in schedule("pe"):
        for job in ring_jobs(seg, l):
            b = n % RING
            count[b] += 1
            place[(it, seg, h, l, job)] = (b, count[b])
            n += 1
    return place


PLACE = psum_places()


class Signal:

    def __init__(self, sem, per, units, early=0):
        self.sem, self.per, self.units, self.early = sem, per, units, early

    def at(self, it, unit, k=None):
        return (it * self.units + unit) * self.per + (self.per if k is None else k) + self.early


class Job(NamedTuple):

    bank: object
    filled: object
    drained: object
    nth: object
    before: object


def vit_kernel(nc, x_main, x_rest, wp_main, wp_rest, cls0, pos, const, wqk, w1, w2, lvec, rows, gate, ew1, ew2, evec, out):
    ctx = ExitStack()
    with ctx:
        def sb(name, shape, dt=F32):
            return ctx.enter_context(nc.sbuf_tensor(name, shape, dt))

        def both(name, shape):
            return [sb(f"{name}{h}", shape) for h in range(HALVES)]

        def shared(name, shape):
            return [sb(name, shape)] * HALVES

        def signal(name, per=1, units=UNITS, early=0):
            return Signal(ctx.enter_context(nc.semaphore(name)), per, units, early)

        S = [ctx.enter_context(nc.psum_tensor(f"S{i}", [D, 2, 512], F32)) for i in range(SBANKS)]
        ringbank = [ctx.enter_context(nc.psum_tensor(f"ring{i}", [D, 512], F32)) for i in range(RING)]
        pp = ctx.enter_context(nc.psum_tensor("pp", [D, 512], F32))

        cst = sb("cst", [D, CONST_W])
        wpm = sb("wpm", [D, MAIN, D])
        wpr = sb("wpr", [REST + 1, D])
        posn = sb("posn", [D, D])
        wq = sb("wq", [D, LAYERS, 3, D])
        w1s = sb("w1s", [D, LAYERS, FF])
        w2s = sb("w2s", [D, LAYERS, FF // D, D])
        vec = sb("vec", [D, LAYERS, NVEC])
        row = sb("row", [D, LAYERS, NROW, D])
        bq4 = sb("bq4", [D, LAYERS])
        bkm = sb("bkm", [D, LAYERS, 2])
        gw = sb("gw", [D, EXPERTS])
        ew1s = sb("ew1s", [D, EXPERTS, DFF])
        ew2s = sb("ew2s", [DFF, EXPERTS, D])
        ev = sb("ev", [D, 2, EXPERTS])
        pix = [sb(f"pix{i}", [D, MAIN, CHUNK]) for i in range(2)]
        pixr = [sb(f"pixr{i}", [REST + 1, CHUNK]) for i in range(2)]

        h0n = [both(f"h0n_{i}_", [D, SLOTN, D]) for i in range(2)]
        xT = both("xT", [D, WIDE])
        xn = both("xn", [D, SLOTN, D + 1])
        qT = both("qT", [D, TOK])
        qx = shared("qx", [D, IMG * (IMG * HEADS + HEADS)])
        kT = both("kT", [D, IMG, 2, SEQ])
        A8 = shared("A8", [D, TILES, SEQ])
        U8 = shared("U8", [D, TILES, SEQ])
        EX = shared("EX", [D, TILES, D + IMG])
        ecl = shared("ecl", [D, TILES])
        ET = shared("ET", [D, TILES, D])
        EcT = shared("EcT", [IMG, TILES, D])
        LC = both("LC", [D, SLOTN, IMG])
        Pc = shared("Pc", [IMG * HEADS, SEQ])
        Vc = shared("Vc", [IMG, 2, SEQ])
        Ec = shared("Ec", [IMG, D + 1])
        r1 = both("r1", [D, SLOTN, D])
        nn = both("nn", [D, SLOTN, D])
        zn = both("zn", [D, SLOTN, D])
        zT = both("zT", [D, WIDE])
        hT = both("hT", [D, FF // D, TOK])
        st = both("st", [D, SLOTN, 6])
        mv = both("mv", [D, SLOTN, 2])
        rs = both("rs", [D, SLOTN])
        sc = both("sc", [D, 16])
        XB = 3
        P = [sb(f"P{i}", [D, HEADS, SEQ]) for i in range(XB)]
        mx = [sb(f"mx{i}", [D, HEADS]) for i in range(XB)]
        sm = [sb(f"sm{i}", [D, HEADS]) for i in range(XB)]
        aff = sb("aff", [D, SLOTN, EXPERTS])
        mxg = sb("mxg", [D, SLOTN])
        smg = sb("smg", [D, SLOTN])
        affT = sb("affT", [D, SEQ])
        gv = sb("gv", [D, SLOTS])
        gi = sb("gi", [D, SLOTS], U32)
        gf = sb("gf", [D, SLOTS])
        OH = sb("OH", [D, SLOTS, D])
        OHc = sb("OHc", [D, SLOTS, IMG])
        OHT = sb("OHT", [D, SLOTS, D])
        OHcT = sb("OHcT", [IMG, SLOTS, D])
        big = sb("big", [D, SLOTS * D])

        def c_(name):
            at, n = CONST[name]
            return cst[:, at:at + n]

        ident = c_("ident")
        onehot = c_("onehot").rearrange("p (s i) -> p s i", s=SLOTN)

        HALF_E = EXPERTS // 2
        XIN = SLOTS * D
        flat = [hT[h][:].rearrange("p f t -> p (f t)") for h in range(HALVES)]
        xin = [f[:, 0:XIN].rearrange("p (e i s) -> p e i s", e=EXPERTS, i=IMG) for f in flat]
        hid = [f[:, XIN:2 * XIN].rearrange("p (e r) -> p e r", e=EXPERTS) for f in flat]
        Y = [f[:, 0:XIN].rearrange("p (s d) -> p s d", s=SLOTS) for f in flat]
        AX = big[:, 0:SLOTN * D].rearrange("p (s i e) -> p s i e", s=SLOTN, i=IMG)
        eo = big[:].rearrange("p (s c) -> p s c", s=SLOTS)
        eo4 = big[:].rearrange("p (s i e) -> p e i s", e=EXPERTS, i=IMG)

        out_h = out.rearrange("(u t a) k d -> u t a k d", t=TILES, a=2)

        w_in = signal("w_in", 16)
        pix_in = [signal(f"pix_in{i}", 64, 1) for i in range(2)]
        out_done = [signal(f"out_done{h}", 48, 1) for h in range(HALVES)]
        set_cls = signal("set_cls")
        set_dve = signal("set_dve")
        set_pool = signal("set_pool")
        filled = [signal(f"filled{b}") for b in range(RING)]
        drained = [signal(f"drained{b}") for b in range(RING)]
        patch_sum = signal("patch_sum", 1, PAIRS)
        patch_out = signal("patch_out", 1, PAIRS)
        qx_in = signal("qx_in")
        s_full = signal("s_full", TILES)
        s_row = signal("s_row", 2 * TILES)
        s_max = signal("s_max", TILES)
        s_sub = signal("s_sub", TILES, early=SBANKS)
        p_exp = signal("p_exp", TILES)
        p_sum = signal("p_sum", TILES)
        p_rec = signal("p_rec", TILES)
        p_mul = signal("p_mul", TILES)
        a_in = signal("a_in", TILES)
        u_in = signal("u_in", 3)
        e_in = signal("e_in")
        ec_in = signal("ec_in")
        cls_dve = signal("cls_dve", 9)
        cls_act = signal("cls_act")
        r_rec = signal("r_rec", 2)
        ln_st = signal("ln_st", 2, 1)
        ln_mv = signal("ln_mv", 2, 1)
        ln_ve = signal("ln_ve", 2, 1)
        ln_rs = signal("ln_rs", 2, 1)
        ln_in = signal("ln_in", 2, 1)
        y_mid = signal("y_mid", 2)
        y_in = signal("y_in", 2)
        z_mid = signal("z_mid")
        z_in = signal("z_in")
        r3_in = signal("r3_in")
        x_mid = signal("x_mid")
        x_in = signal("x_in")
        r0_in = signal("r0_in", 1, HALVES)
        moe_dve = signal("moe_dve", 12, HALVES)
        moe_act = signal("moe_act", 3, HALVES)

        st_order = {(it, n, h, l): i for i, (n, it, h, l) in enumerate(
            x for x in schedule("dve") if x[0] in ("init", "norm1", "norm1b", "out", "moe1"))}
        rs_order = {(it, n, h, l): i for i, (n, it, h, l) in enumerate(
            x for x in schedule("pool") if x[0] in ("init", "norm1", "norm1b", "out", "moe1"))}
        in_order = {(it, n, h, l): i for i, (n, it, h, l) in enumerate(
            x for x in schedule("dve") if x[0] in ("init", "norm2", "norm3", "moe2"))}

        def job(it, seg, h, l, name):
            b, n = PLACE[(it, seg, h, l, name)]
            return Job(ringbank[b], filled[b].sem, drained[b].sem, n, n - 1)

        def jobs(it, seg, h, l, *names):
            return [job(it, seg, h, l, name) for name in names]

        def unit(h, l):
            return l * HALVES + h

        def nat(j):
            return range(0, 2) if j == 0 else range(2, SLOTN)

        def cols(j):
            return slice(0, CHUNK) if j == 0 else slice(CHUNK, TOK)

        def width(j):
            return CHUNK if j == 0 else TOK - CHUNK

        N_W = 19
        block = ctx.enter_context(nc.Block())

        @block.sync
        def _(sp):
            for dst, src in ((wpr[:], wp_rest), (wpm[:], wp_main), (posn[0:PATCHES, :], pos[1:SEQ, :]),
                             (posn[PATCHES:D, :], pos[1:SEQ, :])):
                sp.dma_start(dst, src).then_inc(w_in.sem, 16)

            def load(m, i):
                sp.dma_start(pix[i][:], x_main[m]).then_inc(pix_in[i].sem, 16)
                sp.dma_start(pixr[i][0:REST, :], x_rest[m]).then_inc(pix_in[i].sem, 16)

            sp.wait_ge(set_pool.sem, 2)
            load(0, 0)
            load(1, 1)
            for dst, src in ((cst[:], const), (vec[:], lvec), (big[0:IMG, 0:D], cls0.broadcast_to([IMG, D])),
                             (big[0:IMG, D:2 * D], pos[0:1, :].broadcast_to([IMG, D])),
                             (big[:, 4 * D:8 * D].rearrange("p (l d) -> p l d", l=LAYERS),
                              rows[:, :, NROW].broadcast_to([D, LAYERS, D])),
                             (row[:], rows[:, :, 0:NROW].broadcast_to([D, LAYERS, NROW, D])),
                             (wq[:, :, 0, :], wqk[:, :, 0, :]), (wq[:, :, 1, :], wqk[:, :, 1, :]),
                             (wq[:, :, 2, :], wqk[:, :, 1, :]), (w1s[:], w1), (w2s[:], w2), (gw[:], gate), (ew1s[:], ew1),
                             (ew2s[:], ew2), (ev[:], evec)):
                sp.dma_start(dst, src).then_inc(w_in.sem, 16)

            def reload(it, c):
                sp.wait_ge(patch_sum.sem, patch_sum.at(it, 0, 2 * c - 2))
                load(it * 4 + c, c % 2)

            def iteration(it, more):
                if more:
                    for c in range(4):
                        reload(it + 1, c)
                for h in range(HALVES):
                    o = out_h[it * HALVES + h]
                    for R in jobs(it, "moe9", h, 0, "sum0", "sum1", "sum2", "sum3", "sumc"):
                        sp.wait_ge(R.drained, R.nth)
                    for a in range(2):
                        sp.dma_start(o[:, a, 1:SEQ, :].rearrange("t j d -> j t d"),
                                     nn[h][PATCHES * a:PATCHES * (a + 1), 0:TILES, :]).then_inc(out_done[h].sem, 16)
                    sp.dma_start(o[:, :, 0, :], nn[h][0:IMG, TILES, :]).then_inc(out_done[h].sem, 16)

            reload(0, 2)
            reload(0, 3)
            for it in range(ITERS):
                iteration(it, it + 1 < ITERS)
            for h in range(HALVES):
                sp.wait_ge(out_done[h].sem, out_done[h].at(ITERS - 1, 0))

        @block.gpsimd
        def _(pool):
            for i in range(2):
                pool.memset(pixr[i][:], 1.0).then_inc(set_pool.sem, 1)
            for z in (qx[0], EX[0], r1[0], r1[1], LC[0], LC[1]):
                pool.memset(z[:], 0.0).then_inc(set_pool.sem, 1)

            def rstd(it, key, h):
                u = rs_order[key]
                for j in range(2):
                    s = nat(j)
                    pool.wait_ge(ln_mv.sem, ln_mv.at(st_order[key], 0, j + 1))
                    r = rs[h][:, s[0]:s[-1] + 1]
                    pool.tensor_scalar(r, mv[h][:, s[0]:s[-1] + 1, 1], EPS, 1.0, ALU.add, ALU.mult
                                       ).then_inc(ln_ve.sem, 1)
                    pool.wait_ge(ln_ve.sem, ln_ve.at(u, 0, j + 1))
                    pool.tensor_tensor(r, r, c_("pow")[:, 0:len(s)], ALU.pow).then_inc(ln_rs.sem, 1)

            def row_(l, name):
                return row[:, l, ROW[name]:ROW[name] + 1, :].broadcast_to([D, SLOTN, D])

            def probabilities(it, n, t):
                g = (n * TILES + t) % XB
                pool.wait_ge(p_rec.sem, p_rec.at(it, n, t + 1))
                pool.tensor_tensor(P[g][:], P[g][:], sm[g][:].unsqueeze(2).broadcast_to([D, HEADS, SEQ]),
                                   ALU.mult).then_inc(p_mul.sem, 1)

            pool.wait_ge(w_in.sem, 16 * N_W)
            pool.wait_ge(set_pool.sem, 8)
            pool.wait_ge(set_dve.sem, 1)
            for seg, it, h, l in schedule("pool"):
                n = unit(h, l)
                if seg == "proj":
                    for R in jobs(it, seg, h, l, "q1"):
                        pool.wait_ge(R.drained, R.nth)
                    pool.tensor_tensor(qx[h][:].rearrange("p (i c) -> p i c", i=IMG)[:, :, 0:HEADS],
                                       qT[h][:, CHUNK * 2:TOK].unsqueeze(2).broadcast_to([D, IMG, HEADS]),
                                       c_("headmask").unsqueeze(1).broadcast_to([D, IMG, HEADS]),
                                       ALU.mult).then_inc(qx_in.sem, 1)
                elif seg[:4] == "soft":
                    t = int(seg[4])
                    if t > 0:
                        probabilities(it, n, t - 1)
                elif seg == "mix1":
                    probabilities(it, n, TILES - 1)
                elif seg in ("init", "norm1", "norm1b", "out", "moe1"):
                    rstd(it, (it, seg, h, l), h)
                elif seg == "ffn0":
                    pool.wait_ge(ln_in.sem, ln_in.at(in_order[(it, "norm2", h, l)], 0))
                    pool.tensor_tensor(nn[h][:], zn[h][:], row_(l, "g2"), ALU.mult).then_inc(z_mid.sem, 1)
                    pool.wait_ge(z_mid.sem, z_mid.at(it, n))
                    pool.tensor_tensor(nn[h][:], nn[h][:], row_(l, "bt2"), ALU.add).then_inc(z_in.sem, 1)
                elif seg == "norm3":
                    pool.wait_ge(ln_in.sem, ln_in.at(in_order[(it, seg, h, l)], 0))
                    pool.tensor_tensor(xn[h][:, :, 0:D], nn[h][:], row_(l, "g3"), ALU.mult).then_inc(x_mid.sem, 1)
                    pool.wait_ge(x_mid.sem, x_mid.at(it, n))
                    pool.tensor_tensor(xn[h][:, :, 0:D], xn[h][:, :, 0:D], row_(l, "bt3"), ALU.add
                                       ).then_inc(x_in.sem, 1)

        @block.scalar
        def _(act):
            def evacuate(it, seg, h, l, what, dst, bias=None, scale=1.0):
                J = job(it, seg, h, l, what)
                act.wait_ge(J.filled, J.nth)
                ps = J.bank
                src = ps[:, 0:dst.shape[-1]]
                if bias is None:
                    i = act.copy(dst, src)
                else:
                    i = act.activation(dst, src, ACT.Identity, bias=bias, scale=scale)
                i.then_inc(J.drained, 1)

            def v_(l, name):
                return vec[:, l, VEC[name]:VEC[name] + 1]

            act.wait_ge(w_in.sem, 16 * N_W)
            act.wait_ge(set_pool.sem, 8)
            act.wait_ge(set_dve.sem, 1)
            for seg, it, h, l in schedule("act"):
                n = unit(h, l)
                if seg == "init":
                    for j in range(2):
                        evacuate(it, seg, h, l, f"T{j}", xT[h][:, cols(j)])
                elif seg == "proj":
                    for j in range(2):
                        evacuate(it, seg, h, l, f"q{j}", qT[h][:, cols(j)], bq4[:, l:l + 1], 0.25)
                    for par, what in enumerate(("ke", "ko")):
                        b = bkm[:, l, par:par + 1]
                        for j in range(2):
                            J = job(it, seg, h, l, f"{what}{j}")
                            act.wait_ge(J.filled, J.nth)
                            ps = J.bank
                            i = act.activation(kT[h][:, 4 * j:4 * j + 4, par, 1:SEQ],
                                               ps[:, 0:CHUNK].rearrange("p (i k) -> p i k", i=4),
                                               ACT.Identity, bias=b)
                            if j == 1:
                                i = act.activation(kT[h][:, :, par, 0], ps[:, CHUNK:width(1)], ACT.Identity, bias=b)
                            i.then_inc(J.drained, 1)
                elif seg[:4] == "soft":
                    t = int(seg[4])
                    g = (n * TILES + t) % XB
                    act.wait_ge(s_sub.sem, s_sub.at(it, n, t + 1))
                    act.activation(P[g][:], P[g][:], ACT.Exp).then_inc(p_exp.sem, 1)
                elif seg == "cls1":
                    J = job(it, seg, h, l, "score")
                    act.wait_ge(J.filled, J.nth)
                    ps = J.bank
                    act.wait_ge(cls_dve.sem, cls_dve.at(it, n, 2))
                    act.activation(Pc[h][:], ps[0:IMG * HEADS, 0:SEQ], ACT.Exp, bias=sc[h][0:IMG * HEADS, 1:2],
                                   accum_out=sc[h][0:IMG * HEADS, 2:3]).then_inc(J.drained, 1)
                elif seg == "cls2":
                    act.wait_ge(cls_dve.sem, cls_dve.at(it, n, 6))
                    act.activation(Ec[h][:, 0:D].rearrange("p (a k) -> p a k", a=2),
                                   Vc[h][:, 0, 1:SEQ].unsqueeze(1).broadcast_to([IMG, 2, PATCHES]),
                                   ACT.Exp, scale=1.0 / HEADS)
                    act.activation(Ec[h][:, D:D + 1], Vc[h][:, 0, 0:1], ACT.Exp,
                                   scale=1.0 / HEADS).then_inc(cls_act.sem, 1)
                elif seg == "mix1":
                    act.wait_ge(u_in.sem, u_in.at(it, n))
                    for a in range(2):
                        p = slice(PATCHES * a, PATCHES * (a + 1))
                        act.activation(EX[h][p, :, PATCHES * a:PATCHES * (a + 1)], U8[h][p, :, 1:SEQ], ACT.Exp,
                                       scale=1.0 / HEADS)
                    act.activation(ecl[h][:], U8[h][:, :, 0], ACT.Exp, scale=1.0 / HEADS).then_inc(e_in.sem, 1)
                elif seg == "mix2":
                    J = job(it, seg, h, l, "turn")
                    act.wait_ge(J.filled, J.nth)
                    ps = J.bank
                    act.copy(ET[h][:], ps[:, :].rearrange("p (t q) -> p t q", t=TILES)
                             ).then_inc(J.drained, 1)
                    J = job(it, seg, h, l, "turnc")
                    act.wait_ge(J.filled, J.nth)
                    ps = J.bank
                    act.copy(EcT[h][:], ps[0:IMG, :].rearrange("p (t q) -> p t q", t=TILES)
                             ).then_inc(J.drained, 1)
                elif seg == "norm2":
                    for j in range(2):
                        evacuate(it, seg, h, l, f"T{j}", zT[h][:, cols(j)], v_(l, "bt2"), v_(l, "g2"))
                elif seg[:3] == "ffn":
                    j = int(seg[3])
                    for f in range(FF // D):
                        J = job(it, seg, h, l, f"h{f}")
                        act.wait_ge(J.filled, J.nth)
                        ps = J.bank
                        act.activation(hT[h][:, f, cols(j)], ps[:, 0:width(j)], ACT.Relu,
                                       bias=v_(l, f"b1_{f}")).then_inc(J.drained, 1)
                elif seg == "norm3" and l + 1 < LAYERS:
                    for j in range(2):
                        evacuate(it, seg, h, l, f"T{j}", xT[h][:, cols(j)], v_(l, "bt3"), v_(l, "g3"))
                elif seg == "moe2":
                    for j in range(2):
                        evacuate(it, seg, h, l, f"T{j}", zT[h][:, cols(j)])
                elif seg == "moe3":
                    for R in jobs(it, "moe2", h, l, "gate"):
                        act.wait_ge(R.drained, R.nth)
                    act.activation(aff[:], aff[:], ACT.Exp).then_inc(moe_act.sem, 1)
                    J = job(it, seg, h, l, "aff")
                    act.wait_ge(J.filled, J.nth)
                    ps = J.bank
                    act.copy(affT[:], ps[:, 0:SEQ]).then_inc(J.drained, 1)
                elif seg == "moe4":
                    for u in range(2):
                        evacuate(it, seg, h, l, f"oh{u}", OHT[:, 4 * u:4 * u + 4, :].rearrange("p s c -> p (s c)"))
                    for u in range(2):
                        J = job(it, seg, h, l, f"ohc{u}")
                        act.wait_ge(J.filled, J.nth)
                        ps = J.bank
                        act.copy(OHcT[:, 4 * u:4 * u + 4, :].rearrange("p s c -> p (s c)"), ps[0:IMG, :]
                                 ).then_inc(J.drained, 1)
                elif seg == "moe5":
                    for t in range(TILES):
                        J = job(it, seg, h, l, f"xin{t}")
                        act.wait_ge(J.filled, J.nth)
                        ps = J.bank
                        act.copy(xin[h][:, :, 2 * t:2 * t + 2, :],
                                 ps[:, 0:2 * D].rearrange("p (s a e) -> p e a s", s=SLOTS, a=2)
                                 ).then_inc(J.drained, 1)
                elif seg == "moe6":
                    for u in range(2):
                        for R in jobs(it, seg, h, l, f"up{u}"):
                            act.wait_ge(R.drained, R.nth)
                        v = hid[h][:, HALF_E * u:HALF_E * (u + 1), :]
                        act.activation(v, v, ACT.Gelu_apprx_tanh).then_inc(moe_act.sem, 1)
                elif seg == "moe8":
                    for u in range(2):
                        evacuate(it, seg, h, l, f"yT{u}", Y[h][:, 4 * u:4 * u + 4, :].rearrange("p s d -> p (s d)"))

        @block.vector
        def _(dve):
            dve.wait_ge(w_in.sem, 16 * N_W)
            for h in range(HALVES):
                for z in (xT, zT):
                    dve.memset(z[h][:, TOK:WIDE], 0.0)
                dve.memset(xn[h][:, :, D:D + 1], 1.0)
                for i in range(2):
                    dve.memset(h0n[i][h][:, TILES, :], 0.0).then_inc(set_cls.sem, 1)
            dve.wait_ge(set_cls.sem, 2 * HALVES)
            for h in range(HALVES):
                for i in range(2):
                    dve.tensor_tensor(h0n[i][h][0:IMG, TILES, :], big[0:IMG, 0:D], big[0:IMG, D:2 * D], ALU.mult
                                      ).then_inc(set_cls.sem, 1)
            dve.tensor_tensor(row[:, :, ROW["bt2"], :], row[:, :, ROW["bt2"], :],
                              big[:, 4 * D:8 * D].rearrange("p (l d) -> p l d", l=LAYERS), ALU.add)
            for par in range(2):
                w = wq[:, :, 1 + par, :].rearrange("p l (g a c) -> p l g a c", a=2, c=HD)
                for l in range(LAYERS):
                    dve.memset(w[:, l, :, 1 - par, :], 0.0)
                dve.tensor_scalar(bkm[:, :, par], vec[:, :, VEC["bk"]], c_("par")[:, par:par + 1], None, ALU.mult)
            dve.tensor_scalar(bq4[:], vec[:, :, VEC["bq"]], 0.25, None, ALU.mult).then_inc(set_dve.sem, 1)
            for i in range(SBANKS):
                dve.memset(sc[i][:], 0.0).then_inc(s_sub.sem, 1)

            def statistics(it, seg, h, l, source, ready):
                u = st_order[(it, seg, h, l)]
                for j in range(2):
                    ready(j)
                    for s in nat(j):
                        ins = dve.bn_stats(st[h][:, s, :], source[:, s, 0:D])
                    ins.then_inc(ln_st.sem, 1)
                for j in range(2):
                    dve.wait_ge(ln_st.sem, ln_st.at(u, 0, j + 1))
                    for s in nat(j):
                        ins = dve.bn_aggr(mv[h][:, s, :], st[h][:, s, :])
                    ins.then_inc(ln_mv.sem, 1)

            def normalise(it, seg, h, l, taken, source, dst):
                for j in range(2):
                    dve.wait_ge(ln_rs.sem, ln_rs.at(rs_order[(it, taken, h, l)], 0, j + 1))
                    for s in nat(j):
                        ins = dve.tensor_scalar(dst[:, s, 0:D], source[:, s, 0:D], mv[h][:, s, 0:1], rs[h][:, s:s + 1],
                                                ALU.subtract, ALU.mult)
                    ins.then_inc(ln_in.sem, 1)

            def row_(l, name):
                return row[:, l, ROW[name], :]

            def sums(it, n, t):
                g = (n * TILES + t) % XB
                dve.wait_ge(p_exp.sem, p_exp.at(it, n, t + 1))
                dve.tensor_reduce(sm[g][:], P[g][:], X, ALU.add).then_inc(p_sum.sem, 1)
                dve.wait_ge(p_sum.sem, p_sum.at(it, n, t + 1))
                dve.reciprocal(sm[g][:], sm[g][:]).then_inc(p_rec.sem, 1)

            def heads(it, n, h, t):
                g = (n * TILES + t) % XB
                dve.wait_ge(p_mul.sem, p_mul.at(it, n, t + 1))
                dve.tensor_reduce(A8[h][:, t, :], P[g][:].rearrange("p h k -> p k h"), X, ALU.add).then_inc(a_in.sem, 1)

            for seg, it, h, l in schedule("dve"):
                n = unit(h, l)
                C = IMG * HEADS
                if seg == PATCH[-1]:
                    dve.wait_ge(patch_sum.sem, patch_sum.at(it, h * TILES + l))
                    dve.tensor_tensor(h0n[it % 2][h][:, l, :], pp[:, 0:D], posn[:], ALU.mult
                                      ).then_inc(patch_out.sem, 1)
                elif seg == "init":
                    def ready(j):
                        dve.wait_ge(patch_out.sem, patch_out.at(it, (h + 1) * TILES - 1))
                        dve.wait_ge(set_cls.sem, 4 * HALVES)
                    statistics(it, seg, h, l, h0n[it % 2][h], ready)
                    normalise(it, seg, h, l, "init", h0n[it % 2][h], xn[h])
                elif seg[:4] == "soft":
                    t = int(seg[4])
                    T = n * TILES + t
                    g = T % XB
                    dve.wait_ge(s_full.sem, s_full.at(it, n, t + 1))
                    s4 = S[T % SBANKS][:, :, 0:4 * SEQ].rearrange("p b (h k) -> p b h k", h=4)
                    dve.tensor_reduce(mx[g][:].rearrange("p (b h) -> p b h", b=2), s4, X, ALU.max
                                      ).then_inc(s_max.sem, 1)
                    dve.wait_ge(s_max.sem, s_max.at(it, n, t + 1))
                    dve.tensor_tensor(P[g][:].rearrange("p (b h) k -> p b h k", b=2), s4,
                                      mx[g][:].rearrange("p (b h) -> p b h", b=2).unsqueeze(3)
                                      .broadcast_to([D, 2, 4, SEQ]), ALU.subtract).then_inc(s_sub.sem, 1)
                    if t >= 1:
                        sums(it, n, t - 1)
                    if t >= 2:
                        heads(it, n, h, t - 2)
                elif seg == "cls1":
                    J = job(it, seg, h, l, "score")
                    dve.wait_ge(J.filled, J.nth)
                    ps = J.bank
                    dve.tensor_reduce(sc[h][0:C, 0:1], ps[0:C, 0:SEQ], X, ALU.max).then_inc(cls_dve.sem, 1)
                    dve.wait_ge(cls_dve.sem, cls_dve.at(it, n, 1))
                    dve.tensor_scalar(sc[h][0:C, 1:2], sc[h][0:C, 0:1], -1.0, None, ALU.mult
                                      ).then_inc(cls_dve.sem, 1)
                elif seg == "cls2":
                    for R in jobs(it, "cls1", h, l, "score"):
                        dve.wait_ge(R.drained, R.nth)
                    dve.reciprocal(sc[h][0:C, 3:4], sc[h][0:C, 2:3]).then_inc(cls_dve.sem, 1)
                    dve.wait_ge(cls_dve.sem, cls_dve.at(it, n, 3))
                    dve.tensor_scalar(Pc[h][:], Pc[h][:], sc[h][0:C, 3:4], None, ALU.mult).then_inc(cls_dve.sem, 1)
                    J = job(it, seg, h, l, "heads")
                    dve.wait_ge(J.filled, J.nth)
                    ps = J.bank
                    dve.scalar_tensor_tensor(Vc[h][:, 0, :], ps[0:IMG, 0:SEQ], 0.0, c_("negc")[0:IMG, :],
                                             ALU.not_equal, ALU.mult).then_inc(cls_dve.sem, 1)
                    dve.tensor_tensor(Vc[h][:, 1, :], ps[0:IMG, 0:SEQ], c_("posc")[0:IMG, :], ALU.add
                                      ).then_inc(J.drained, 1)
                    dve.wait_ge(cls_dve.sem, cls_dve.at(it, n, 5))
                    for R in jobs(it, seg, h, l, "heads"):
                        dve.wait_ge(R.drained, R.nth)
                    dve.tensor_tensor(Vc[h][:, 0, :], Vc[h][:, 0, :], Vc[h][:, 1, :], ALU.add
                                      ).then_inc(cls_dve.sem, 1)
                elif seg == "cls3":
                    dve.wait_ge(cls_act.sem, cls_act.at(it, n))
                    dve.tensor_reduce(sc[h][0:IMG, 4:5], Ec[h][:, PATCHES:D + 1], X, ALU.add
                                      ).then_inc(cls_dve.sem, 1)
                    dve.wait_ge(cls_dve.sem, cls_dve.at(it, n, 7))
                    dve.reciprocal(sc[h][0:IMG, 5:6], sc[h][0:IMG, 4:5]).then_inc(cls_dve.sem, 1)
                    dve.tensor_scalar(LC[h][0:IMG, TILES, :], ident[0:IMG, 0:IMG], Ec[h][:, D:D + 1], None,
                                      ALU.mult).then_inc(cls_dve.sem, 1)
                    J = job(it, seg, h, l, "turn")
                    dve.wait_ge(J.filled, J.nth)
                    ps = J.bank
                    dve.tensor_tensor(LC[h][:, 0:TILES, :], onehot[:, 0:TILES, :],
                                      ps[:, 0:IMG].unsqueeze(1).broadcast_to([D, TILES, IMG]), ALU.mult
                                      ).then_inc(J.drained, 1)
                elif seg == "mix1":
                    sums(it, n, TILES - 1)
                    heads(it, n, h, TILES - 2)
                    heads(it, n, h, TILES - 1)
                    dve.wait_ge(a_in.sem, a_in.at(it, n))
                    dve.scalar_tensor_tensor(U8[h][:], A8[h][:], 0.0,
                                             c_("neg").unsqueeze(1).broadcast_to([D, TILES, SEQ]),
                                             ALU.not_equal, ALU.mult).then_inc(u_in.sem, 1)
                    dve.tensor_tensor(A8[h][:], A8[h][:], c_("pos8").unsqueeze(1).broadcast_to([D, TILES, SEQ]),
                                      ALU.add).then_inc(u_in.sem, 1)
                    dve.wait_ge(u_in.sem, u_in.at(it, n, 2))
                    dve.tensor_tensor(U8[h][:], U8[h][:], A8[h][:], ALU.add).then_inc(u_in.sem, 1)
                    dve.wait_ge(e_in.sem, e_in.at(it, n))
                    dve.tensor_tensor(EX[h][:, :, D:D + IMG], onehot[:, 0:TILES, :],
                                      ecl[h][:].unsqueeze(2).broadcast_to([D, TILES, IMG]), ALU.mult
                                      ).then_inc(ec_in.sem, 1)
                elif seg == "mix3":
                    for j in range(2):
                        J = job(it, seg, h, l, f"mix{j}")
                        dve.wait_ge(J.filled, J.nth)
                        ps = J.bank
                        v = ps[:, 0:2 * (D + 1)].rearrange("p (t d) -> p t d", t=2)
                        dve.reciprocal(sc[h][:, 8 + 2 * j:10 + 2 * j], v[:, :, D]).then_inc(r_rec.sem, 1)
                        dve.wait_ge(r_rec.sem, r_rec.at(it, n, j + 1))
                        for i in range(2):
                            t = 2 * j + i
                            ins = dve.scalar_tensor_tensor(r1[h][:, t, :], v[:, i, 0:D], sc[h][:, 8 + t:9 + t],
                                                           xn[h][:, t, 0:D], ALU.mult, ALU.add)
                        ins.then_inc(J.drained, 1)
                    J = job(it, seg, h, l, "mixc")
                    dve.wait_ge(J.filled, J.nth)
                    ps = J.bank
                    dve.wait_ge(cls_dve.sem, cls_dve.at(it, n, 8))
                    dve.scalar_tensor_tensor(r1[h][0:IMG, TILES, :], ps[0:IMG, 0:D], sc[h][0:IMG, 5:6],
                                             xn[h][0:IMG, TILES, 0:D], ALU.mult, ALU.add
                                             ).then_inc(J.drained, 1)
                elif seg == "norm1":
                    def ready(j):
                        for R in jobs(it, "mix3", h, l, *((f"mix{j}",) if j == 0 else ("mix1", "mixc"))):
                            dve.wait_ge(R.drained, R.nth)
                    statistics(it, seg, h, l, r1[h], ready)
                elif seg == "norm1b":
                    if l == 0 and it > 0:
                        dve.wait_ge(out_done[h].sem, out_done[h].at(it, 0, 0))
                    for j in range(2):
                        dve.wait_ge(ln_mv.sem, ln_mv.at(st_order[(it, "norm1", h, l)], 0, j + 1))
                        for s in nat(j):
                            ins = dve.scalar_tensor_tensor(nn[h][:, s, :], r1[h][:, s, :], mv[h][:, s, 0:1],
                                                           row_(l, "g1"), ALU.subtract, ALU.mult)
                        ins.then_inc(y_mid.sem, 1)
                    for j in range(2):
                        dve.wait_ge(ln_rs.sem, ln_rs.at(rs_order[(it, "norm1", h, l)], 0, j + 1))
                        dve.wait_ge(y_mid.sem, y_mid.at(it, n, j + 1))
                        for s in nat(j):
                            ins = dve.scalar_tensor_tensor(nn[h][:, s, :], nn[h][:, s, :], rs[h][:, s:s + 1],
                                                           row_(l, "bt1"), ALU.mult, ALU.add)
                        ins.then_inc(y_in.sem, 1)

                    def ready(j):
                        dve.wait_ge(y_in.sem, y_in.at(it, n, j + 1))
                    statistics(it, seg, h, l, nn[h], ready)
                elif seg == "norm2":
                    normalise(it, seg, h, l, "norm1b", nn[h], zn[h])
                elif seg == "out":
                    dve.wait_ge(z_in.sem, z_in.at(it, n))
                    for j in range(2):
                        J = job(it, seg, h, l, f"out{j}")
                        dve.wait_ge(J.filled, J.nth)
                        ps = J.bank
                        if j == 1:
                            dve.tensor_tensor(r1[h][0:IMG, TILES, :], ps[0:IMG, 2 * D:3 * D],
                                              nn[h][0:IMG, TILES, :], ALU.add).then_inc(r3_in.sem, 1)
                        dve.tensor_tensor(r1[h][:, 2 * j:2 * j + 2, :],
                                          ps[:, 0:2 * D].rearrange("p (t d) -> p t d", t=2),
                                          nn[h][:, 2 * j:2 * j + 2, :], ALU.add).then_inc(J.drained, 1)

                    def ready(j):
                        for R in jobs(it, "out", h, l, f"out{j}"):
                            dve.wait_ge(R.drained, R.nth)
                        if j == 1:
                            dve.wait_ge(r3_in.sem, r3_in.at(it, n))
                    statistics(it, seg, h, l, r1[h], ready)
                elif seg == "norm3":
                    normalise(it, seg, h, l, "out", r1[h], nn[h])
                elif seg == "moe1":
                    dve.wait_ge(x_in.sem, x_in.at(it, unit(h, LAYERS - 1)))
                    dve.tensor_tensor(r1[h][:], h0n[it % 2][h][:], xn[h][:, :, 0:D], ALU.add).then_inc(r0_in.sem, 1)

                    def ready(j):
                        dve.wait_ge(r0_in.sem, r0_in.at(it, h))
                    statistics(it, seg, h, l, r1[h], ready)
                elif seg == "moe2":
                    normalise(it, seg, h, l, "moe1", r1[h], nn[h])
                    J = job(it, seg, h, l, "gate")
                    dve.wait_ge(J.filled, J.nth)
                    ps = J.bank
                    g3 = ps[:, 0:SLOTN * EXPERTS].rearrange("p (s e) -> p s e", e=EXPERTS)
                    dve.tensor_reduce(mxg[:], g3, X, ALU.max).then_inc(moe_dve.sem, 1)
                    dve.wait_ge(moe_dve.sem, moe_dve.at(it, h, 1))
                    dve.tensor_tensor(aff[:], g3, mxg[:].unsqueeze(2).broadcast_to([D, SLOTN, EXPERTS]),
                                      ALU.subtract).then_inc(J.drained, 1)
                elif seg == "moe3":
                    dve.wait_ge(moe_act.sem, moe_act.at(it, h, 1))
                    dve.tensor_reduce(smg[:], aff[:], X, ALU.add).then_inc(moe_dve.sem, 1)
                    dve.wait_ge(moe_dve.sem, moe_dve.at(it, h, 2))
                    dve.reciprocal(smg[:], smg[:]).then_inc(moe_dve.sem, 1)
                    dve.wait_ge(moe_dve.sem, moe_dve.at(it, h, 3))
                    dve.tensor_tensor(aff[:], aff[:], smg[:].unsqueeze(2).broadcast_to([D, SLOTN, EXPERTS]),
                                      ALU.mult).then_inc(moe_dve.sem, 1)
                    dve.wait_ge(moe_dve.sem, moe_dve.at(it, h, 4))
                    dve.tensor_tensor(AX, aff[:].unsqueeze(2).broadcast_to([D, SLOTN, IMG, EXPERTS]),
                                      onehot.unsqueeze(3).broadcast_to([D, SLOTN, IMG, EXPERTS]), ALU.mult
                                      ).then_inc(moe_dve.sem, 1)
                elif seg == "moe4":
                    for R in jobs(it, "moe3", h, l, "aff"):
                        dve.wait_ge(R.drained, R.nth)
                    dve.max(gv[:], affT[:]).then_inc(moe_dve.sem, 1)
                    dve.wait_ge(moe_dve.sem, moe_dve.at(it, h, 6))
                    dve.max_index(gi[:], gv[:], affT[:]).then_inc(moe_dve.sem, 1)
                    dve.wait_ge(moe_dve.sem, moe_dve.at(it, h, 7))
                    dve.tensor_copy(gf[:], gi[:]).then_inc(moe_dve.sem, 1)
                    dve.wait_ge(moe_dve.sem, moe_dve.at(it, h, 8))
                    dve.tensor_tensor(OHc[:], gf[:].unsqueeze(2).broadcast_to([D, SLOTS, IMG]),
                                      c_("targetc").unsqueeze(1).broadcast_to([D, SLOTS, IMG]), ALU.is_equal
                                      ).then_inc(moe_dve.sem, 1)
                    dve.tensor_tensor(OH[:], gf[:].unsqueeze(2).broadcast_to([D, SLOTS, D]),
                                      c_("target").unsqueeze(1).broadcast_to([D, SLOTS, D]), ALU.is_equal
                                      ).then_inc(moe_dve.sem, 1)
                elif seg == "moe5":
                    J = job(it, "moe4", h, l, "ohc1")
                    dve.wait_ge(J.filled, J.nth)
                    dve.tensor_tensor(OH[:], OH[:], gv[:].unsqueeze(2).broadcast_to([D, SLOTS, D]), ALU.mult
                                      ).then_inc(moe_dve.sem, 1)
                    dve.tensor_tensor(OHc[:], OHc[:], gv[:].unsqueeze(2).broadcast_to([D, SLOTS, IMG]),
                                      ALU.mult).then_inc(moe_dve.sem, 1)
                elif seg in ("moe6", "moe7"):
                    hid4 = hid[h].rearrange("p e (i s) -> p e i s", i=IMG)
                    name, dst, k = ("up", hid4, 0) if seg == "moe6" else ("down", eo4, 1)
                    for u in range(2):
                        e = slice(HALF_E * u, HALF_E * (u + 1))
                        J = job(it, seg, h, l, f"{name}{u}")
                        dve.wait_ge(J.filled, J.nth)
                        ps = J.bank
                        dve.tensor_tensor(dst[:, e, :, :], ps[:, :].rearrange("p (e i s) -> p e i s", i=IMG, s=SLOTS),
                                          ev[:, k, e].unsqueeze(2).unsqueeze(3).broadcast_to([D, HALF_E, IMG, SLOTS]),
                                          ALU.add).then_inc(J.drained, 1)
                elif seg == "moe9":
                    for t in range(TILES):
                        J = job(it, seg, h, l, f"sum{t}")
                        dve.wait_ge(J.filled, J.nth)
                        ps = J.bank
                        dve.tensor_tensor(nn[h][:, t, :], ps[:, 0:D], r1[h][:, t, :], ALU.add
                                          ).then_inc(J.drained, 1)
                    J = job(it, seg, h, l, "sumc")
                    dve.wait_ge(J.filled, J.nth)
                    ps = J.bank
                    dve.tensor_tensor(nn[h][0:IMG, TILES, :], ps[0:IMG, 0:D], r1[h][0:IMG, TILES, :], ALU.add
                                      ).then_inc(J.drained, 1)

        @block.tensor
        def _(pe):
            mm = pe.matmul

            def patch(it, h, t, part):
                c, half = 2 * h + t // 2, t % 2
                i = c % 2
                if part == 0:
                    pe.wait_ge(pix_in[i].sem, pix_in[i].at(it, 0, 32 * (c // 2 + 1)))
                    if it + h + t > 0:
                        pe.wait_ge(patch_out.sem, patch_out.at(it, h * TILES + t - 1))
                tokens = slice(D * half, D * (half + 1))
                for k in range(PIECE * part, min(PIECE * (part + 1), BLOCKS)):
                    if k < MAIN:
                        mm(pp[:, 0:D], pix[i][:, k, tokens], wpm[:, k, :], start=(k == 0), stop=False)
                    else:
                        mm(pp[:, 0:D], pixr[i][:, tokens], wpr[:], start=False, stop=True).then_inc(patch_sum.sem, 1)

            def to_T(it, seg, h, l, src):
                for j in range(2):
                    pe.wait_ge(ln_in.sem, ln_in.at(in_order[(it, seg, h, l)], 0, j + 1))
                    J = job(it, seg, h, l, f"T{j}")
                    pe.wait_ge(J.drained, J.before)
                    ps = J.bank
                    for i, s in enumerate(nat(j)):
                        if s < TILES:
                            ins = pe.transpose(ps[:, D * i:D * (i + 1)], src[:, s, 0:D], ident)
                        else:
                            ins = pe.transpose(ps[:, D * i:D * i + IMG], src[0:IMG, s, 0:D], ident[0:IMG, 0:IMG])
                    ins.then_inc(J.filled, 1)

            pe.wait_ge(w_in.sem, 16 * N_W)
            pe.wait_ge(set_pool.sem, 8)
            pe.wait_ge(set_dve.sem, 1)
            for seg, it, h, l in schedule("pe"):
                n = unit(h, l)
                if seg[:5] == "patch":
                    patch(it, h, l, int(seg[5:]))
                elif seg == "init":
                    to_T(it, seg, h, l, xn[h])
                elif seg == "proj":
                    for k, what in enumerate(("q", "ke", "ko")):
                        for j in range(2):
                            if k == 0:
                                for R in jobs(it, *(("init", h, 0) if l == 0 else ("norm3", h, l - 1)), f"T{j}"):
                                    pe.wait_ge(R.drained, R.nth)
                            J = job(it, seg, h, l, f"{what}{j}")
                            pe.wait_ge(J.drained, J.before)
                            ps = J.bank
                            mm(ps[:, 0:width(j)], wq[:, l, k, :], xT[h][:, cols(j)], start=True, stop=True
                               ).then_inc(J.filled, 1)
                elif seg[:4] == "soft":
                    t = int(seg[4])
                    T = n * TILES + t
                    if t == 0:
                        for R in jobs(it, "proj", h, l, "q0", "q1", "ke0", "ke1", "ko0", "ko1"):
                            pe.wait_ge(R.drained, R.nth)
                    pe.wait_ge(s_sub.sem, s_sub.at(it, n, t - 1))
                    for k, g in enumerate((0, 2, 1, 3)):
                        f = slice(32 * g, 32 * g + 32)
                        if k >= 2:
                            pe.wait_ge(s_row.sem, s_row.at(it, n, 2 * t + k - 1))
                        for a in range(2):
                            i = 2 * t + a
                            ins = mm(S[T % SBANKS][PATCHES * a:PATCHES * (a + 1), g // 2,
                                                   2 * SEQ * (g % 2):2 * SEQ * (g % 2 + 1)],
                                     qT[h][f, PATCHES * i:PATCHES * (i + 1)],
                                     kT[h][f, i, :, :].rearrange("p a k -> p (a k)"), start=True, stop=True)
                        if k < 2:
                            ins.then_inc(s_row.sem, 1)
                    ins.then_inc(s_full.sem, 1)
                elif seg == "cls1":
                    pe.wait_ge(qx_in.sem, qx_in.at(it, n))
                    J = job(it, seg, h, l, "score")
                    pe.wait_ge(J.drained, J.before)
                    ps = J.bank
                    C = IMG * HEADS
                    for i in range(IMG):
                        for par in range(2):
                            ins = mm(ps[0:C, 0:SEQ], qx[h][:, C * i:C * (i + 1)], kT[h][:, i, par, :],
                                     start=(i == 0 and par == 0), stop=(i == IMG - 1 and par == 1))
                    ins.then_inc(J.filled, 1)
                elif seg == "cls2":
                    pe.wait_ge(cls_dve.sem, cls_dve.at(it, n, 4))
                    J = job(it, seg, h, l, "heads")
                    pe.wait_ge(J.drained, J.before)
                    ps = J.bank
                    mm(ps[0:IMG, 0:SEQ], c_("hsum")[0:C, :], Pc[h][:], start=True, stop=True
                       ).then_inc(J.filled, 1)
                elif seg == "cls3":
                    pe.wait_ge(cls_act.sem, cls_act.at(it, n))
                    J = job(it, seg, h, l, "turn")
                    pe.wait_ge(J.drained, J.before)
                    ps = J.bank
                    pe.transpose(ps[:, 0:IMG], Ec[h][:, 0:D], ident[0:IMG, 0:IMG]
                                 ).then_inc(J.filled, 1)
                elif seg == "mix2":
                    pe.wait_ge(ec_in.sem, ec_in.at(it, n))
                    J = job(it, seg, h, l, "turn")
                    pe.wait_ge(J.drained, J.before)
                    ps = J.bank
                    for t in range(TILES):
                        ins = pe.transpose(ps[:, D * t:D * (t + 1)], EX[h][:, t, 0:D], ident)
                    ins.then_inc(J.filled, 1)
                    J = job(it, seg, h, l, "turnc")
                    pe.wait_ge(J.drained, J.before)
                    ps = J.bank
                    for t in range(TILES):
                        ins = pe.transpose(ps[0:IMG, D * t:D * (t + 1)], EX[h][:, t, D:D + IMG], ident)
                    ins.then_inc(J.filled, 1)
                elif seg == "mix3":
                    for R in jobs(it, "mix2", h, l, "turn", "turnc"):
                        pe.wait_ge(R.drained, R.nth)
                    if l > 0:
                        pe.wait_ge(x_in.sem, x_in.at(it, n - HALVES))
                    for j in range(2):
                        J = job(it, seg, h, l, f"mix{j}")
                        pe.wait_ge(J.drained, J.before)
                        ps = J.bank
                        for i in range(2):
                            t = 2 * j + i
                            o = ps[:, (D + 1) * i:(D + 1) * (i + 1)]
                            mm(o, ET[h][:, t, :], xn[h][:, t, :], start=True, stop=False)
                            ins = mm(o, EcT[h][:, t, :], xn[h][0:IMG, TILES, :], start=False, stop=True)
                        ins.then_inc(J.filled, 1)
                    J = job(it, seg, h, l, "mixc")
                    pe.wait_ge(J.drained, J.before)
                    ps = J.bank
                    pe.wait_ge(cls_dve.sem, cls_dve.at(it, n, 9))
                    for R in jobs(it, "cls3", h, l, "turn"):
                        pe.wait_ge(R.drained, R.nth)
                    for t in range(TILES):
                        mm(ps[0:IMG, 0:D], LC[h][:, t, :], xn[h][:, t, 0:D], start=(t == 0), stop=False)
                    mm(ps[0:IMG, 0:D], LC[h][0:IMG, TILES, :], xn[h][0:IMG, TILES, 0:D], start=False, stop=True
                       ).then_inc(J.filled, 1)
                elif seg == "norm2":
                    to_T(it, seg, h, l, zn[h])
                elif seg[:3] == "ffn":
                    j = int(seg[3])
                    for R in jobs(it, "norm2", h, l, f"T{j}"):
                        pe.wait_ge(R.drained, R.nth)
                    for f in range(FF // D):
                        J = job(it, seg, h, l, f"h{f}")
                        pe.wait_ge(J.drained, J.before)
                        ps = J.bank
                        mm(ps[:, 0:width(j)], w1s[:, l, D * f:D * (f + 1)], zT[h][:, cols(j)], start=True,
                           stop=True).then_inc(J.filled, 1)
                elif seg == "out":
                    for j in range(2):
                        for R in jobs(it, f"ffn{j}", h, l, "h0", "h1", "h2", "h3"):
                            pe.wait_ge(R.drained, R.nth)
                        J = job(it, seg, h, l, f"out{j}")
                        pe.wait_ge(J.drained, J.before)
                        ps = J.bank
                        for i, s in enumerate(nat(j)):
                            rows_ = D if s < TILES else IMG
                            for f in range(FF // D):
                                ins = mm(ps[0:rows_, D * i:D * (i + 1)], hT[h][:, f, D * s:D * s + rows_],
                                         w2s[:, l, f, :], start=(f == 0), stop=(f == FF // D - 1))
                        ins.then_inc(J.filled, 1)
                elif seg == "norm3" and l + 1 < LAYERS:
                    to_T(it, seg, h, l, nn[h])
                elif seg == "moe2":
                    to_T(it, seg, h, l, nn[h])
                    for R in jobs(it, seg, h, l, "T0", "T1"):
                        pe.wait_ge(R.drained, R.nth)
                    J = job(it, seg, h, l, "gate")
                    pe.wait_ge(J.drained, J.before)
                    ps = J.bank
                    for s in range(SLOTN):
                        ins = mm(ps[:, EXPERTS * s:EXPERTS * (s + 1)], zT[h][:, D * s:D * (s + 1)], gw[:],
                                 start=True, stop=True)
                    ins.then_inc(J.filled, 1)
                elif seg == "moe3":
                    pe.wait_ge(moe_dve.sem, moe_dve.at(it, h, 5))
                    J = job(it, seg, h, l, "aff")
                    pe.wait_ge(J.drained, J.before)
                    ps = J.bank
                    mm(ps[:, 0:1], AX[:, TILES].rearrange("p i e -> p (i e)"), xn[h][:, 0, D:D + 1], start=True,
                       stop=True)
                    for t in range(TILES):
                        ins = mm(ps[:, 1:SEQ], AX[:, t].rearrange("p i e -> p (i e)"), c_("stackI"), start=(t == 0),
                                 stop=(t == TILES - 1))
                    ins.then_inc(J.filled, 1)
                elif seg == "moe4":
                    pe.wait_ge(moe_dve.sem, moe_dve.at(it, h, 10))
                    for u in range(2):
                        J = job(it, seg, h, l, f"oh{u}")
                        pe.wait_ge(J.drained, J.before)
                        ps = J.bank
                        for k in range(4):
                            ins = pe.transpose(ps[:, D * k:D * (k + 1)], OH[:, 4 * u + k, :], ident)
                        ins.then_inc(J.filled, 1)
                    for u in range(2):
                        J = job(it, seg, h, l, f"ohc{u}")
                        pe.wait_ge(J.drained, J.before)
                        ps = J.bank
                        for k in range(4):
                            ins = pe.transpose(ps[0:IMG, D * k:D * (k + 1)], OHc[:, 4 * u + k, :], ident)
                        ins.then_inc(J.filled, 1)
                elif seg == "moe5":
                    for R in jobs(it, "moe4", h, l, "oh0", "oh1", "ohc0", "ohc1"):
                        pe.wait_ge(R.drained, R.nth)
                    for t in range(TILES):
                        J = job(it, seg, h, l, f"xin{t}")
                        pe.wait_ge(J.drained, J.before)
                        ps = J.bank
                        pair = slice(32 * t, 32 * t + 32)
                        mm(ps[:, 0:2 * D], nn[h][:, t, :], OHT[:, :, pair], start=True, stop=False)
                        mm(ps[:, 0:2 * D], nn[h][0:IMG, TILES, :], OHcT[:, :, pair], start=False, stop=True
                           ).then_inc(J.filled, 1)
                elif seg == "moe6":
                    for R in jobs(it, "moe5", h, l, "xin0", "xin1", "xin2", "xin3"):
                        pe.wait_ge(R.drained, R.nth)
                    for u in range(2):
                        J = job(it, seg, h, l, f"up{u}")
                        pe.wait_ge(J.drained, J.before)
                        ps = J.bank
                        for k in range(HALF_E):
                            e = HALF_E * u + k
                            ins = mm(ps[:, PATCHES * k:PATCHES * (k + 1)], ew1s[:, e, :],
                                     xin[h][:, e].rearrange("p i s -> p (i s)"), start=True, stop=True)
                        ins.then_inc(J.filled, 1)
                elif seg == "moe7":
                    for u in range(2):
                        pe.wait_ge(moe_act.sem, moe_act.at(it, h, 2 + u))
                        J = job(it, seg, h, l, f"down{u}")
                        pe.wait_ge(J.drained, J.before)
                        ps = J.bank
                        for k in range(HALF_E):
                            e = HALF_E * u + k
                            ins = mm(ps[:, PATCHES * k:PATCHES * (k + 1)], ew2s[:, e, :], hid[h][:, e, :],
                                     start=True, stop=True)
                        ins.then_inc(J.filled, 1)
                elif seg == "moe8":
                    for R in jobs(it, "moe7", h, l, "down0", "down1"):
                        pe.wait_ge(R.drained, R.nth)
                    for u in range(2):
                        J = job(it, seg, h, l, f"yT{u}")
                        pe.wait_ge(J.drained, J.before)
                        ps = J.bank
                        for k in range(4):
                            ins = pe.transpose(ps[:, D * k:D * (k + 1)], eo[:, 4 * u + k, :], ident)
                        ins.then_inc(J.filled, 1)
                elif seg == "moe9":
                    for R in jobs(it, "moe8", h, l, "yT0", "yT1"):
                        pe.wait_ge(R.drained, R.nth)
                    pe.wait_ge(moe_dve.sem, moe_dve.at(it, h, 12))
                    for t in range(TILES):
                        J = job(it, seg, h, l, f"sum{t}")
                        pe.wait_ge(J.drained, J.before)
                        ps = J.bank
                        pair = slice(32 * t, 32 * t + 32)
                        for s in range(SLOTS):
                            ins = mm(ps[:, 0:D], OH[pair, s, :], Y[h][pair, s, :], start=(s == 0),
                                     stop=(s == SLOTS - 1))
                        ins.then_inc(J.filled, 1)
                    J = job(it, seg, h, l, "sumc")
                    pe.wait_ge(J.drained, J.before)
                    ps = J.bank
                    for s in range(SLOTS):
                        ins = mm(ps[0:IMG, 0:D], OHc[:, s, :], Y[h][:, s, :], start=(s == 0),
                                 stop=(s == SLOTS - 1))
                    ins.then_inc(J.filled, 1)



def kernel(**inputs):
    import concourse.bacc as _bacc
    from concourse.bass_utils import run_bass_kernel_spmd as _run

    a = {k: np.asarray(v) for k, v in inputs.items()}
    chunks = B // 4
    x = a["x"].reshape(chunks, 4, 3, 8, 28, 8, 28).transpose(0, 2, 4, 6, 1, 3, 5).reshape(chunks, IN_D, CHUNK)
    w = a["L0_tok_W"].T
    L = "L0_attn_"
    vecs = [a[L + "bqkv"][:, 0:D], a[L + "bqkv"][:, D:2 * D], a[L + "g1"], a[L + "bt1"], a[L + "g2"], a[L + "bt2"],
            a[L + "g3"], a[L + "bt3"]] + [a[L + "b1"][:, D * f:D * (f + 1)] for f in range(FF // D)]
    arrays = {
        "x_main": x[:, :MAIN * D].reshape(chunks, D, MAIN, CHUNK),
        "x_rest": x[:, MAIN * D:],
        "wp_main": w[:MAIN * D].reshape(D, MAIN, D),
        "wp_rest": np.concatenate([w[MAIN * D:], a["L0_tok_b"][None]], 0),
        "cls0": a["L0_tok_class_token"],
        "pos": a["L0_tok_pos_embed"],
        "const": shape_constants(),
        "wqk": a[L + "Wqkv"][:, 0:2 * D].reshape(LAYERS, 2, D, D).transpose(3, 0, 1, 2),
        "w1": a[L + "W1"].transpose(2, 0, 1),
        "w2": a[L + "W2"].reshape(LAYERS, D, FF // D, D).transpose(3, 0, 2, 1),
        "lvec": np.stack(vecs, 2).transpose(1, 0, 2),
        "rows": np.stack([a[L + n] for n in ("g1", "bt1", "g2", "bt2", "g3", "bt3", "b2")], 1)[None],
        "gate": a["L0_ffn_gate_weight"],
        "ew1": a["L0_ffn_w1"].transpose(1, 0, 2),
        "ew2": a["L0_ffn_w2"].transpose(1, 0, 2),
        "evec": np.stack([a["L0_ffn_b1"], a["L0_ffn_b2"]]).transpose(2, 0, 1),
    }
    arrays = {k: np.ascontiguousarray(v) for k, v in arrays.items()}
    nc = _bacc.Bacc("TRN2", target_bir_lowering=False, num_devices=1)
    args = [nc.dram_tensor(k, v.shape, mybir.dt.from_np(v.dtype), kind="ExternalInput").ap() for k, v in arrays.items()]
    args.append(nc.dram_tensor("out", (B, SEQ, D), F32, kind="ExternalOutput").ap())
    vit_kernel(nc, *args)
    r = _run(nc, [arrays], core_ids=[0])
    return r.results[0]["out"]
```

```python
from contextlib import ExitStack
from typing import NamedTuple

import numpy as np

import concourse.bass as bass
from concourse import mybir

F32 = mybir.dt.float32
U32 = mybir.dt.uint32
ALU = mybir.AluOpType
ACT = mybir.ActivationFunctionType
X = mybir.AxisListType.X

B = 64
PATCHES = 64
SEQ = PATCHES + 1
D = 128
IN_D = 2352
MAIN = IN_D // D
REST = IN_D - MAIN * D
LAYERS, HEADS, HD, FF = 4, 8, 16, 512
EXPERTS, SLOTS, DFF = 16, 8, 128
EPS = 1e-5

HALVES = 2
IMG = 8
ITERS = B // (HALVES * IMG)
TILES = 4
SLOTN = TILES + 1
TOK = IMG * SEQ
WIDE = SLOTN * D
CHUNK = 256
UNITS = LAYERS * HALVES
PAIRS = TILES * HALVES
BLOCKS = MAIN + 1
XB = 3
SBANKS = 2
ACT_HEADS = 5

CONST = {}
for _name, _n in (("ident", D), ("stackI", PATCHES), ("pos8", SEQ), ("neg", SEQ), ("posc", SEQ), ("negc", SEQ),
                  ("onehot", SLOTN * IMG), ("headmask", HEADS), ("hsum", IMG), ("target", D), ("targetc", IMG),
                  ("pow", 16), ("imgsel", IMG), ("expsel", EXPERTS)):
    _at = sum(w for _, w in CONST.values())
    CONST[_name] = (_at, _n)
CONST_W = sum(w for _, w in CONST.values())
VEC = {n: i for i, n in enumerate(("bq", "bk", "g1", "bt1", "g2", "bt2", "g3", "bt3", "b1_0", "b1_1", "b1_2", "b1_3"))}
NVEC = len(VEC)
ROW = {n: i for i, n in enumerate(("g1", "bt1", "g2", "bt2", "g3", "bt3"))}
NROW = len(ROW)


def shape_constants():
    c = np.zeros((D, CONST_W), np.float32)

    def put(name, a):
        at, n = CONST[name]
        a = np.asarray(a, np.float32)
        c[:a.shape[0], at:at + n] = a.reshape(a.shape[0], n)

    p = np.arange(D)
    q = 1 + p % PATCHES
    k = np.arange(SEQ)
    far = -1e5
    put("ident", np.eye(D))
    put("stackI", p[:, None] % PATCHES == np.arange(PATCHES)[None, :])
    put("pos8", HEADS * np.exp(-np.abs(q[:, None] - k[None, :]).astype(np.float32) * np.float32(0.1)))
    put("neg", far * (k[None, :] > q[:, None]))
    put("posc", np.broadcast_to(HEADS * np.exp(-k.astype(np.float32) * np.float32(0.1)), (D, SEQ)))
    put("negc", np.broadcast_to(far * (k > 0), (D, SEQ)))
    one = np.zeros((D, SLOTN, IMG))
    for t in range(TILES):
        one[p, t, 2 * t + p // PATCHES] = 1
    one[np.arange(IMG), TILES, np.arange(IMG)] = 1
    put("onehot", one)
    put("headmask", p[:, None] // HD == np.arange(HEADS)[None, :])
    put("hsum", p[:, None] // HEADS == np.arange(IMG)[None, :])
    img = p // EXPERTS
    put("target", np.where(img[:, None] % 2 == p[None, :] // PATCHES, 1 + p[None, :] % PATCHES, -1))
    put("targetc", np.where(img[:, None] == np.arange(IMG)[None, :], 0, -1))
    put("pow", np.full((D, 16), -0.5))
    put("imgsel", img[:, None] == np.arange(IMG)[None, :])
    put("expsel", p[:, None] % EXPERTS == np.arange(EXPERTS)[None, :])
    return c


DVE_SLOTS = 3
PIX = 3
PIECE = 5
PIECES = -(-BLOCKS // PIECE)
ATTN = ("proj", "keys", "soft0", "cls1", "soft1", "sum0", "cls2", "soft2", "sum1", "head0", "cls3", "soft3", "sum2",
        "head1", "sum3", "head2", "head3", "mix1", "spread", "mix2", "mix3")
FFN = ("norm1", "norm1b", "norm2", "ffn0", "ffn1", "out", "norm3")
MOE = tuple(f"moe{k}" for k in range(1, 10))
PATCH = tuple(f"patch{k}" for k in range(PIECES))
ORDER = {
    ("layer", "pe"):
        "proj patch0 patch1 soft0 cls1 soft1 norm2 patch2 cls2 soft2 cls3 soft3 ffn0 ffn1 out patch3 mix2 "
        "mix3 norm3",
    ("layer", "act"):
        "proj keys soft0 norm2 cls1 soft1 cls2 soft2 ffn0 soft3 ffn1 mix1 mix2 norm3",
    ("layer", "dve"):
        "norm1 norm1b soft0 norm2 cls1 soft1 sum0 cls2 soft2 sum1 head0 cls3 soft3 sum2 head1 sum3 head2 "
        "head3 mix1 spread out patch3 norm3 mix3",
    ("layer", "pool"):
        "norm1 keys cls1 norm1b sum0 sum1 ffn0 sum2 sum3 out norm3",
    ("last", "pe"):
        "moe2 patch0 patch1 patch2 moe3 norm2 moe4 ffn0 moe5 patch3 moe6 ffn1 out norm3 moe7 moe8 moe9",
    ("last", "act"):
        "moe2 moe3 norm2 moe4 ffn0 moe5 moe6 ffn1 norm3 moe8",
    ("last", "dve"):
        "moe1 moe2 norm1 norm1b moe3 norm2 moe4 moe5 patch3 moe6 out moe7 norm3 moe9",
    ("last", "pool"):
        "moe1 norm1 norm1b ffn0 out norm3",
    ("turn", "pe"):
        "init proj moe2 soft0 moe3 cls1 soft1 moe4 moe5 cls2 soft2 moe6 cls3 soft3 moe7 moe8 moe9 mix2 "
        "init1 mix3",
    ("turn", "act"):
        "init proj moe2 keys soft0 moe3 cls1 moe4 moe5 soft1 cls2 moe6 soft2 soft3 moe8 mix1 mix2 init1",
    ("turn", "dve"):
        "init moe1 moe2 soft0 moe3 cls1 moe4 moe5 soft1 sum0 cls2 soft2 sum1 head0 moe6 cls3 soft3 sum2 "
        "head1 moe7 sum3 head2 head3 mix1 spread init1 moe9 mix3",
    ("turn", "pool"):
        "init moe1 keys cls1 sum0 sum1 sum2 sum3 init1",
}


def schedule(engine):
    def listed(names, *where):
        return [(n, *where) for n in names]

    def weave(slot, *lists):
        items = {x[0] + ("1" if x[0] == "init" and x[2] == 1 else ""): x for each in lists for x in each}
        return [items[name] for name in ORDER[slot, engine].split() if name in items]

    def patches(it, n):
        return listed(PATCH, it, n // TILES, n % TILES) if it < ITERS else []

    out = []
    for n in range(TILES):
        out += patches(0, n)
    out.append(("init", 0, 0, 0))
    behind = {"keys": TILES, "soft1": TILES + 1, "soft2": TILES + 2, "soft3": TILES + 3}
    for x in listed(ATTN, 0, 0, 0):
        out.append(x)
        if x[0] in behind:
            out += patches(0, behind[x[0]])
    out.append(("init", 0, 1, 0))
    for it in range(ITERS):
        for l in range(LAYERS):
            out += weave("layer", listed(ATTN, it, 1, l), listed(FFN, it, 0, l), patches(it + 1, 2 * l))
            if l + 1 < LAYERS:
                out += weave("layer", listed(ATTN, it, 0, l + 1), listed(FFN, it, 1, l), patches(it + 1, 2 * l + 1))
            else:
                out += weave("last", listed(FFN, it, 1, l), listed(MOE, it, 0, 0), patches(it + 1, 2 * l + 1))
        if it + 1 < ITERS:
            out += weave("turn", listed(MOE, it, 1, 0),
                         listed(("init",) + ATTN, it + 1, 0, 0), [("init", it + 1, 1, 0)])
        else:
            out += listed(MOE, it, 1, 0)
    return out


def ring_jobs(seg, l):
    if seg == "norm3" and l + 1 == LAYERS:
        return []
    return {
        "init": ["T0", "T1"],
        "proj": ["q0", "q1", "k0", "k1"],
        "cls1": ["score"], "cls2": ["heads"], "cls3": ["turn"],
        "mix2": ["turn", "turnc"], "mix3": ["mix0", "mix1", "mixc"],
        "norm2": ["T0", "T1"],
        "ffn0": ["h0", "h1", "h2", "h3"],
        "ffn1": ["h0", "h1", "h2", "h3"],
        "out": ["out0", "out1"],
        "norm3": ["T0", "T1"],
        "moe2": ["T0", "T1", "gate"], "moe3": ["aff"], "moe4": ["gates", "oh0", "oh1", "ohc0", "ohc1"],
        "moe5": ["ohg", "ohcg", "xin0", "xin1", "xin2", "xin3"], "moe6": ["up0", "up1"], "moe7": ["down0", "down1"],
        "moe8": ["yT0", "yT1"], "moe9": ["sum", "sumc"],
    }.get(seg, [])


RING = 3


def psum_places():
    place, count, n = {}, [0] * RING, 0
    for seg, it, h, l in schedule("pe"):
        for job in ring_jobs(seg, l):
            b = n % RING
            count[b] += 1
            place[(it, seg, h, l, job)] = (b, count[b])
            n += 1
    return place


PLACE = psum_places()


class Signal:

    def __init__(self, sem, per, units, early=0):
        self.sem, self.per, self.units, self.early = sem, per, units, early

    def at(self, it, unit, k=None):
        return (it * self.units + unit) * self.per + (self.per if k is None else k) + self.early


class Job(NamedTuple):

    bank: object
    filled: object
    drained: object
    nth: object
    before: object


def vit_kernel(nc, x_main, x_rest, wp_main, wp_rest, cls0, pos, const, wqk, w1, w2, lvec, rows, gate, ew1, ew2, evec, out):
    ctx = ExitStack()
    with ctx:
        def sb(name, shape, dt=F32):
            return ctx.enter_context(nc.sbuf_tensor(name, shape, dt))

        def both(name, shape):
            return [sb(f"{name}{h}", shape) for h in range(HALVES)]

        def shared(name, shape):
            return [sb(name, shape)] * HALVES

        def signal(name, per=1, units=UNITS, early=0):
            return Signal(ctx.enter_context(nc.semaphore(name)), per, units, early)

        S = [ctx.enter_context(nc.psum_tensor(f"S{i}", [D, 2, 512], F32)) for i in range(SBANKS)]
        ringbank = [ctx.enter_context(nc.psum_tensor(f"ring{i}", [D, 512], F32)) for i in range(RING)]
        pp = ctx.enter_context(nc.psum_tensor("pp", [D, 512], F32))

        cst = sb("cst", [D, CONST_W])
        wpm = sb("wpm", [D, MAIN, D])
        wpr = sb("wpr", [REST + 1, D])
        posn = sb("posn", [D, D])
        wq = sb("wq", [D, LAYERS, 2, D])
        w1s = sb("w1s", [D, LAYERS, FF])
        w2s = sb("w2s", [D, LAYERS, FF // D, D])
        vec = sb("vec", [D, LAYERS, NVEC])
        row = sb("row", [D, LAYERS, NROW, D])
        bq4 = sb("bq4", [D, LAYERS])
        gw = sb("gw", [D, EXPERTS])
        ew1s = sb("ew1s", [D, EXPERTS, DFF])
        ew2s = sb("ew2s", [DFF, EXPERTS, D])
        ev = sb("ev", [D, 2, EXPERTS])
        pix = [sb(f"pix{i}", [D, MAIN, D]) for i in range(PIX)]
        pixr = [sb(f"pixr{i}", [REST + 1, D]) for i in range(PIX)]

        h0n = [both(f"h0n_{i}_", [D, SLOTN, D]) for i in range(2)]
        xT = both("xT", [D, WIDE])
        xn = both("xn", [D, SLOTN, D + 1])
        qT = shared("qT", [D, TOK])
        qx = shared("qx", [D, IMG * (IMG * HEADS + HEADS)])
        kP = shared("kP", [D, IMG, SEQ])
        kX = shared("kX", [D, IMG, HEADS, SEQ])
        A8 = shared("A8", [D, TILES, SEQ])
        U8 = shared("U8", [D, TILES, SEQ])
        EX = shared("EX", [D, TILES, D + IMG])
        ecl = shared("ecl", [D, TILES])
        ET = shared("ET", [D, TILES, D])
        EcT = shared("EcT", [IMG, TILES, D])
        LC = both("LC", [D, SLOTN, IMG])
        Pc = shared("Pc", [IMG * HEADS, SEQ])
        Vc = shared("Vc", [IMG, 2, SEQ])
        Ec = shared("Ec", [IMG, D + 1])
        r1 = both("r1", [D, SLOTN, D])
        nn = both("nn", [D, SLOTN, D])
        zn = both("zn", [D, SLOTN, D])
        zT = both("zT", [D, WIDE])
        hT = both("hT", [D, FF // D, TOK])
        st = both("st", [D, SLOTN, 6])
        mv = both("mv", [D, SLOTN, 2])
        rs = both("rs", [D, SLOTN])
        nm = both("nm", [D, SLOTN])
        sc = both("sc", [D, 16])
        P = [sb(f"P{i}", [D, HEADS, SEQ]) for i in range(XB)]
        mx = [sb(f"mx{i}", [D, HEADS]) for i in range(XB)]
        sm = [sb(f"sm{i}", [D, HEADS]) for i in range(XB)]
        aff = sb("aff", [D, SLOTN, EXPERTS])
        mxg = sb("mxg", [D, SLOTN])
        smg = sb("smg", [D, SLOTN])
        affT = sb("affT", [D, SEQ])
        gv = sb("gv", [D, SLOTS])
        gi = sb("gi", [D, SLOTS], U32)
        gf = sb("gf", [D, SLOTS])
        OH = sb("OH", [D, SLOTS, D])
        OHc = sb("OHc", [D, SLOTS, IMG])
        OHT = sb("OHT", [D, SLOTS * D])
        OHcT = sb("OHcT", [IMG, SLOTS * D])
        GX = sb("GX", [D, SLOTS, EXPERTS])
        gG = sb("gG", [D, IMG])
        OHG = sb("OHG", [D, IMG, PATCHES])
        OHcG = sb("OHcG", [D, IMG, IMG])
        big = sb("big", [D, SLOTS * D])

        def c_(name):
            at, n = CONST[name]
            return cst[:, at:at + n]

        ident = c_("ident")
        onehot = c_("onehot").rearrange("p (s i) -> p s i", s=SLOTN)

        HALF_E = EXPERTS // 2
        XIN = SLOTS * D
        flat = [hT[h][:].rearrange("p f t -> p (f t)") for h in range(HALVES)]
        xin = [f[:, 0:XIN].rearrange("p (e i s) -> p e i s", e=EXPERTS, i=IMG) for f in flat]
        hid = [f[:, XIN:2 * XIN].rearrange("p (e r) -> p e r", e=EXPERTS) for f in flat]
        Y = [f[:, 0:XIN].rearrange("p (i d) -> p i d", i=IMG) for f in flat]
        AX = big[:, 0:SLOTN * D].rearrange("p (s i e) -> p s i e", s=SLOTN, i=IMG)
        eo = big[:].rearrange("p (i c) -> p i c", i=IMG)
        eo4 = big[:].rearrange("p (i s e) -> p e i s", e=EXPERTS, i=IMG)

        out_h = out.rearrange("(u t a) k d -> u t a k d", t=TILES, a=2)

        wp_in = signal("wp_in", 16)
        w_in = signal("w_in", 16)
        late_in = signal("late_in", 16)
        pix_in = [signal(f"pix_in{i}", 32, 1) for i in range(PIX)]
        out_done = [signal(f"out_done{h}", 48, 1) for h in range(HALVES)]
        set_cls = signal("set_cls")
        set_dve = signal("set_dve")
        set_pool = signal("set_pool")
        filled = [signal(f"filled{b}") for b in range(RING)]
        drained = [signal(f"drained{b}") for b in range(RING)]
        patch_sum = signal("patch_sum", 1, PAIRS)
        patch_out = signal("patch_out", 1, PAIRS)
        qx_in = signal("qx_in")
        s_full = signal("s_full", TILES)
        kx_act = signal("kx_act", ACT_HEADS)
        kx_pool = signal("kx_pool")
        s_max = signal("s_max", TILES)
        s_sub = signal("s_sub", TILES, early=SBANKS)
        p_exp = signal("p_exp", TILES)
        p_sum = signal("p_sum", TILES)
        p_rec = signal("p_rec", TILES)
        p_mul = signal("p_mul", TILES)
        a_in = signal("a_in", TILES)
        u_in = signal("u_in", 3)
        e_in = signal("e_in")
        ec_in = signal("ec_in")
        cls_dve = signal("cls_dve", 9)
        cls_act = signal("cls_act")
        r_rec = signal("r_rec", 2)
        ln_st = signal("ln_st", 2, 1)
        ln_mv = signal("ln_mv", 2, 1)
        ln_ve = signal("ln_ve", 1, 1)
        ln_rs = signal("ln_rs", 1, 1)
        ln_nm = signal("ln_nm", 2, 1)
        ln_act = signal("ln_act")
        ln_act3 = signal("ln_act3")
        ln_in = signal("ln_in", 2, 1)
        y_mid = signal("y_mid", 2)
        y_in = signal("y_in", 2)
        z_mid = signal("z_mid")
        z_in = signal("z_in")
        r3_in = signal("r3_in")
        x_mid = signal("x_mid")
        x_in = signal("x_in")
        r0_in = signal("r0_in", 1, HALVES)
        moe_dve = signal("moe_dve", 11, HALVES)
        moe_act = signal("moe_act", 3, HALVES)

        st_order = {(it, n, h, l): i for i, (n, it, h, l) in enumerate(
            x for x in schedule("dve") if x[0] in ("init", "norm1", "norm1b", "out", "moe1"))}
        rs_order = {(it, n, h, l): i for i, (n, it, h, l) in enumerate(
            x for x in schedule("pool") if x[0] in ("init", "norm1", "norm1b", "out", "moe1"))}
        in_order = {(it, n, h, l): i for i, (n, it, h, l) in enumerate(
            x for x in schedule("dve") if x[0] in ("init", "norm2", "norm3", "moe2"))}

        def job(it, seg, h, l, name):
            b, n = PLACE[(it, seg, h, l, name)]
            return Job(ringbank[b], filled[b].sem, drained[b].sem, n, n - 1)

        def jobs(it, seg, h, l, *names):
            return [job(it, seg, h, l, name) for name in names]

        def unit(h, l):
            return l * HALVES + h

        def nat(j):
            return range(0, 2) if j == 0 else range(2, SLOTN)

        def cols(j):
            return slice(0, CHUNK) if j == 0 else slice(CHUNK, TOK)

        def width(j):
            return CHUNK if j == 0 else TOK - CHUNK

        N_WP = 4
        N_W = 5
        N_LATE = 8
        block = ctx.enter_context(nc.Block())

        @block.sync
        def _(sp):
            for dst, src in ((wpr[:], wp_rest), (wpm[:], wp_main), (posn[0:PATCHES, :], pos[1:SEQ, :]),
                             (posn[PATCHES:D, :], pos[1:SEQ, :])):
                sp.dma_start(dst, src).then_inc(wp_in.sem, 16)

            def load(it, n):
                i = (it * PAIRS + n) % PIX
                sp.dma_start(pix[i][:], x_main[it * PAIRS + n]).then_inc(pix_in[i].sem, 16)
                sp.dma_start(pixr[i][0:REST, :], x_rest[it * PAIRS + n]).then_inc(pix_in[i].sem, 16)

            sp.wait_ge(set_pool.sem, PIX)
            for n in range(PIX):
                load(0, n)
            for dst, src in ((cst[:], const), (vec[:], lvec), (big[0:IMG, 0:D], cls0.broadcast_to([IMG, D])),
                             (big[0:IMG, D:2 * D], pos[0:1, :].broadcast_to([IMG, D])),
                             (wq[:], wqk)):
                sp.dma_start(dst, src).then_inc(w_in.sem, 16)

            def reload(it, n):
                sp.wait_ge(patch_sum.sem, patch_sum.at(it, n - PIX))
                load(it, n)

            def iteration(it, more):
                if more:
                    for n in range(PAIRS):
                        reload(it + 1, n)
                for h in range(HALVES):
                    o = out_h[it * HALVES + h]
                    for R in jobs(it, "moe9", h, 0, "sum", "sumc"):
                        sp.wait_ge(R.drained, R.nth)
                    for a in range(2):
                        sp.dma_start(o[:, a, 1:SEQ, :].rearrange("t j d -> j t d"),
                                     nn[h][PATCHES * a:PATCHES * (a + 1), 0:TILES, :]).then_inc(out_done[h].sem, 16)
                    sp.dma_start(o[:, :, 0, :], nn[h][0:IMG, TILES, :]).then_inc(out_done[h].sem, 16)

            for n in range(PIX, PAIRS):
                reload(0, n)
            for it in range(ITERS):
                iteration(it, it + 1 < ITERS)
            for h in range(HALVES):
                sp.wait_ge(out_done[h].sem, out_done[h].at(ITERS - 1, 0))

        @block.gpsimd
        def _(pool):
            for i in range(PIX):
                pool.memset(pixr[i][:], 1.0).then_inc(set_pool.sem, 1)
            for z in (qx[0], EX[0], r1[0], r1[1], LC[0], LC[1]):
                pool.memset(z[:], 0.0).then_inc(set_pool.sem, 1)

            def rstd(it, key, h):
                u = rs_order[key]
                if u > 0:
                    pool.wait_ge(ln_nm.sem, ln_nm.at(u - 1, 0))
                pool.wait_ge(ln_mv.sem, ln_mv.at(st_order[key], 0))
                pool.tensor_scalar(rs[h][:], mv[h][:, :, 1], EPS, 1.0, ALU.add, ALU.mult).then_inc(ln_ve.sem, 1)
                pool.tensor_scalar(nm[h][:], mv[h][:, :, 0], -1.0, 1.0, ALU.mult, ALU.mult).then_inc(ln_nm.sem, 1)
                pool.wait_ge(ln_ve.sem, ln_ve.at(u, 0))
                pool.tensor_tensor(rs[h][:], rs[h][:], c_("pow")[:, 0:SLOTN], ALU.pow).then_inc(ln_rs.sem, 1)
                pool.wait_ge(ln_nm.sem, ln_nm.at(u, 0, 1))
                pool.wait_ge(ln_rs.sem, ln_rs.at(u, 0))
                pool.tensor_tensor(nm[h][:], nm[h][:], rs[h][:], ALU.mult).then_inc(ln_nm.sem, 1)

            def row_(l, name):
                return row[:, l, ROW[name]:ROW[name] + 1, :].broadcast_to([D, SLOTN, D])

            def probabilities(it, n, t):
                g = (n * TILES + t) % XB
                pool.wait_ge(p_rec.sem, p_rec.at(it, n, t + 1))
                pool.tensor_tensor(P[g][:], P[g][:], sm[g][:].unsqueeze(2).broadcast_to([D, HEADS, SEQ]),
                                   ALU.mult).then_inc(p_mul.sem, 1)

            pool.wait_ge(w_in.sem, 16 * N_W)
            pool.wait_ge(set_pool.sem, PIX + 6)
            pool.wait_ge(set_dve.sem, 1)
            for seg, it, h, l in schedule("pool"):
                n = unit(h, l)
                if seg == "keys":
                    for R in jobs(it, "proj", h, l, "k0", "k1"):
                        pool.wait_ge(R.drained, R.nth)
                    for k in range(ACT_HEADS, HEADS):
                        i = pool.tensor_scalar(kX[h][:, :, k, :], kP[h][:], c_("headmask")[:, k:k + 1], 1.0, ALU.mult,
                                               ALU.mult)
                    i.then_inc(kx_pool.sem, 1)
                elif seg == "cls1":
                    for R in jobs(it, "proj", h, l, "q1"):
                        pool.wait_ge(R.drained, R.nth)
                    pool.tensor_tensor(qx[h][:].rearrange("p (i c) -> p i c", i=IMG)[:, :, 0:HEADS],
                                       qT[h][:, CHUNK * 2:TOK].unsqueeze(2).broadcast_to([D, IMG, HEADS]),
                                       c_("headmask").unsqueeze(1).broadcast_to([D, IMG, HEADS]),
                                       ALU.mult).then_inc(qx_in.sem, 1)
                elif seg[:3] == "sum":
                    probabilities(it, n, int(seg[3]))
                elif seg in ("init", "norm1", "norm1b", "out", "moe1"):
                    rstd(it, (it, seg, h, l), h)
                elif seg == "ffn0":
                    pool.wait_ge(ln_in.sem, ln_in.at(in_order[(it, "norm2", h, l)], 0))
                    pool.wait_ge(ln_act.sem, ln_act.at(it, n))
                    pool.tensor_tensor(nn[h][:], zn[h][:], row_(l, "g2"), ALU.mult).then_inc(z_mid.sem, 1)
                    pool.wait_ge(z_mid.sem, z_mid.at(it, n))
                    pool.tensor_tensor(nn[h][:], nn[h][:], row_(l, "bt2"), ALU.add).then_inc(z_in.sem, 1)
                elif seg == "norm3":
                    pool.wait_ge(ln_in.sem, ln_in.at(in_order[(it, seg, h, l)], 0))
                    pool.wait_ge(ln_act3.sem, ln_act3.at(it, n))
                    pool.tensor_tensor(xn[h][:, :, 0:D], nn[h][:], row_(l, "g3"), ALU.mult).then_inc(x_mid.sem, 1)
                    pool.wait_ge(x_mid.sem, x_mid.at(it, n))
                    pool.tensor_tensor(xn[h][:, :, 0:D], xn[h][:, :, 0:D], row_(l, "bt3"), ALU.add
                                       ).then_inc(x_in.sem, 1)

        @block.scalar
        def _(act):
            def evacuate(it, seg, h, l, what, dst, bias=None, scale=1.0):
                J = job(it, seg, h, l, what)
                act.wait_ge(J.filled, J.nth)
                ps = J.bank
                src = ps[:, 0:dst.shape[-1]]
                if bias is None:
                    i = act.copy(dst, src)
                else:
                    i = act.activation(dst, src, ACT.Identity, bias=bias, scale=scale)
                i.then_inc(J.drained, 1)

            def normalise(it, h, l, taken, source, dst, done):
                act.wait_ge(ln_nm.sem, ln_nm.at(rs_order[(it, taken, h, l)], 0))
                for s in range(DVE_SLOTS, SLOTN):
                    i = act.activation(dst[:, s, :], source[:, s, :], ACT.Identity, bias=nm[h][:, s:s + 1],
                                       scale=rs[h][:, s:s + 1])
                i.then_inc(done.sem, 1)

            def v_(l, name):
                return vec[:, l, VEC[name]:VEC[name] + 1]

            act.wait_ge(pix_in[PIX - 1].sem, pix_in[PIX - 1].at(0, 0))
            for dst, src in ((row[:], rows[:, :, 0:NROW].broadcast_to([D, LAYERS, NROW, D])),
                             (big[:, 4 * D:8 * D].rearrange("p (l d) -> p l d", l=LAYERS),
                              rows[:, :, NROW].broadcast_to([D, LAYERS, D])), (w1s[:], w1), (w2s[:], w2), (gw[:], gate), (ew1s[:], ew1), (ew2s[:], ew2),
                             (ev[:], evec)):
                act.dma_start(dst, src).then_inc(late_in.sem, 16)
            act.wait_ge(w_in.sem, 16 * N_W)
            act.wait_ge(set_pool.sem, PIX + 6)
            act.wait_ge(set_dve.sem, 1)
            for seg, it, h, l in schedule("act"):
                n = unit(h, l)
                if seg == "init":
                    for j in range(2):
                        evacuate(it, seg, h, l, f"T{j}", xT[h][:, cols(j)])
                elif seg == "proj":
                    for j in range(2):
                        evacuate(it, seg, h, l, f"q{j}", qT[h][:, cols(j)], bq4[:, l:l + 1], 0.25)
                    for j in range(2):
                        J = job(it, seg, h, l, f"k{j}")
                        act.wait_ge(J.filled, J.nth)
                        ps = J.bank
                        i = act.activation(kP[h][:, 4 * j:4 * j + 4, 1:SEQ],
                                           ps[:, 0:CHUNK].rearrange("p (i k) -> p i k", i=4),
                                           ACT.Identity, bias=v_(l, "bk"))
                        if j == 1:
                            i = act.activation(kP[h][:, :, 0], ps[:, CHUNK:width(1)], ACT.Identity, bias=v_(l, "bk"))
                        i.then_inc(J.drained, 1)
                elif seg == "keys":
                    for R in jobs(it, "proj", h, l, "k0", "k1"):
                        act.wait_ge(R.drained, R.nth)
                    for k in range(ACT_HEADS):
                        act.activation(kX[h][:, :, k, :], kP[h][:], ACT.Copy, scale=c_("headmask")[:, k:k + 1]
                                       ).then_inc(kx_act.sem, 1)
                elif seg[:4] == "soft":
                    t = int(seg[4])
                    g = (n * TILES + t) % XB
                    act.wait_ge(s_sub.sem, s_sub.at(it, n, t + 1))
                    act.activation(P[g][:], P[g][:], ACT.Exp).then_inc(p_exp.sem, 1)
                elif seg == "cls1":
                    J = job(it, seg, h, l, "score")
                    act.wait_ge(J.filled, J.nth)
                    ps = J.bank
                    act.wait_ge(cls_dve.sem, cls_dve.at(it, n, 2))
                    act.activation(Pc[h][:], ps[0:IMG * HEADS, 0:SEQ], ACT.Exp, bias=sc[h][0:IMG * HEADS, 1:2],
                                   accum_out=sc[h][0:IMG * HEADS, 2:3]).then_inc(J.drained, 1)
                elif seg == "cls2":
                    act.wait_ge(cls_dve.sem, cls_dve.at(it, n, 6))
                    act.activation(Ec[h][:, 0:D].rearrange("p (a k) -> p a k", a=2),
                                   Vc[h][:, 0, 1:SEQ].unsqueeze(1).broadcast_to([IMG, 2, PATCHES]),
                                   ACT.Exp, scale=1.0 / HEADS)
                    act.activation(Ec[h][:, D:D + 1], Vc[h][:, 0, 0:1], ACT.Exp,
                                   scale=1.0 / HEADS).then_inc(cls_act.sem, 1)
                elif seg == "mix1":
                    act.wait_ge(u_in.sem, u_in.at(it, n))
                    for a in range(2):
                        p = slice(PATCHES * a, PATCHES * (a + 1))
                        act.activation(EX[h][p, :, PATCHES * a:PATCHES * (a + 1)], U8[h][p, :, 1:SEQ], ACT.Exp,
                                       scale=1.0 / HEADS)
                    act.activation(ecl[h][:], U8[h][:, :, 0], ACT.Exp, scale=1.0 / HEADS).then_inc(e_in.sem, 1)
                elif seg == "mix2":
                    J = job(it, seg, h, l, "turn")
                    act.wait_ge(J.filled, J.nth)
                    ps = J.bank
                    act.copy(ET[h][:], ps[:, :].rearrange("p (t q) -> p t q", t=TILES)
                             ).then_inc(J.drained, 1)
                    J = job(it, seg, h, l, "turnc")
                    act.wait_ge(J.filled, J.nth)
                    ps = J.bank
                    act.copy(EcT[h][:], ps[0:IMG, :].rearrange("p (t q) -> p t q", t=TILES)
                             ).then_inc(J.drained, 1)
                elif seg == "norm2":
                    normalise(it, h, l, "norm1b", nn[h], zn[h], ln_act)
                    for j in range(2):
                        evacuate(it, seg, h, l, f"T{j}", zT[h][:, cols(j)], v_(l, "bt2"), v_(l, "g2"))
                elif seg[:3] == "ffn":
                    j = int(seg[3])
                    for f in range(FF // D):
                        J = job(it, seg, h, l, f"h{f}")
                        act.wait_ge(J.filled, J.nth)
                        ps = J.bank
                        act.activation(hT[h][:, f, cols(j)], ps[:, 0:width(j)], ACT.Relu,
                                       bias=v_(l, f"b1_{f}")).then_inc(J.drained, 1)
                elif seg == "norm3":
                    normalise(it, h, l, "out", r1[h], nn[h], ln_act3)
                    if l + 1 == LAYERS:
                        continue
                    for j in range(2):
                        evacuate(it, seg, h, l, f"T{j}", xT[h][:, cols(j)], v_(l, "bt3"), v_(l, "g3"))
                elif seg == "moe2":
                    for j in range(2):
                        evacuate(it, seg, h, l, f"T{j}", zT[h][:, cols(j)])
                elif seg == "moe3":
                    for R in jobs(it, "moe2", h, l, "gate"):
                        act.wait_ge(R.drained, R.nth)
                    act.activation(aff[:], aff[:], ACT.Exp).then_inc(moe_act.sem, 1)
                    J = job(it, seg, h, l, "aff")
                    act.wait_ge(J.filled, J.nth)
                    ps = J.bank
                    act.copy(affT[:], ps[:, 0:SEQ]).then_inc(J.drained, 1)
                elif seg == "moe4":
                    evacuate(it, seg, h, l, "gates", gG[:])
                    for u in range(2):
                        J = job(it, seg, h, l, f"oh{u}")
                        act.wait_ge(J.filled, J.nth)
                        ps = J.bank
                        act.copy(OHT[:].rearrange("p (i s e) -> p s i e", i=IMG, s=SLOTS)[:, 4 * u:4 * u + 4],
                                 ps[:, :].rearrange("p (s i e) -> p s i e", s=4, i=IMG)).then_inc(J.drained, 1)
                    for u in range(2):
                        J = job(it, seg, h, l, f"ohc{u}")
                        act.wait_ge(J.filled, J.nth)
                        ps = J.bank
                        act.copy(OHcT[:].rearrange("p (i s e) -> p s i e", i=IMG, s=SLOTS)[:, 4 * u:4 * u + 4],
                                 ps[0:IMG, :].rearrange("p (s i e) -> p s i e", s=4, i=IMG)).then_inc(J.drained, 1)
                elif seg == "moe5":
                    for t in range(TILES):
                        J = job(it, seg, h, l, f"xin{t}")
                        act.wait_ge(J.filled, J.nth)
                        ps = J.bank
                        act.copy(xin[h][:, :, 2 * t:2 * t + 2, :],
                                 ps[:, 0:2 * D].rearrange("p (a s e) -> p e a s", s=SLOTS, a=2)
                                 ).then_inc(J.drained, 1)
                elif seg == "moe6":
                    for u in range(2):
                        for R in jobs(it, seg, h, l, f"up{u}"):
                            act.wait_ge(R.drained, R.nth)
                        v = hid[h][:, HALF_E * u:HALF_E * (u + 1), :]
                        act.activation(v, v, ACT.Gelu_apprx_tanh).then_inc(moe_act.sem, 1)
                elif seg == "moe8":
                    for u in range(2):
                        evacuate(it, seg, h, l, f"yT{u}", Y[h][:, 4 * u:4 * u + 4, :].rearrange("p i d -> p (i d)"))

        @block.vector
        def _(dve):
            for h in range(HALVES):
                for z in (xT, zT):
                    dve.memset(z[h][:, TOK:WIDE], 0.0)
                dve.memset(xn[h][:, :, D:D + 1], 1.0)
                for i in range(2):
                    dve.memset(h0n[i][h][:, TILES, :], 0.0).then_inc(set_cls.sem, 1)
            for i in range(SBANKS):
                dve.memset(sc[i][:], 0.0).then_inc(s_sub.sem, 1)
            dve.wait_ge(wp_in.sem, 16 * N_WP)

            def setup():
                dve.wait_ge(w_in.sem, 16 * N_W)
                dve.wait_ge(set_cls.sem, 2 * HALVES)
                for h in range(HALVES):
                    for i in range(2):
                        dve.tensor_tensor(h0n[i][h][0:IMG, TILES, :], big[0:IMG, 0:D], big[0:IMG, D:2 * D], ALU.mult
                                          ).then_inc(set_cls.sem, 1)
                dve.tensor_scalar(bq4[:], vec[:, :, VEC["bq"]], 0.25, None, ALU.mult).then_inc(set_dve.sem, 1)

            def statistics(it, seg, h, l, source, ready):
                u = st_order[(it, seg, h, l)]
                for j in range(2):
                    ready(j)
                    for s in nat(j):
                        ins = dve.bn_stats(st[h][:, s, :], source[:, s, 0:D])
                    ins.then_inc(ln_st.sem, 1)
                for j in range(2):
                    dve.wait_ge(ln_st.sem, ln_st.at(u, 0, j + 1))
                    for s in nat(j):
                        ins = dve.bn_aggr(mv[h][:, s, :], st[h][:, s, :])
                    ins.then_inc(ln_mv.sem, 1)

            def normalise(it, seg, h, l, taken, source, dst, slots=SLOTN):
                dve.wait_ge(ln_rs.sem, ln_rs.at(rs_order[(it, taken, h, l)], 0))
                for j in range(2):
                    for s in [s for s in nat(j) if s < slots]:
                        ins = dve.tensor_scalar(dst[:, s, 0:D], source[:, s, 0:D], mv[h][:, s, 0:1], rs[h][:, s:s + 1],
                                                ALU.subtract, ALU.mult)
                    ins.then_inc(ln_in.sem, 1)

            def row_(l, name):
                return row[:, l, ROW[name], :]

            def sums(it, n, t):
                g = (n * TILES + t) % XB
                dve.wait_ge(p_exp.sem, p_exp.at(it, n, t + 1))
                dve.tensor_reduce(sm[g][:], P[g][:], X, ALU.add).then_inc(p_sum.sem, 1)
                dve.wait_ge(p_sum.sem, p_sum.at(it, n, t + 1))
                dve.reciprocal(sm[g][:], sm[g][:]).then_inc(p_rec.sem, 1)

            def heads(it, n, h, t):
                g = (n * TILES + t) % XB
                dve.wait_ge(p_mul.sem, p_mul.at(it, n, t + 1))
                dve.tensor_reduce(A8[h][:, t, :], P[g][:].rearrange("p h k -> p k h"), X, ALU.add).then_inc(a_in.sem, 1)

            for seg, it, h, l in schedule("dve"):
                n = unit(h, l)
                C = IMG * HEADS
                if seg == PATCH[-1]:
                    dve.wait_ge(patch_sum.sem, patch_sum.at(it, h * TILES + l))
                    dve.tensor_tensor(h0n[it % 2][h][:, l, :], pp[:, 0:D], posn[:], ALU.mult
                                      ).then_inc(patch_out.sem, 1)
                elif seg == "init":
                    if it == 0 and h == 0:
                        setup()

                    def ready(j):
                        dve.wait_ge(patch_out.sem, patch_out.at(it, (h + 1) * TILES - 1))
                        dve.wait_ge(set_cls.sem, 4 * HALVES)
                    statistics(it, seg, h, l, h0n[it % 2][h], ready)
                    normalise(it, seg, h, l, "init", h0n[it % 2][h], xn[h])
                elif seg[:4] == "soft":
                    t = int(seg[4])
                    T = n * TILES + t
                    g = T % XB
                    dve.wait_ge(s_full.sem, s_full.at(it, n, t + 1))
                    s4 = S[T % SBANKS][:, :, 0:4 * SEQ].rearrange("p b (h k) -> p b h k", h=4)
                    dve.tensor_reduce(mx[g][:].rearrange("p (b h) -> p b h", b=2), s4, X, ALU.max
                                      ).then_inc(s_max.sem, 1)
                    dve.wait_ge(s_max.sem, s_max.at(it, n, t + 1))
                    dve.tensor_tensor(P[g][:].rearrange("p (b h) k -> p b h k", b=2), s4,
                                      mx[g][:].rearrange("p (b h) -> p b h", b=2).unsqueeze(3)
                                      .broadcast_to([D, 2, 4, SEQ]), ALU.subtract).then_inc(s_sub.sem, 1)
                elif seg[:3] == "sum":
                    sums(it, n, int(seg[3]))
                elif seg[:4] == "head":
                    heads(it, n, h, int(seg[4]))
                elif seg == "cls1":
                    J = job(it, seg, h, l, "score")
                    dve.wait_ge(J.filled, J.nth)
                    ps = J.bank
                    dve.tensor_reduce(sc[h][0:C, 0:1], ps[0:C, 0:SEQ], X, ALU.max).then_inc(cls_dve.sem, 1)
                    dve.wait_ge(cls_dve.sem, cls_dve.at(it, n, 1))
                    dve.tensor_scalar(sc[h][0:C, 1:2], sc[h][0:C, 0:1], -1.0, None, ALU.mult
                                      ).then_inc(cls_dve.sem, 1)
                elif seg == "cls2":
                    for R in jobs(it, "cls1", h, l, "score"):
                        dve.wait_ge(R.drained, R.nth)
                    dve.reciprocal(sc[h][0:C, 3:4], sc[h][0:C, 2:3]).then_inc(cls_dve.sem, 1)
                    dve.wait_ge(cls_dve.sem, cls_dve.at(it, n, 3))
                    dve.tensor_scalar(Pc[h][:], Pc[h][:], sc[h][0:C, 3:4], None, ALU.mult).then_inc(cls_dve.sem, 1)
                    J = job(it, seg, h, l, "heads")
                    dve.wait_ge(J.filled, J.nth)
                    ps = J.bank
                    dve.scalar_tensor_tensor(Vc[h][:, 0, :], ps[0:IMG, 0:SEQ], 0.0, c_("negc")[0:IMG, :],
                                             ALU.not_equal, ALU.mult).then_inc(cls_dve.sem, 1)
                    dve.tensor_tensor(Vc[h][:, 1, :], ps[0:IMG, 0:SEQ], c_("posc")[0:IMG, :], ALU.add
                                      ).then_inc(J.drained, 1)
                    dve.wait_ge(cls_dve.sem, cls_dve.at(it, n, 5))
                    for R in jobs(it, seg, h, l, "heads"):
                        dve.wait_ge(R.drained, R.nth)
                    dve.tensor_tensor(Vc[h][:, 0, :], Vc[h][:, 0, :], Vc[h][:, 1, :], ALU.add
                                      ).then_inc(cls_dve.sem, 1)
                elif seg == "cls3":
                    dve.wait_ge(cls_act.sem, cls_act.at(it, n))
                    dve.tensor_reduce(sc[h][0:IMG, 4:5], Ec[h][:, PATCHES:D + 1], X, ALU.add
                                      ).then_inc(cls_dve.sem, 1)
                    dve.wait_ge(cls_dve.sem, cls_dve.at(it, n, 7))
                    dve.reciprocal(sc[h][0:IMG, 5:6], sc[h][0:IMG, 4:5]).then_inc(cls_dve.sem, 1)
                    dve.tensor_scalar(LC[h][0:IMG, TILES, :], ident[0:IMG, 0:IMG], Ec[h][:, D:D + 1], None,
                                      ALU.mult).then_inc(cls_dve.sem, 1)
                    J = job(it, seg, h, l, "turn")
                    dve.wait_ge(J.filled, J.nth)
                    ps = J.bank
                    dve.tensor_tensor(LC[h][:, 0:TILES, :], onehot[:, 0:TILES, :],
                                      ps[:, 0:IMG].unsqueeze(1).broadcast_to([D, TILES, IMG]), ALU.mult
                                      ).then_inc(J.drained, 1)
                elif seg == "mix1":
                    dve.wait_ge(a_in.sem, a_in.at(it, n))
                    dve.scalar_tensor_tensor(U8[h][:], A8[h][:], 0.0,
                                             c_("neg").unsqueeze(1).broadcast_to([D, TILES, SEQ]),
                                             ALU.not_equal, ALU.mult).then_inc(u_in.sem, 1)
                    dve.tensor_tensor(A8[h][:], A8[h][:], c_("pos8").unsqueeze(1).broadcast_to([D, TILES, SEQ]),
                                      ALU.add).then_inc(u_in.sem, 1)
                    dve.wait_ge(u_in.sem, u_in.at(it, n, 2))
                    dve.tensor_tensor(U8[h][:], U8[h][:], A8[h][:], ALU.add).then_inc(u_in.sem, 1)
                elif seg == "spread":
                    dve.wait_ge(e_in.sem, e_in.at(it, n))
                    dve.tensor_tensor(EX[h][:, :, D:D + IMG], onehot[:, 0:TILES, :],
                                      ecl[h][:].unsqueeze(2).broadcast_to([D, TILES, IMG]), ALU.mult
                                      ).then_inc(ec_in.sem, 1)
                elif seg == "mix3":
                    for j in range(2):
                        J = job(it, seg, h, l, f"mix{j}")
                        dve.wait_ge(J.filled, J.nth)
                        ps = J.bank
                        v = ps[:, 0:2 * (D + 1)].rearrange("p (t d) -> p t d", t=2)
                        dve.reciprocal(sc[h][:, 8 + 2 * j:10 + 2 * j], v[:, :, D]).then_inc(r_rec.sem, 1)
                        dve.wait_ge(r_rec.sem, r_rec.at(it, n, j + 1))
                        for i in range(2):
                            t = 2 * j + i
                            ins = dve.scalar_tensor_tensor(r1[h][:, t, :], v[:, i, 0:D], sc[h][:, 8 + t:9 + t],
                                                           xn[h][:, t, 0:D], ALU.mult, ALU.add)
                        ins.then_inc(J.drained, 1)
                    J = job(it, seg, h, l, "mixc")
                    dve.wait_ge(J.filled, J.nth)
                    ps = J.bank
                    dve.wait_ge(cls_dve.sem, cls_dve.at(it, n, 8))
                    dve.scalar_tensor_tensor(r1[h][0:IMG, TILES, :], ps[0:IMG, 0:D], sc[h][0:IMG, 5:6],
                                             xn[h][0:IMG, TILES, 0:D], ALU.mult, ALU.add
                                             ).then_inc(J.drained, 1)
                elif seg == "norm1":
                    def ready(j):
                        for R in jobs(it, "mix3", h, l, *((f"mix{j}",) if j == 0 else ("mix1", "mixc"))):
                            dve.wait_ge(R.drained, R.nth)
                    statistics(it, seg, h, l, r1[h], ready)
                elif seg == "norm1b":
                    if it == 0 and n == 0:
                        dve.wait_ge(late_in.sem, 16 * N_LATE)
                        dve.tensor_tensor(row[:, :, ROW["bt2"], :], row[:, :, ROW["bt2"], :],
                                          big[:, 4 * D:8 * D].rearrange("p (l d) -> p l d", l=LAYERS), ALU.add)
                    if l == 0 and it > 0:
                        dve.wait_ge(out_done[h].sem, out_done[h].at(it, 0, 0))
                    for j in range(2):
                        dve.wait_ge(ln_mv.sem, ln_mv.at(st_order[(it, "norm1", h, l)], 0, j + 1))
                        for s in nat(j):
                            ins = dve.scalar_tensor_tensor(nn[h][:, s, :], r1[h][:, s, :], mv[h][:, s, 0:1],
                                                           row_(l, "g1"), ALU.subtract, ALU.mult)
                        ins.then_inc(y_mid.sem, 1)
                    dve.wait_ge(ln_rs.sem, ln_rs.at(rs_order[(it, "norm1", h, l)], 0))
                    for j in range(2):
                        dve.wait_ge(y_mid.sem, y_mid.at(it, n, j + 1))
                        for s in nat(j):
                            ins = dve.scalar_tensor_tensor(nn[h][:, s, :], nn[h][:, s, :], rs[h][:, s:s + 1],
                                                           row_(l, "bt1"), ALU.mult, ALU.add)
                        ins.then_inc(y_in.sem, 1)

                    def ready(j):
                        dve.wait_ge(y_in.sem, y_in.at(it, n, j + 1))
                    statistics(it, seg, h, l, nn[h], ready)
                elif seg == "norm2":
                    normalise(it, seg, h, l, "norm1b", nn[h], zn[h], DVE_SLOTS)
                elif seg == "out":
                    dve.wait_ge(z_in.sem, z_in.at(it, n))
                    for j in range(2):
                        J = job(it, seg, h, l, f"out{j}")
                        dve.wait_ge(J.filled, J.nth)
                        ps = J.bank
                        if j == 1:
                            dve.tensor_tensor(r1[h][0:IMG, TILES, :], ps[0:IMG, 2 * D:3 * D],
                                              nn[h][0:IMG, TILES, :], ALU.add).then_inc(r3_in.sem, 1)
                        dve.tensor_tensor(r1[h][:, 2 * j:2 * j + 2, :],
                                          ps[:, 0:2 * D].rearrange("p (t d) -> p t d", t=2),
                                          nn[h][:, 2 * j:2 * j + 2, :], ALU.add).then_inc(J.drained, 1)

                    def ready(j):
                        for R in jobs(it, "out", h, l, f"out{j}"):
                            dve.wait_ge(R.drained, R.nth)
                        if j == 1:
                            dve.wait_ge(r3_in.sem, r3_in.at(it, n))
                    statistics(it, seg, h, l, r1[h], ready)
                elif seg == "norm3":
                    normalise(it, seg, h, l, "out", r1[h], nn[h], DVE_SLOTS)
                elif seg == "moe1":
                    dve.wait_ge(x_in.sem, x_in.at(it, unit(h, LAYERS - 1)))
                    dve.tensor_tensor(r1[h][:], h0n[it % 2][h][:], xn[h][:, :, 0:D], ALU.add).then_inc(r0_in.sem, 1)

                    def ready(j):
                        dve.wait_ge(r0_in.sem, r0_in.at(it, h))
                    statistics(it, seg, h, l, r1[h], ready)
                elif seg == "moe2":
                    normalise(it, seg, h, l, "moe1", r1[h], nn[h])
                    J = job(it, seg, h, l, "gate")
                    dve.wait_ge(J.filled, J.nth)
                    ps = J.bank
                    g3 = ps[:, 0:SLOTN * EXPERTS].rearrange("p (s e) -> p s e", e=EXPERTS)
                    dve.tensor_reduce(mxg[:], g3, X, ALU.max).then_inc(moe_dve.sem, 1)
                    dve.wait_ge(moe_dve.sem, moe_dve.at(it, h, 1))
                    dve.tensor_tensor(aff[:], g3, mxg[:].unsqueeze(2).broadcast_to([D, SLOTN, EXPERTS]),
                                      ALU.subtract).then_inc(J.drained, 1)
                elif seg == "moe3":
                    dve.wait_ge(moe_act.sem, moe_act.at(it, h, 1))
                    dve.tensor_reduce(smg[:], aff[:], X, ALU.add).then_inc(moe_dve.sem, 1)
                    dve.wait_ge(moe_dve.sem, moe_dve.at(it, h, 2))
                    dve.reciprocal(smg[:], smg[:]).then_inc(moe_dve.sem, 1)
                    dve.wait_ge(moe_dve.sem, moe_dve.at(it, h, 3))
                    dve.tensor_tensor(aff[:], aff[:], smg[:].unsqueeze(2).broadcast_to([D, SLOTN, EXPERTS]),
                                      ALU.mult).then_inc(moe_dve.sem, 1)
                    dve.wait_ge(moe_dve.sem, moe_dve.at(it, h, 4))
                    dve.tensor_tensor(AX, aff[:].unsqueeze(2).broadcast_to([D, SLOTN, IMG, EXPERTS]),
                                      onehot.unsqueeze(3).broadcast_to([D, SLOTN, IMG, EXPERTS]), ALU.mult
                                      ).then_inc(moe_dve.sem, 1)
                elif seg == "moe4":
                    for R in jobs(it, "moe3", h, l, "aff"):
                        dve.wait_ge(R.drained, R.nth)
                    dve.max(gv[:], affT[:]).then_inc(moe_dve.sem, 1)
                    dve.wait_ge(moe_dve.sem, moe_dve.at(it, h, 6))
                    dve.tensor_tensor(GX[:], gv[:].unsqueeze(2).broadcast_to([D, SLOTS, EXPERTS]),
                                      c_("expsel").unsqueeze(1).broadcast_to([D, SLOTS, EXPERTS]), ALU.mult
                                      ).then_inc(moe_dve.sem, 1)
                    dve.max_index(gi[:], gv[:], affT[:]).then_inc(moe_dve.sem, 1)
                    dve.wait_ge(moe_dve.sem, moe_dve.at(it, h, 8))
                    dve.tensor_copy(gf[:], gi[:]).then_inc(moe_dve.sem, 1)
                    dve.wait_ge(moe_dve.sem, moe_dve.at(it, h, 9))
                    dve.tensor_tensor(OHc[:], gf[:].unsqueeze(2).broadcast_to([D, SLOTS, IMG]),
                                      c_("targetc").unsqueeze(1).broadcast_to([D, SLOTS, IMG]), ALU.is_equal
                                      ).then_inc(moe_dve.sem, 1)
                    dve.tensor_tensor(OH[:], gf[:].unsqueeze(2).broadcast_to([D, SLOTS, D]),
                                      c_("target").unsqueeze(1).broadcast_to([D, SLOTS, D]), ALU.is_equal
                                      ).then_inc(moe_dve.sem, 1)
                elif seg == "moe5":
                    for R in jobs(it, "moe4", h, l, "gates"):
                        dve.wait_ge(R.drained, R.nth)
                    for name, dst, w in (("ohg", OHG, PATCHES), ("ohcg", OHcG, IMG)):
                        J = job(it, seg, h, l, name)
                        dve.wait_ge(J.filled, J.nth)
                        ps = J.bank
                        dve.tensor_tensor(dst[:], ps[:, 0:IMG * w].rearrange("p (i t) -> p i t", i=IMG),
                                          gG[:].unsqueeze(2).broadcast_to([D, IMG, w]), ALU.mult).then_inc(J.drained, 1)
                elif seg in ("moe6", "moe7"):
                    hid4 = hid[h].rearrange("p e (i s) -> p e i s", i=IMG)
                    name, dst, k = ("up", hid4, 0) if seg == "moe6" else ("down", eo4, 1)
                    for u in range(2):
                        e = slice(HALF_E * u, HALF_E * (u + 1))
                        J = job(it, seg, h, l, f"{name}{u}")
                        dve.wait_ge(J.filled, J.nth)
                        ps = J.bank
                        dve.tensor_tensor(dst[:, e, :, :], ps[:, :].rearrange("p (e i s) -> p e i s", i=IMG, s=SLOTS),
                                          ev[:, k, e].unsqueeze(2).unsqueeze(3).broadcast_to([D, HALF_E, IMG, SLOTS]),
                                          ALU.add).then_inc(J.drained, 1)
                elif seg == "moe9":
                    J = job(it, seg, h, l, "sum")
                    dve.wait_ge(J.filled, J.nth)
                    ps = J.bank
                    dve.tensor_tensor(nn[h][:, 0:TILES, :], ps[:, :].rearrange("p (t d) -> p t d", t=TILES),
                                      r1[h][:, 0:TILES, :], ALU.add).then_inc(J.drained, 1)
                    J = job(it, seg, h, l, "sumc")
                    dve.wait_ge(J.filled, J.nth)
                    ps = J.bank
                    dve.tensor_tensor(nn[h][0:IMG, TILES, :], ps[0:IMG, 0:D], r1[h][0:IMG, TILES, :], ALU.add
                                      ).then_inc(J.drained, 1)

        @block.tensor
        def _(pe):
            mm = pe.matmul

            def patch(it, h, t, part):
                g = it * PAIRS + h * TILES + t
                i = g % PIX
                if part == 0:
                    pe.wait_ge(pix_in[i].sem, pix_in[i].at(g // PIX, 0))
                    if it + h + t > 0:
                        pe.wait_ge(patch_out.sem, patch_out.at(it, h * TILES + t - 1))
                for k in range(PIECE * part, min(PIECE * (part + 1), BLOCKS)):
                    if k < MAIN:
                        mm(pp[:, 0:D], pix[i][:, k, :], wpm[:, k, :], start=(k == 0), stop=False)
                    else:
                        mm(pp[:, 0:D], pixr[i][:], wpr[:], start=False, stop=True).then_inc(patch_sum.sem, 1)

            def to_T(it, seg, h, l, src):
                for j in range(2):
                    pe.wait_ge(ln_in.sem, ln_in.at(in_order[(it, seg, h, l)], 0, j + 1))
                    if j == 1 and seg == "norm2":
                        pe.wait_ge(ln_act.sem, ln_act.at(it, unit(h, l)))
                    if j == 1 and seg == "norm3":
                        pe.wait_ge(ln_act3.sem, ln_act3.at(it, unit(h, l)))
                    J = job(it, seg, h, l, f"T{j}")
                    pe.wait_ge(J.drained, J.before)
                    ps = J.bank
                    for i, s in enumerate(nat(j)):
                        if s < TILES:
                            ins = pe.transpose(ps[:, D * i:D * (i + 1)], src[:, s, 0:D], ident)
                        else:
                            ins = pe.transpose(ps[:, D * i:D * i + IMG], src[0:IMG, s, 0:D], ident[0:IMG, 0:IMG])
                    ins.then_inc(J.filled, 1)

            pe.wait_ge(wp_in.sem, 16 * N_WP)
            for seg, it, h, l in schedule("pe"):
                n = unit(h, l)
                if seg[:5] == "patch":
                    patch(it, h, l, int(seg[5:]))
                elif seg == "init":
                    if it == 0 and h == 0:
                        pe.wait_ge(w_in.sem, 16 * N_W)
                        pe.wait_ge(set_pool.sem, PIX + 6)
                        pe.wait_ge(set_dve.sem, 1)
                    to_T(it, seg, h, l, xn[h])
                elif seg == "proj":
                    for k, what in enumerate(("q", "k")):
                        for j in range(2):
                            if k == 0:
                                for R in jobs(it, *(("init", h, 0) if l == 0 else ("norm3", h, l - 1)), f"T{j}"):
                                    pe.wait_ge(R.drained, R.nth)
                            J = job(it, seg, h, l, f"{what}{j}")
                            pe.wait_ge(J.drained, J.before)
                            ps = J.bank
                            mm(ps[:, 0:width(j)], wq[:, l, k, :], xT[h][:, cols(j)], start=True, stop=True
                               ).then_inc(J.filled, 1)
                elif seg[:4] == "soft":
                    t = int(seg[4])
                    T = n * TILES + t
                    if t == 0:
                        for R in jobs(it, "proj", h, l, "q0", "q1"):
                            pe.wait_ge(R.drained, R.nth)
                    pe.wait_ge(s_sub.sem, s_sub.at(it, n, t - 1))
                    for b in range(2):
                        if t == 0:
                            pe.wait_ge(kx_act.sem, kx_act.at(it, n, min(4 * (b + 1), ACT_HEADS)))
                            if b == 1:
                                pe.wait_ge(kx_pool.sem, kx_pool.at(it, n))
                        for a in range(2):
                            i = 2 * t + a
                            ins = mm(S[T % SBANKS][PATCHES * a:PATCHES * (a + 1), b, 0:4 * SEQ],
                                     qT[h][:, PATCHES * i:PATCHES * (i + 1)],
                                     kX[h][:, i, 4 * b:4 * b + 4, :].rearrange("p h k -> p (h k)"), start=True,
                                     stop=True)
                    ins.then_inc(s_full.sem, 1)
                elif seg == "cls1":
                    pe.wait_ge(qx_in.sem, qx_in.at(it, n))
                    J = job(it, seg, h, l, "score")
                    pe.wait_ge(J.drained, J.before)
                    ps = J.bank
                    C = IMG * HEADS
                    for i in range(IMG):
                        ins = mm(ps[0:C, 0:SEQ], qx[h][:, C * i:C * (i + 1)], kP[h][:, i, :], start=(i == 0),
                                 stop=(i == IMG - 1))
                    ins.then_inc(J.filled, 1)
                elif seg == "cls2":
                    pe.wait_ge(cls_dve.sem, cls_dve.at(it, n, 4))
                    J = job(it, seg, h, l, "heads")
                    pe.wait_ge(J.drained, J.before)
                    ps = J.bank
                    mm(ps[0:IMG, 0:SEQ], c_("hsum")[0:C, :], Pc[h][:], start=True, stop=True
                       ).then_inc(J.filled, 1)
                elif seg == "cls3":
                    pe.wait_ge(cls_act.sem, cls_act.at(it, n))
                    J = job(it, seg, h, l, "turn")
                    pe.wait_ge(J.drained, J.before)
                    ps = J.bank
                    pe.transpose(ps[:, 0:IMG], Ec[h][:, 0:D], ident[0:IMG, 0:IMG]
                                 ).then_inc(J.filled, 1)
                elif seg == "mix2":
                    pe.wait_ge(ec_in.sem, ec_in.at(it, n))
                    J = job(it, seg, h, l, "turn")
                    pe.wait_ge(J.drained, J.before)
                    ps = J.bank
                    for t in range(TILES):
                        ins = pe.transpose(ps[:, D * t:D * (t + 1)], EX[h][:, t, 0:D], ident)
                    ins.then_inc(J.filled, 1)
                    J = job(it, seg, h, l, "turnc")
                    pe.wait_ge(J.drained, J.before)
                    ps = J.bank
                    for t in range(TILES):
                        ins = pe.transpose(ps[0:IMG, D * t:D * (t + 1)], EX[h][:, t, D:D + IMG], ident)
                    ins.then_inc(J.filled, 1)
                elif seg == "mix3":
                    for R in jobs(it, "mix2", h, l, "turn", "turnc"):
                        pe.wait_ge(R.drained, R.nth)
                    if l > 0:
                        pe.wait_ge(x_in.sem, x_in.at(it, n - HALVES))
                    for j in range(2):
                        J = job(it, seg, h, l, f"mix{j}")
                        pe.wait_ge(J.drained, J.before)
                        ps = J.bank
                        for i in range(2):
                            t = 2 * j + i
                            o = ps[:, (D + 1) * i:(D + 1) * (i + 1)]
                            mm(o, ET[h][:, t, :], xn[h][:, t, :], start=True, stop=False)
                            ins = mm(o, EcT[h][:, t, :], xn[h][0:IMG, TILES, :], start=False, stop=True)
                        ins.then_inc(J.filled, 1)
                    J = job(it, seg, h, l, "mixc")
                    pe.wait_ge(J.drained, J.before)
                    ps = J.bank
                    pe.wait_ge(cls_dve.sem, cls_dve.at(it, n, 9))
                    for R in jobs(it, "cls3", h, l, "turn"):
                        pe.wait_ge(R.drained, R.nth)
                    for t in range(TILES):
                        mm(ps[0:IMG, 0:D], LC[h][:, t, :], xn[h][:, t, 0:D], start=(t == 0), stop=False)
                    mm(ps[0:IMG, 0:D], LC[h][0:IMG, TILES, :], xn[h][0:IMG, TILES, 0:D], start=False, stop=True
                       ).then_inc(J.filled, 1)
                elif seg == "norm2":
                    to_T(it, seg, h, l, zn[h])
                elif seg[:3] == "ffn":
                    j = int(seg[3])
                    if it == 0 and n == 0:
                        pe.wait_ge(late_in.sem, 16 * N_LATE)
                    for R in jobs(it, "norm2", h, l, f"T{j}"):
                        pe.wait_ge(R.drained, R.nth)
                    for f in range(FF // D):
                        J = job(it, seg, h, l, f"h{f}")
                        pe.wait_ge(J.drained, J.before)
                        ps = J.bank
                        mm(ps[:, 0:width(j)], w1s[:, l, D * f:D * (f + 1)], zT[h][:, cols(j)], start=True,
                           stop=True).then_inc(J.filled, 1)
                elif seg == "out":
                    for j in range(2):
                        for R in jobs(it, f"ffn{j}", h, l, "h0", "h1", "h2", "h3"):
                            pe.wait_ge(R.drained, R.nth)
                        J = job(it, seg, h, l, f"out{j}")
                        pe.wait_ge(J.drained, J.before)
                        ps = J.bank
                        for i, s in enumerate(nat(j)):
                            rows_ = D if s < TILES else IMG
                            for f in range(FF // D):
                                ins = mm(ps[0:rows_, D * i:D * (i + 1)], hT[h][:, f, D * s:D * s + rows_],
                                         w2s[:, l, f, :], start=(f == 0), stop=(f == FF // D - 1))
                        ins.then_inc(J.filled, 1)
                elif seg == "norm3" and l + 1 < LAYERS:
                    to_T(it, seg, h, l, nn[h])
                elif seg == "moe2":
                    to_T(it, seg, h, l, nn[h])
                    for R in jobs(it, seg, h, l, "T0", "T1"):
                        pe.wait_ge(R.drained, R.nth)
                    J = job(it, seg, h, l, "gate")
                    pe.wait_ge(J.drained, J.before)
                    ps = J.bank
                    for s in range(SLOTN):
                        ins = mm(ps[:, EXPERTS * s:EXPERTS * (s + 1)], zT[h][:, D * s:D * (s + 1)], gw[:],
                                 start=True, stop=True)
                    ins.then_inc(J.filled, 1)
                elif seg == "moe3":
                    pe.wait_ge(moe_dve.sem, moe_dve.at(it, h, 5))
                    J = job(it, seg, h, l, "aff")
                    pe.wait_ge(J.drained, J.before)
                    ps = J.bank
                    mm(ps[:, 0:1], AX[:, TILES].rearrange("p i e -> p (i e)"), xn[h][:, 0, D:D + 1], start=True,
                       stop=True)
                    for t in range(TILES):
                        ins = mm(ps[:, 1:SEQ], AX[:, t].rearrange("p i e -> p (i e)"), c_("stackI"), start=(t == 0),
                                 stop=(t == TILES - 1))
                    ins.then_inc(J.filled, 1)
                elif seg == "moe4":
                    pe.wait_ge(moe_dve.sem, moe_dve.at(it, h, 7))
                    J = job(it, seg, h, l, "gates")
                    pe.wait_ge(J.drained, J.before)
                    ps = J.bank
                    mm(ps[:, 0:IMG], GX[:].rearrange("p s e -> p (s e)"), c_("imgsel"), start=True, stop=True
                       ).then_inc(J.filled, 1)
                    pe.wait_ge(moe_dve.sem, moe_dve.at(it, h, 11))
                    for u in range(2):
                        J = job(it, seg, h, l, f"oh{u}")
                        pe.wait_ge(J.drained, J.before)
                        ps = J.bank
                        for k in range(4):
                            ins = pe.transpose(ps[:, D * k:D * (k + 1)], OH[:, 4 * u + k, :], ident)
                        ins.then_inc(J.filled, 1)
                    for u in range(2):
                        J = job(it, seg, h, l, f"ohc{u}")
                        pe.wait_ge(J.drained, J.before)
                        ps = J.bank
                        for k in range(4):
                            ins = pe.transpose(ps[0:IMG, D * k:D * (k + 1)], OHc[:, 4 * u + k, :], ident)
                        ins.then_inc(J.filled, 1)
                elif seg == "moe5":
                    for R in jobs(it, "moe4", h, l, "oh0", "oh1", "ohc0", "ohc1"):
                        pe.wait_ge(R.drained, R.nth)
                    J = job(it, seg, h, l, "ohg")
                    pe.wait_ge(J.drained, J.before)
                    ps = J.bank
                    for i in range(IMG):
                        ins = mm(ps[:, PATCHES * i:PATCHES * (i + 1)], OHT[:, D * i:D * (i + 1)], c_("stackI"),
                                 start=True, stop=True)
                    ins.then_inc(J.filled, 1)
                    J = job(it, seg, h, l, "ohcg")
                    pe.wait_ge(J.drained, J.before)
                    ps = J.bank
                    for i in range(IMG):
                        ins = pe.transpose(ps[:, IMG * i:IMG * (i + 1)], OHcT[:, D * i:D * (i + 1)],
                                           ident[0:IMG, 0:IMG])
                    ins.then_inc(J.filled, 1)
                    for t in range(TILES):
                        J = job(it, seg, h, l, f"xin{t}")
                        pe.wait_ge(J.drained, J.before)
                        ps = J.bank
                        pair = slice(2 * D * t, 2 * D * (t + 1))
                        mm(ps[:, 0:2 * D], nn[h][:, t, :], OHT[:, pair], start=True, stop=False)
                        mm(ps[:, 0:2 * D], nn[h][0:IMG, TILES, :], OHcT[:, pair], start=False, stop=True
                           ).then_inc(J.filled, 1)
                elif seg == "moe6":
                    for R in jobs(it, "moe5", h, l, "xin0", "xin1", "xin2", "xin3"):
                        pe.wait_ge(R.drained, R.nth)
                    for u in range(2):
                        J = job(it, seg, h, l, f"up{u}")
                        pe.wait_ge(J.drained, J.before)
                        ps = J.bank
                        for k in range(HALF_E):
                            e = HALF_E * u + k
                            ins = mm(ps[:, PATCHES * k:PATCHES * (k + 1)], ew1s[:, e, :],
                                     xin[h][:, e].rearrange("p i s -> p (i s)"), start=True, stop=True)
                        ins.then_inc(J.filled, 1)
                elif seg == "moe7":
                    for u in range(2):
                        pe.wait_ge(moe_act.sem, moe_act.at(it, h, 2 + u))
                        J = job(it, seg, h, l, f"down{u}")
                        pe.wait_ge(J.drained, J.before)
                        ps = J.bank
                        for k in range(HALF_E):
                            e = HALF_E * u + k
                            ins = mm(ps[:, PATCHES * k:PATCHES * (k + 1)], ew2s[:, e, :], hid[h][:, e, :],
                                     start=True, stop=True)
                        ins.then_inc(J.filled, 1)
                elif seg == "moe8":
                    for R in jobs(it, "moe7", h, l, "down0", "down1"):
                        pe.wait_ge(R.drained, R.nth)
                    for u in range(2):
                        J = job(it, seg, h, l, f"yT{u}")
                        pe.wait_ge(J.drained, J.before)
                        ps = J.bank
                        for k in range(4):
                            ins = pe.transpose(ps[:, D * k:D * (k + 1)], eo[:, 4 * u + k, :], ident)
                        ins.then_inc(J.filled, 1)
                elif seg == "moe9":
                    for R in jobs(it, "moe8", h, l, "yT0", "yT1"):
                        pe.wait_ge(R.drained, R.nth)
                    for R in jobs(it, "moe5", h, l, "ohg", "ohcg"):
                        pe.wait_ge(R.drained, R.nth)
                    J = job(it, seg, h, l, "sum")
                    pe.wait_ge(J.drained, J.before)
                    ps = J.bank
                    for i in range(IMG):
                        t, a = i // 2, i % 2
                        ins = mm(ps[PATCHES * a:PATCHES * (a + 1), D * t:D * (t + 1)], OHG[:, i, :], Y[h][:, i, :],
                                 start=True, stop=True)
                    ins.then_inc(J.filled, 1)
                    J = job(it, seg, h, l, "sumc")
                    pe.wait_ge(J.drained, J.before)
                    ps = J.bank
                    for i in range(IMG):
                        ins = mm(ps[0:IMG, 0:D], OHcG[:, i, :], Y[h][:, i, :], start=(i == 0), stop=(i == IMG - 1))
                    ins.then_inc(J.filled, 1)


def kernel(**inputs):
    import concourse.bacc as _bacc
    from concourse.bass_utils import run_bass_kernel_spmd as _run

    a = {k: np.asarray(v) for k, v in inputs.items()}
    pairs = B // 2
    x = a["x"].reshape(pairs, 2, 3, 8, 28, 8, 28).transpose(0, 2, 4, 6, 1, 3, 5).reshape(pairs, IN_D, D)
    w = a["L0_tok_W"].T
    L = "L0_attn_"
    vecs = [a[L + "bqkv"][:, 0:D], a[L + "bqkv"][:, D:2 * D], a[L + "g1"], a[L + "bt1"], a[L + "g2"], a[L + "bt2"],
            a[L + "g3"], a[L + "bt3"]] + [a[L + "b1"][:, D * f:D * (f + 1)] for f in range(FF // D)]
    arrays = {
        "x_main": x[:, :MAIN * D].reshape(pairs, D, MAIN, D),
        "x_rest": x[:, MAIN * D:],
        "wp_main": w[:MAIN * D].reshape(D, MAIN, D),
        "wp_rest": np.concatenate([w[MAIN * D:], a["L0_tok_b"][None]], 0),
        "cls0": a["L0_tok_class_token"],
        "pos": a["L0_tok_pos_embed"],
        "const": shape_constants(),
        "wqk": a[L + "Wqkv"][:, 0:2 * D].reshape(LAYERS, 2, D, D).transpose(3, 0, 1, 2),
        "w1": a[L + "W1"].transpose(2, 0, 1),
        "w2": a[L + "W2"].reshape(LAYERS, D, FF // D, D).transpose(3, 0, 2, 1),
        "lvec": np.stack(vecs, 2).transpose(1, 0, 2),
        "rows": np.stack([a[L + n] for n in ("g1", "bt1", "g2", "bt2", "g3", "bt3", "b2")], 1)[None],
        "gate": a["L0_ffn_gate_weight"],
        "ew1": a["L0_ffn_w1"].transpose(1, 0, 2),
        "ew2": a["L0_ffn_w2"].transpose(1, 0, 2),
        "evec": np.stack([a["L0_ffn_b1"], a["L0_ffn_b2"]]).transpose(2, 0, 1),
    }
    arrays = {k: np.ascontiguousarray(v) for k, v in arrays.items()}
    nc = _bacc.Bacc("TRN2", target_bir_lowering=False, num_devices=1)
    args = [nc.dram_tensor(k, v.shape, mybir.dt.from_np(v.dtype), kind="ExternalInput").ap() for k, v in arrays.items()]
    args.append(nc.dram_tensor("out", (B, SEQ, D), F32, kind="ExternalOutput").ap())
    vit_kernel(nc, *args)
    r = _run(nc, [arrays], core_ids=[0])
    return r.results[0]["out"]
```
